# Optimizing a Trainium2 kernel written in Bass

```python
import numpy as np
import jax
import jax.numpy as jnp

def _softmax(x, axis=-1):
    return jax.nn.softmax(x, axis=axis)

def _gelu(x):
    return jax.nn.gelu(x, approximate=True)

def _silu(x):
    return jax.nn.silu(x)

def _sigmoid(x):
    return jax.nn.sigmoid(x)

def _layernorm(x, axis=-1, eps=1e-05):
    m = jnp.mean(x, axis=axis, keepdims=True)
    v = jnp.var(x, axis=axis, keepdims=True)
    return (x - m) / jnp.sqrt(v + eps)

def _scatter_add(tgt, idx, src, axis=0):
    return tgt.at[idx].add(src)

def _segment_sum(src, seg, n):
    return jax.ops.segment_sum(src, seg, n)
kernel_name = 'mk_decoder_preln_d2_seqx_r8_2145bf'

def setup_inputs(seed: int=0):
    np.random.seed(seed)
    _w = jnp.asarray

    def _rec_inputs():
        import jax
        import jax.numpy as jnp
        _rk = jax.random.key(seed)
        x = -0.0002928 + 1 * jax.random.normal(jax.random.fold_in(_rk, 1), (128, 64, 128), jnp.float32)
        _lenS = 64 - jax.random.randint(jax.random.fold_in(_rk, 7), (128,), 0, max(1, 64 // 4) + 1, jnp.int32)
        _lenS2 = 64 - jax.random.randint(jax.random.fold_in(_rk, 8), (128,), 0, max(1, 64 // 4) + 1, jnp.int32)
        _ctx_1024P = jax.random.normal(jax.random.fold_in(_rk, 11), (128, 16, 128), jnp.float32)
        _ctx_1024c = jax.random.dirichlet(jax.random.fold_in(_rk, 511), 0.3 * jnp.ones((16,), jnp.float32), (128, 64))
        _ctx_1024t = jnp.einsum('bsk,bkd->bsd', _ctx_1024c, _ctx_1024P)
        _ctx_1024t = _ctx_1024t * jax.lax.rsqrt(jnp.mean(jnp.square(_ctx_1024t)) + 1e-12) * 0.953939
        ctx_1024 = -1.39393e-06 + 0.999914 * (_ctx_1024t + 0.3 * jax.random.normal(jax.random.fold_in(_rk, 611), (128, 64, 128), jnp.float32))
        _validS = jnp.arange(64)[None, :] < _lenS[:, None]
        _validS2 = jnp.arange(64)[None, :] < _lenS2[:, None]
        _causal = jnp.tril(jnp.ones((64, 64), dtype=bool))
        mask_BxSxS2_ik1 = jnp.where(jnp.broadcast_to(_validS2[:, None, :], (128, 64, 64)), 1, 0).astype(jnp.int32)
        return (x, ctx_1024, mask_BxSxS2_ik1)
    x, ctx_1024, mask_BxSxS2_ik1 = _rec_inputs()

    def _L0_attn_setup():
        import jax, jax.numpy as jnp
        import numpy as np
        B, S, E, H = (2, 256, 128, 16)
        D = E // H
        key = jax.random.key(seed)
        ks = jax.random.split(key, 6)
        scale = 1.0 / np.sqrt(E)
        return {'x': jax.random.normal(ks[0], (B, S, E), dtype=jnp.float32), 'Wqkv_w': jax.random.normal(ks[1], (3 * E, E), dtype=jnp.float32) * scale, 'Wqkv_b': jax.random.normal(ks[2], (3 * E,), dtype=jnp.float32) * 0.01, 'out_w': jax.random.normal(ks[3], (E, E), dtype=jnp.float32) * scale, 'out_b': jax.random.normal(ks[4], (E,), dtype=jnp.float32) * 0.01, 'distance_decay': jax.random.normal(ks[5], (1,), dtype=jnp.float32)}
    _L0_attn_all = _L0_attn_setup()
    _L0_attn_in = {k: v for k, v in _L0_attn_all.items() if k in ('Wqkv_w', 'Wqkv_b', 'out_w', 'out_b', 'distance_decay')}
    del _L0_attn_all

    def _L0_xattn_setup():
        import jax, jax.numpy as jnp
        import numpy as np
        E = 128
        HQ = 16
        HK = 4
        D = E // HQ
        G = HQ // HK
        KVE = D * HK
        B = 2
        N = 256
        LN_EPS = 1e-05

        def _xavier(k, fan_out, fan_in):
            std = np.sqrt(2.0 / (fan_in + fan_out)).astype(np.float32)
            return jax.random.normal(k, (fan_out, fan_in), jnp.float32) * std
        key = jax.random.key(seed)
        ks = jax.random.split(key, 8)
        return {'query': jax.random.normal(ks[0], (B, N, E), jnp.float32), 'key': jax.random.normal(ks[1], (B, N, E), jnp.float32), 'value': jax.random.normal(ks[2], (B, N, E), jnp.float32), 'adj': jax.random.randint(ks[3], (B, N, N), 0, 2, jnp.int32), 'Wq': _xavier(ks[4], E, E), 'bq': jnp.zeros((E,), jnp.float32), 'Wk': _xavier(ks[5], KVE, E), 'bk': jnp.zeros((KVE,), jnp.float32), 'Wv': _xavier(ks[6], KVE, E), 'bv': jnp.zeros((KVE,), jnp.float32), 'Wo': _xavier(ks[7], E, E), 'bo': jnp.zeros((E,), jnp.float32), 'ln_g': jnp.ones((E,), jnp.float32), 'ln_b': jnp.zeros((E,), jnp.float32)}
    _L0_xattn_all = _L0_xattn_setup()
    _L0_xattn_in = {k: v for k, v in _L0_xattn_all.items() if k in ('Wq', 'bq', 'Wk', 'bk', 'Wv', 'bv', 'Wo', 'bo', 'ln_g', 'ln_b')}
    del _L0_xattn_all

    def _L0_ffn_setup():
        import jax, jax.numpy as jnp
        import numpy as np
        B, T = (2, 256)
        D_MODEL, D_HIDDEN = (128, 256)
        N_EXPERTS, TOP_K = (8, 2)
        N_TOKENS = B * T
        CAPACITY = 2 * N_TOKENS * TOP_K // N_EXPERTS
        key = jax.random.key(seed)
        k_x, k_rw, k_w, k_v, k_o = jax.random.split(key, 5)
        x = jax.random.normal(k_x, (B, T, D_MODEL), jnp.float32)
        router_w = jax.random.normal(k_rw, (N_EXPERTS, D_MODEL), jnp.float32) * D_MODEL ** (-0.5)
        router_b = jnp.zeros((N_EXPERTS,), jnp.float32)
        W = jax.random.normal(k_w, (N_EXPERTS, D_MODEL, D_HIDDEN), jnp.float32) * D_MODEL ** (-0.5)
        V = jax.random.normal(k_v, (N_EXPERTS, D_MODEL, D_HIDDEN), jnp.float32) * D_MODEL ** (-0.5)
        W_out = jax.random.normal(k_o, (N_EXPERTS, D_HIDDEN, D_MODEL), jnp.float32) * D_HIDDEN ** (-0.5)
        return {'x': x, 'router_w': router_w, 'router_b': router_b, 'W': W, 'V': V, 'W_out': W_out}
    _L0_ffn_all = _L0_ffn_setup()
    _L0_ffn_in = {k: v for k, v in _L0_ffn_all.items() if k in ('router_w', 'router_b', 'W', 'V', 'W_out')}
    del _L0_ffn_all

    def _L1_attn_setup():
        import jax, jax.numpy as jnp
        import numpy as np
        HEADS = 16
        DIM_HEAD = 64
        B, T, C = (4, 256, 128)

        def apply_rope(x):
            d = x.shape[-1]
            seq_len = x.shape[1]
            inv_freq = 1.0 / 10000.0 ** (jnp.arange(0, d, 2, dtype=jnp.float32) / d)
            pos = jnp.arange(seq_len, dtype=jnp.float32)
            ang = pos[:, None] * inv_freq[None, :]
            sin = jnp.sin(ang)[None]
            cos = jnp.cos(ang)[None]
            x1, x2 = (x[..., 0::2], x[..., 1::2])
            rot = jnp.stack([x1 * cos - x2 * sin, x1 * sin + x2 * cos], axis=-1)
            return rot.reshape(x.shape)
        key = jax.random.key(seed)
        ks = jax.random.split(key, 6)
        inner = HEADS * DIM_HEAD
        w = 0.02
        return {'x': jax.random.normal(ks[0], (B, T, C), dtype=jnp.float32), 'Wq': jax.random.normal(ks[1], (C, inner), dtype=jnp.float32) * w, 'Wk': jax.random.normal(ks[2], (C, inner), dtype=jnp.float32) * w, 'Wv': jax.random.normal(ks[3], (C, inner), dtype=jnp.float32) * w, 'Wo': jax.random.normal(ks[4], (inner, C), dtype=jnp.float32) * w, 'bo': jnp.zeros((C,), dtype=jnp.float32)}
    _L1_attn_all = _L1_attn_setup()
    _L1_attn_in = {k: v for k, v in _L1_attn_all.items() if k in ('Wq', 'Wk', 'Wv', 'Wo', 'bo')}
    del _L1_attn_all

    def _L1_xattn_setup():
        import jax, jax.numpy as jnp
        import numpy as np
        B, C_LEN, Q_LEN, D = (8, 256, 64, 128)
        key = jax.random.key(seed)
        ks = jax.random.split(key, 10)
        scale = 1.0 / np.sqrt(D)
        return {'c': jax.random.normal(ks[0], (B, C_LEN, D), dtype=jnp.float32), 'q': jax.random.normal(ks[1], (B, Q_LEN, D), dtype=jnp.float32), 'w_cq': jax.random.normal(ks[2], (D,), dtype=jnp.float32) * scale, 'b_cq': jax.random.normal(ks[3], (), dtype=jnp.float32) * scale, 'w_c': jax.random.normal(ks[4], (D,), dtype=jnp.float32) * scale, 'b_c': jax.random.normal(ks[5], (), dtype=jnp.float32) * scale, 'w_q': jax.random.normal(ks[6], (D,), dtype=jnp.float32) * scale, 'b_q': jax.random.normal(ks[7], (), dtype=jnp.float32) * scale, 'W_l': jax.random.normal(ks[8], (D, 4 * D), dtype=jnp.float32) * (1.0 / np.sqrt(4 * D)), 'b_l': jax.random.normal(ks[9], (D,), dtype=jnp.float32) * (1.0 / np.sqrt(4 * D))}
    _L1_xattn_all = _L1_xattn_setup()
    _L1_xattn_in = {k: v for k, v in _L1_xattn_all.items() if k in ('w_cq', 'b_cq', 'w_c', 'b_c', 'w_q', 'b_q', 'W_l', 'b_l')}
    del _L1_xattn_all

    def _L1_ffn_setup():
        import jax, jax.numpy as jnp
        import numpy as np
        B, S, H, F, E = (4, 256, 128, 512, 8)
        key = jax.random.key(seed)
        ks = jax.random.split(key, 8)
        s = 1.0 / np.sqrt(H)
        sf = 1.0 / np.sqrt(F)
        return {'x': jax.random.normal(ks[0], (B, S, H), jnp.float32), 'wr': jax.random.uniform(ks[1], (H, E), jnp.float32, -s, s), 'br': jax.random.uniform(ks[2], (E,), jnp.float32, -s, s), 'w1': jax.random.uniform(ks[3], (E, H, F), jnp.float32, -s, s), 'b1': jax.random.uniform(ks[4], (E, F), jnp.float32, -s, s), 'w2': jax.random.uniform(ks[5], (E, F, H), jnp.float32, -sf, sf), 'b2': jax.random.uniform(ks[6], (E, H), jnp.float32, -sf, sf)}
    _L1_ffn_all = _L1_ffn_setup()
    _L1_ffn_in = {k: v for k, v in _L1_ffn_all.items() if k in ('wr', 'br', 'w1', 'b1', 'w2', 'b2')}
    del _L1_ffn_all
    return {'x': x, 'ctx_1024': ctx_1024, 'mask_BxSxS2_ik1': mask_BxSxS2_ik1, 'L0_attn_Wqkv_w': _L0_attn_in['Wqkv_w'], 'L0_attn_Wqkv_b': _L0_attn_in['Wqkv_b'], 'L0_attn_out_w': _L0_attn_in['out_w'], 'L0_attn_out_b': _L0_attn_in['out_b'], 'L0_attn_distance_decay': _L0_attn_in['distance_decay'], 'L0_xattn_Wq': _L0_xattn_in['Wq'], 'L0_xattn_bq': _L0_xattn_in['bq'], 'L0_xattn_Wk': _L0_xattn_in['Wk'], 'L0_xattn_bk': _L0_xattn_in['bk'], 'L0_xattn_Wv': _L0_xattn_in['Wv'], 'L0_xattn_bv': _L0_xattn_in['bv'], 'L0_xattn_Wo': _L0_xattn_in['Wo'], 'L0_xattn_bo': _L0_xattn_in['bo'], 'L0_xattn_ln_g': _L0_xattn_in['ln_g'], 'L0_xattn_ln_b': _L0_xattn_in['ln_b'], 'L0_ffn_router_w': _L0_ffn_in['router_w'], 'L0_ffn_router_b': _L0_ffn_in['router_b'], 'L0_ffn_W': _L0_ffn_in['W'], 'L0_ffn_V': _L0_ffn_in['V'], 'L0_ffn_W_out': _L0_ffn_in['W_out'], 'L1_attn_Wq': _L1_attn_in['Wq'], 'L1_attn_Wk': _L1_attn_in['Wk'], 'L1_attn_Wv': _L1_attn_in['Wv'], 'L1_attn_Wo': _L1_attn_in['Wo'], 'L1_attn_bo': _L1_attn_in['bo'], 'L1_xattn_w_cq': _L1_xattn_in['w_cq'], 'L1_xattn_b_cq': _L1_xattn_in['b_cq'], 'L1_xattn_w_c': _L1_xattn_in['w_c'], 'L1_xattn_b_c': _L1_xattn_in['b_c'], 'L1_xattn_w_q': _L1_xattn_in['w_q'], 'L1_xattn_b_q': _L1_xattn_in['b_q'], 'L1_xattn_W_l': _L1_xattn_in['W_l'], 'L1_xattn_b_l': _L1_xattn_in['b_l'], 'L1_ffn_wr': _L1_ffn_in['wr'], 'L1_ffn_br': _L1_ffn_in['br'], 'L1_ffn_w1': _L1_ffn_in['w1'], 'L1_ffn_b1': _L1_ffn_in['b1'], 'L1_ffn_w2': _L1_ffn_in['w2'], 'L1_ffn_b2': _L1_ffn_in['b2']}

def reference(x, ctx_1024, mask_BxSxS2_ik1, L0_attn_Wqkv_w, L0_attn_Wqkv_b, L0_attn_out_w, L0_attn_out_b, L0_attn_distance_decay, L0_xattn_Wq, L0_xattn_bq, L0_xattn_Wk, L0_xattn_bk, L0_xattn_Wv, L0_xattn_bv, L0_xattn_Wo, L0_xattn_bo, L0_xattn_ln_g, L0_xattn_ln_b, L0_ffn_router_w, L0_ffn_router_b, L0_ffn_W, L0_ffn_V, L0_ffn_W_out, L1_attn_Wq, L1_attn_Wk, L1_attn_Wv, L1_attn_Wo, L1_attn_bo, L1_xattn_w_cq, L1_xattn_b_cq, L1_xattn_w_c, L1_xattn_b_c, L1_xattn_w_q, L1_xattn_b_q, L1_xattn_W_l, L1_xattn_b_l, L1_ffn_wr, L1_ffn_br, L1_ffn_w1, L1_ffn_b1, L1_ffn_w2, L1_ffn_b2):
    import jax
    import jax.numpy as jnp

    def _L0_attn_ref(x, Wqkv_w, Wqkv_b, out_w, out_b, distance_decay):
        import jax, jax.numpy as jnp
        import numpy as np
        B, S, E, H = (2, 256, 128, 16)
        D = E // H
        b, s, e = x.shape
        qkv = x @ Wqkv_w.T + Wqkv_b
        qkv = qkv.reshape(b, s, 3, H, D).transpose(2, 0, 3, 1, 4)
        q, k, v = (qkv[0], qkv[1], qkv[2])
        scores = jnp.einsum('bhsd,bhtd->bhst', q, k) / jnp.sqrt(jnp.asarray(D, x.dtype))
        idx = jnp.arange(s, dtype=x.dtype)
        dist = jnp.abs(idx[:, None] - idx[None, :])
        decay = jnp.exp(-jnp.abs(distance_decay[0]) * dist)
        scores = scores * decay
        attn = jax.nn.softmax(scores, axis=-1)
        out = jnp.einsum('bhst,bhtd->bhsd', attn, v)
        out = out.transpose(0, 2, 1, 3).reshape(b, s, e)
        return out @ out_w.T + out_b

    def _L0_xattn_ref(query, key, value, adj, Wq, bq, Wk, bk, Wv, bv, Wo, bo, ln_g, ln_b):
        import jax, jax.numpy as jnp
        import numpy as np
        E = 128
        HQ = 16
        HK = 4
        D = E // HQ
        G = HQ // HK
        KVE = D * HK
        B = 2
        N = 256
        LN_EPS = 1e-05

        def _xavier(k, fan_out, fan_in):
            std = np.sqrt(2.0 / (fan_in + fan_out)).astype(np.float32)
            return jax.random.normal(k, (fan_out, fan_in), jnp.float32) * std
        b, n, _ = query.shape
        q = query @ Wq.T + bq
        k = key @ Wk.T + bk
        v = value @ Wv.T + bv
        q = q.reshape(b, n, HQ, D).transpose(0, 2, 1, 3) / np.float32(np.sqrt(D))
        q = q.reshape(b, HK, G, n, D).transpose(0, 2, 1, 3, 4)
        k = k.reshape(b, n, HK, D).transpose(0, 2, 1, 3)
        v = v.reshape(b, n, HK, D).transpose(0, 2, 1, 3)
        sim = jnp.einsum('bghnd,bhsd->bghns', q, k)
        causal = jnp.tril(jnp.ones((n, n), bool))
        mask = causal[None, None, None, :, :] & (adj != 0)[:, None, None, :, :]
        neg = jnp.finfo(sim.dtype).min
        sim = jnp.where(mask, sim, neg)
        attn = jax.nn.softmax(sim, axis=-1)
        out = jnp.einsum('bghns,bhsd->bghnd', attn, v)
        out = out.transpose(0, 3, 2, 1, 4).reshape(b, n, E)
        mu = out.mean(-1, keepdims=True)
        var = jnp.mean(jnp.square(out - mu), -1, keepdims=True)
        out = (out - mu) / jnp.sqrt(var + LN_EPS) * ln_g + ln_b
        return out @ Wo.T + bo

    def _L0_ffn_ref(x, router_w, router_b, W, V, W_out):
        import jax, jax.numpy as jnp
        import numpy as np
        B, T = (2, 256)
        D_MODEL, D_HIDDEN = (128, 256)
        N_EXPERTS, TOP_K = (8, 2)
        N_TOKENS = B * T
        CAPACITY = 2 * N_TOKENS * TOP_K // N_EXPERTS
        Bq, Tq, D = x.shape
        N = Bq * Tq
        x_flat = x.reshape(N, D)
        router_logits = x_flat @ router_w.T + router_b
        top_vals, top_ids = jax.lax.top_k(router_logits, TOP_K)
        top_probs = jax.nn.softmax(top_vals, axis=-1)
        x_pad = jnp.concatenate([x_flat, jnp.zeros((1, D), x_flat.dtype)], axis=0)
        probs_pad = jnp.concatenate([top_probs, jnp.zeros((1, TOP_K), top_probs.dtype)], axis=0)
        out = jnp.zeros((N + 1, D), x_flat.dtype)
        for e in range(N_EXPERTS):
            tok, slot = jnp.nonzero(top_ids == e, size=CAPACITY, fill_value=(N, 0))
            w = probs_pad[tok, slot][:, None]
            xin = x_pad[tok]
            a = xin @ W[e]
            b = xin @ V[e]
            y = a * (b * jax.nn.sigmoid(b)) @ W_out[e]
            out = out.at[tok].add(y * w)
        return out[:N].reshape(Bq, Tq, D)

    def _L1_attn_ref(x, Wq, Wk, Wv, Wo, bo):
        import jax, jax.numpy as jnp
        import numpy as np
        HEADS = 16
        DIM_HEAD = 64
        B, T, C = (4, 256, 128)

        def apply_rope(x):
            d = x.shape[-1]
            seq_len = x.shape[1]
            inv_freq = 1.0 / 10000.0 ** (jnp.arange(0, d, 2, dtype=jnp.float32) / d)
            pos = jnp.arange(seq_len, dtype=jnp.float32)
            ang = pos[:, None] * inv_freq[None, :]
            sin = jnp.sin(ang)[None]
            cos = jnp.cos(ang)[None]
            x1, x2 = (x[..., 0::2], x[..., 1::2])
            rot = jnp.stack([x1 * cos - x2 * sin, x1 * sin + x2 * cos], axis=-1)
            return rot.reshape(x.shape)
        b, t, c = x.shape
        h, d = (HEADS, DIM_HEAD)
        scale = d ** (-0.5)

        def split_heads(z):
            return z.reshape(b, t, h, d).transpose(0, 2, 1, 3).reshape(b * h, t, d)
        q = split_heads(x @ Wq)
        k = split_heads(x @ Wk)
        v = split_heads(x @ Wv)
        q = apply_rope(q)
        k = apply_rope(k)
        sim = jnp.einsum('bid,bjd->bij', q, k) * scale
        causal = jnp.tril(jnp.ones((t, t), dtype=bool))
        sim = jnp.where(causal[None], sim, -jnp.inf)
        attn = jax.nn.softmax(sim, axis=-1)
        out = jnp.einsum('bij,bjd->bid', attn, v)
        out = out.reshape(b, h, t, d).transpose(0, 2, 1, 3).reshape(b, t, h * d)
        return out @ Wo + bo

    def _L1_xattn_ref(c, q, w_cq, b_cq, w_c, b_c, w_q, b_q, W_l, b_l):
        import jax, jax.numpy as jnp
        import numpy as np
        B, C_LEN, Q_LEN, D = (8, 256, 64, 128)
        cq = jnp.einsum('bcd,bqd,d->bcq', c, q, w_cq) + b_cq
        s = (c @ w_c + b_c)[:, :, None] + (q @ w_q + b_q)[:, None, :] + cq
        a = jax.nn.softmax(s, axis=2)
        c2q_att = jnp.einsum('bcq,bqd->bcd', a, q)
        b_att = jax.nn.softmax(jnp.max(s, axis=2), axis=1)
        q2c_att = jnp.einsum('bc,bcd->bd', b_att, c)[:, None, :]
        x = jnp.concatenate([c, c2q_att, c * c2q_att, c * q2c_att], axis=-1)
        z = x @ W_l.T + b_l
        return z

    def _L1_ffn_ref(x, wr, br, w1, b1, w2, b2):
        import jax, jax.numpy as jnp
        import numpy as np
        B, S, H, F, E = (4, 256, 128, 512, 8)
        scores = jnp.einsum('bsh,he->bse', x, wr) + br
        expert_id = jnp.argmax(scores, axis=-1)
        h = jnp.einsum('bsh,ehf->ebsf', x, w1) + b1[:, None, None, :]
        h = jax.nn.gelu(h, approximate=False)
        y = jnp.einsum('ebsf,efh->ebsh', h, w2) + b2[:, None, None, :]
        one_hot = jax.nn.one_hot(expert_id, E, dtype=x.dtype)
        out = jnp.einsum('ebsh,bse->bsh', y, one_hot)
        return out
    x = x + _L0_attn_ref(_layernorm(x, axis=-1), L0_attn_Wqkv_w, L0_attn_Wqkv_b, L0_attn_out_w, L0_attn_out_b, L0_attn_distance_decay)
    x = x + _L0_xattn_ref(_layernorm(x, axis=-1), ctx_1024, ctx_1024, mask_BxSxS2_ik1, L0_xattn_Wq, L0_xattn_bq, L0_xattn_Wk, L0_xattn_bk, L0_xattn_Wv, L0_xattn_bv, L0_xattn_Wo, L0_xattn_bo, L0_xattn_ln_g, L0_xattn_ln_b)
    x = x + _L0_ffn_ref(_layernorm(x, axis=-1), L0_ffn_router_w, L0_ffn_router_b, L0_ffn_W, L0_ffn_V, L0_ffn_W_out)
    x = x + _L1_attn_ref(_layernorm(x, axis=-1), L1_attn_Wq, L1_attn_Wk, L1_attn_Wv, L1_attn_Wo, L1_attn_bo)
    x = x + _L1_xattn_ref(_layernorm(x, axis=-1), ctx_1024, L1_xattn_w_cq, L1_xattn_b_cq, L1_xattn_w_c, L1_xattn_b_c, L1_xattn_w_q, L1_xattn_b_q, L1_xattn_W_l, L1_xattn_b_l)
    x = x + _L1_ffn_ref(_layernorm(x, axis=-1), L1_ffn_wr, L1_ffn_br, L1_ffn_w1, L1_ffn_b1, L1_ffn_w2, L1_ffn_b2)
    return x

_drawn_inputs = setup_inputs


def setup_inputs(seed=0):
    import zlib

    import numpy as np

    out = dict(_drawn_inputs(seed))
    spreads = {'L0_xattn_bq': (0.0, 0.1),
     'L0_xattn_bk': (0.0, 0.8),
     'L0_xattn_bv': (0.0, 0.1),
     'L0_xattn_bo': (0.0, 0.1),
     'L0_xattn_ln_g': (1.0, 0.2),
     'L0_xattn_ln_b': (0.0, 0.1),
     'L0_ffn_router_b': (0.0, 0.1),
     'L1_attn_bo': (0.0, 0.1)}
    factors = {'L0_attn_Wqkv_b': 2.892,
     'L0_attn_out_b': 2.931,
     'L1_attn_Wq': 8.0,
     'L1_attn_Wk': 8.0,
     'L1_ffn_b1': 5.063,
     'L1_ffn_b2': 3.626}
    for name, (base, spread) in spreads.items():
        noise = np.random.default_rng([zlib.crc32(name.encode()), seed]).standard_normal(out[name].shape)
        drawn = base * np.exp(spread * noise) if base else spread * noise
        out[name] = jnp.asarray(drawn.astype(out[name].dtype))
    for name, factor in factors.items():
        out[name] = (out[name] * factor).astype(out[name].dtype)
    return out
```

```python
from contextlib import ExitStack, contextmanager

import numpy as np

import concourse.bass as bass
from concourse import mybir

F32 = mybir.dt.float32
BF16 = mybir.dt.bfloat16
I32 = mybir.dt.int32
U32 = mybir.dt.uint32
ALU = mybir.AluOpType
ACT = mybir.ActivationFunctionType
AX = mybir.AxisListType

P = 128
SEQ = 64
LN_EPS = 1e-5
NEG = -1e30

H0, D0 = 16, 8
GRP = 4
H1, D1 = 16, 64
NE = 8
CAP = 256
PAIRS = 8
UNROLL = 4
PEEL = 8


class Kept:

    def __init__(self, tiles):
        self.tiles = tiles


@contextmanager
def stage_semaphores(nc):
    made = []

    def new(name):
        made.append(nc.alloc_semaphore(name))
        return made[-1]

    yield new
    numbers = sorted(s.num for s in made)
    while numbers:
        n = next((n for n in range(1, len(numbers)) if numbers[n] != numbers[0] + n), len(numbers))
        nc.gpsimd.sem_clear(range(numbers[0], numbers[0] + n))
        numbers = numbers[n:]
    for s in made:
        nc.release_semaphore(s)


def pipeline(eng, tiles, step, lag, unroll=UNROLL, peel=PEEL):
    body = (tiles - peel) // unroll
    for i in range(peel):
        step(i, i % unroll)
    with eng.Fori(0, body) as j:
        for u in range(unroll):
            step(j * unroll + (peel + u), u)
    for i in range(peel + body * unroll, tiles + lag):
        step(i, i % unroll)


def late(t, n):
    return not isinstance(t, int) or t >= n


def has(t, tiles):
    return not isinstance(t, int) or 0 <= t < tiles


def bc(ap, axis, n):
    return ap.unsqueeze(axis).to_broadcast([*ap.shape[:axis], n, *ap.shape[axis:]])


def keep_with_stats(dve, row, kept, st, mv, kept_mv, t, st_ready, mv_ready, mv_kept):
    dve.bn_stats(st, row).then_inc(st_ready, 1)
    dve.wait_ge(st_ready, t + 1)
    dve.tensor_scalar(kept, row, 1.0, None, ALU.mult)
    dve.bn_aggr(mv, st).then_inc(mv_ready, 1)
    dve.wait_ge(mv_ready, t + 1)
    dve.tensor_scalar(kept_mv, mv, 1.0, None, ALU.mult).then_inc(mv_kept, 1)


def layer_norm_scales(nc, k, mean_var, scale, shift, name):
    with ExitStack() as c:
        tiles = mean_var.shape[1]
        ve = c.enter_context(nc.sbuf_tensor(f"{name}_ve", [P, tiles], F32))
        root = c.enter_context(nc.sbuf_tensor(f"{name}_root", [P, tiles], F32))
        guess = c.enter_context(nc.sbuf_tensor(f"{name}_guess", [P, tiles], F32))
        corr = c.enter_context(nc.sbuf_tensor(f"{name}_corr", [P, tiles], F32))
        new_sem = c.enter_context(stage_semaphores(nc))
        var_done, root_done, newton = (new_sem(f"{name}_{n}") for n in ("var_done", "root_done", "newton"))
        block = c.enter_context(nc.Block())

        @block.vector
        def _(dve):
            dve.tensor_scalar(ve[:], mean_var[:, :, 1], LN_EPS, None, ALU.add).then_inc(var_done, 1)
            dve.wait_ge(root_done, 1)
            dve.reciprocal(guess[:], root[:]).then_inc(newton, 1)
            dve.wait_ge(newton, 1)
            dve.tensor_tensor(corr[:], guess[:], guess[:], ALU.mult).then_inc(newton, 1)
            dve.wait_ge(newton, 2)
            dve.tensor_tensor(corr[:], corr[:], ve[:], ALU.mult).then_inc(newton, 1)
            dve.wait_ge(newton, 3)
            dve.tensor_scalar(corr[:], corr[:], -0.5, 1.5, ALU.mult, ALU.add).then_inc(newton, 1)
            dve.wait_ge(newton, 4)
            dve.tensor_tensor(scale, guess[:], corr[:], ALU.mult).then_inc(newton, 1)
            dve.wait_ge(newton, 5)
            dve.scalar_tensor_tensor(out=shift, in0=mean_var[:, :, 0], scalar=-1.0, in1=scale,
                                     op0=ALU.mult, op1=ALU.mult)

        @block.scalar
        def _(act):
            act.wait_ge(var_done, 1)
            act.activation(root[:], ve[:], ACT.Sqrt).then_inc(root_done, 1)


def small_head_attention(nc, k, name, cross):
    NT = k.tiles
    scale = float(1.0 / np.sqrt(D0))
    wq, wk, wv, bq, bk, bv = ((k.x_wq, k.x_wk, k.x_wv, k.x_bq, k.x_bk, k.x_bv_rows) if cross else
                              (k.a_wq, k.a_wk, k.a_wv, k.a_bq, k.a_bk, k.a_bv))
    with ExitStack() as c:
        def sb(n, shape, dt=F32):
            return c.enter_context(nc.sbuf_tensor(f"{name}_{n}", shape, dt))

        def ps(n, shape):
            return c.enter_context(nc.psum_tensor(f"{name}_{n}", shape, F32))

        new_sem = c.enter_context(stage_semaphores(nc))

        def sem(n):
            return new_sem(f"{name}_{n}")

        xn = sb("xn", [P, 2, P])
        xt = sb("xt", [P, 2, P])
        q_sb = sb("q", [P, 2, P])
        k_sb = sb("k", [P, 2, P])
        qm = sb("qm", [P, 2, GRP, P])
        km = sb("km", [P, 2, GRP, P])
        vbd = sb("vbd", [P, 4, 2, PAIRS, 2, D0 + 1])
        sd = sb("sd", [P, 2, H0, SEQ])
        mx = sb("mx", [P, 2, H0])
        pt = sb("pt", [P, 2, PAIRS, P])
        rec = sb("rec", [P, 2, H0])
        o_sb = sb("o", [P, 2, H0, D0])
        ctx_t = sb("ctx_t", [P, 4, P]) if cross else None
        ot_sb = sb("ot", [P, 2, P])
        xb = sb("xb", [P, 2, P])
        row = sb("row", [P, 2, P])
        st = sb("st", [P, 2, 6])
        mv = sb("mv", [P, 2, 2])

        ps_xt = ps("ps_xt", [P, 512])
        ps_qkv = ps("ps_qkv", [P, 4, P])
        ps_s = ps("ps_s", [P, H0, SEQ])
        ps_pt = ps("ps_pt", [P, PAIRS, P])
        ps_o = ps("ps_o", [P, 512])
        ps_y = ps("ps_y", [P, 512])
        o_ps = ps_o[:, 0:H0 * (D0 + 1)].rearrange("p (h d) -> p h d", d=D0 + 1)
        ot_ps, y_ps = ps_y[:, 0:P], ps_y[:, P:2 * P]

        setup = sem("setup")
        ctx_loaded = [sem(f"ctx_loaded{n}") for n in range(4)]
        xn_ready = sem("xn_ready")
        xt_made = sem("xt_made")
        xt_ready = sem("xt_ready")
        qkv_made = sem("qkv_made")
        qkv_ready = sem("qkv_ready")
        masked = sem("masked")
        s_made = sem("s_made")
        s_taken = sem("s_taken")
        mx_ready = sem("mx_ready")
        sub_ready = sem("sub_ready")
        p_ready = sem("p_ready")
        pt_made = sem("pt_made")
        pt_ready = sem("pt_ready")
        o_made = sem("o_made")
        rec_ready = sem("rec_ready")
        o_ready = sem("o_ready")
        ot_made = sem("ot_made")
        ot_ready = sem("ot_ready")
        y_made = sem("y_made")
        xb_ready = sem("xb_ready")
        x_added = sem("x_added")
        st_ready = sem("st_ready")
        mv_ready = sem("mv_ready")
        mv_kept = sem("mv_kept")

        nc.scalar.preload_act_table(ACT.Exp)
        block = c.enter_context(nc.Block())

        @block.sync
        def _(sp):
            if not cross:
                return

            def load_ctx(t, u):
                if late(t, 4):
                    sp.wait_ge(qkv_made, t - 3)
                sp.dma_start(ctx_t[:, u, :], k.in_ctx_t[t]).then_inc(ctx_loaded[u], 16)

            pipeline(sp, NT, load_ctx, 0)

        @block.gpsimd
        def _(pool):
            pool.memset(vbd[:], 0.0).then_inc(setup, 1)
            pool.wait_ge(setup, 1)
            pool.memset(vbd[0:SEQ, :, :, :, 0, D0:D0 + 1], 1.0)
            pool.memset(vbd[SEQ:P, :, :, :, 1, D0:D0 + 1], 1.0).then_inc(setup, 1)

            def subtract_max(t, v):
                pool.wait_ge(mx_ready, t + 1)
                pool.tensor_tensor(sd[:, v % 2], sd[:, v % 2], mx[:, v % 2].unsqueeze(2).to_broadcast([P, H0, SEQ]),
                                   ALU.subtract).then_inc(sub_ready, 1)

            def split_heads(t, v):
                pool.wait_ge(qkv_ready, t + 1)
                if late(t, 2):
                    pool.wait_ge(s_made, t - 1)
                pool.tensor_tensor(km[:, v % 2], bc(k_sb[:, v % 2], 1, GRP), k.head_mask[:].to_broadcast([P, GRP, P]),
                                   ALU.mult)
                pool.tensor_tensor(qm[:, v % 2], bc(q_sb[:, v % 2], 1, GRP), k.group_mask[:].to_broadcast([P, GRP, P]),
                                   ALU.mult).then_inc(masked, 1)

            def add_bias(t, v):
                if cross:
                    pool.wait_ge(o_ready, t + 1)
                    if late(t, 2):
                        pool.wait_ge(mv_kept, t - 1)
                    pool.tensor_tensor(row[:, v % 2], o_sb[:, v % 2].rearrange("p h d -> p (h d)"), bv[:],
                                       ALU.add).then_inc(xb_ready, 1)
                else:
                    if late(t, 2):
                        pool.wait_ge(x_added, t - 1)
                    pool.tensor_tensor(xb[:, v % 2], k.x_res[:, t], k.a_bo[:], ALU.add).then_inc(xb_ready, 1)

            def step(i, u):
                for stage, behind in ((subtract_max, 4), (split_heads, 2), (add_bias, 5)):
                    if cross and stage is subtract_max:
                        continue
                    if has(i - behind, NT):
                        stage(i - behind, (u - behind) % UNROLL)

            pipeline(pool, NT, step, 5)

        @block.tensor
        def _(pe):
            pe.wait_ge(setup, 2)

            def x_transpose(t, v):
                pe.wait_ge(xn_ready, t + 1)
                if late(t, 1):
                    pe.wait_ge(xt_ready, t)
                pe.transpose(ps_xt[:, 0:P], xn[:, v % 2], k.ident[:]).then_inc(xt_made, 1)

            def project(t, v):
                pe.wait_ge(xt_ready, t + 1)
                if late(t, 1):
                    pe.wait_ge(qkv_ready, t)
                if cross:
                    pe.wait_ge(ctx_loaded[v], 16 + 4 * (t - v))
                kv = ctx_t[:, v] if cross else xt[:, v % 2]
                pe.matmul(ps_qkv[:, 0], wq[:], xt[:, v % 2], start=True, stop=True)
                pe.matmul(ps_qkv[:, 1], wk[:], kv, start=True, stop=True)
                for b in range(2):
                    for half in range(2):
                        mm = pe.matmul(ps_qkv[half * SEQ:(half + 1) * SEQ, 2 + b], kv[:, b * SEQ:(b + 1) * SEQ],
                                       wv[:], start=True, stop=True)
                mm.then_inc(qkv_made, 1)

            def scores(t, v):
                pe.wait_ge(masked, t + 1)
                if late(t, 1):
                    pe.wait_ge(s_taken, t)
                if cross:
                    for half in range(2):
                        pe.matmul(ps_s[:, 8 * half:8 * half + 8], k.ident_bf[:], bc(k.mask_all[:, t], 1, 8),
                                  start=True, stop=True)
                for g in range(GRP):
                    for b in range(2):
                        rows = slice(b * SEQ, (b + 1) * SEQ)
                        mm = pe.matmul(ps_s[rows, GRP * g:GRP * g + GRP], qm[:, v % 2, g, rows],
                                       km[:, v % 2, :, rows], start=not cross, stop=True, skip_group_check=cross)
                mm.then_inc(s_made, 1)

            def p_transpose(t, v):
                pe.wait_ge(p_ready, t + 1)
                if late(t, 1):
                    pe.wait_ge(pt_ready, t)
                flat = sd[:, v % 2].rearrange("p (n h) s -> p n (h s)", h=2)
                for n in range(PAIRS):
                    mm = pe.transpose(ps_pt[:, n], flat[:, n], k.ident[:])
                mm.then_inc(pt_made, 1)

            def values(t, v):
                pe.wait_ge(pt_ready, t + 1)
                if late(t, 1):
                    pe.wait_ge(o_ready, t)
                for n in range(PAIRS):
                    for b in range(2):
                        rows = slice(b * SEQ, (b + 1) * SEQ)
                        mm = pe.matmul(o_ps[rows, 2 * n:2 * n + 2], pt[:, v % 2, n, rows], vbd[:, v, b, n],
                                       start=True, stop=True)
                mm.then_inc(o_made, 1)

            def o_transpose(t, v):
                pe.wait_ge(o_ready, t + 1)
                if late(t, 1):
                    pe.wait_ge(x_added, t)
                pe.transpose(ot_ps, o_sb[:, v % 2].rearrange("p h d -> p (h d)"), k.ident[:]).then_inc(ot_made, 1)

            def out_project(t, v):
                pe.wait_ge(ot_ready, t + 1)
                pe.matmul(y_ps, ot_sb[:, v % 2], k.a_wo[:], start=True, stop=True).then_inc(y_made, 1)

            def step(i, u):
                for stage, behind in ((x_transpose, 1), (o_transpose, 6), (p_transpose, 5), (project, 2),
                                      (out_project, 6), (values, 5), (scores, 3)):
                    if cross and stage in (o_transpose, out_project):
                        continue
                    if has(i - behind, NT):
                        stage(i - behind, (u - behind) % UNROLL)

            pipeline(pe, NT, step, 6)

        @block.scalar
        def _(act):
            act.wait_ge(setup, 2)

            def x_copy(t, v):
                act.wait_ge(xt_made, t + 1)
                if late(t, 2):
                    act.wait_ge(qkv_made, t - 1)
                act.copy(xt[:, v % 2], ps_xt[:, 0:P]).then_inc(xt_ready, 1)

            def qkv_copy(t, v):
                act.wait_ge(qkv_made, t + 1)
                if late(t, 2):
                    act.wait_ge(masked, t - 1)
                act.activation(k_sb[:, v % 2], ps_qkv[:, 1], ACT.Identity, bias=bk[:])
                act.activation(q_sb[:, v % 2], ps_qkv[:, 0], ACT.Identity, bias=bq[:])
                if late(t, 4):
                    act.wait_ge(o_made, t - 3)
                for half in range(2):
                    rows = slice(half * SEQ, (half + 1) * SEQ)
                    src = ps_qkv[rows, 2:4].rearrange("p b (n h d) -> p b n h d", h=2, d=D0)
                    op = act.copy(vbd[rows, v, :, :, half, 0:D0], src[:, :, :, half])
                op.then_inc(qkv_ready, 1)

            def exponential(t, v):
                act.wait_ge(s_taken if cross else sub_ready, t + 1)
                act.activation(sd[:, v % 2], sd[:, v % 2], ACT.Exp, scale=scale).then_inc(p_ready, 1)

            def p_copy(t, v):
                act.wait_ge(pt_made, t + 1)
                if late(t, 2):
                    act.wait_ge(o_made, t - 1)
                act.copy(pt[:, v % 2], ps_pt[:]).then_inc(pt_ready, 1)

            def o_copy(t, v):
                act.wait_ge(ot_made, t + 1)
                if late(t, 2):
                    act.wait_ge(y_made, t - 1)
                act.activation(ot_sb[:, v % 2], ot_ps, ACT.Identity, bias=bv[:]).then_inc(ot_ready, 1)

            def step(i, u):
                for stage, behind in ((x_copy, 1), (o_copy, 6), (p_copy, 5), (qkv_copy, 2), (exponential, 4)):
                    if cross and stage is o_copy:
                        continue
                    if has(i - behind, NT):
                        stage(i - behind, (u - behind) % UNROLL)

            pipeline(act, NT, step, 6)

        @block.vector
        def _(dve):
            def normalise(t, v):
                if late(t, 2):
                    dve.wait_ge(xt_made, t - 1)
                dve.tensor_scalar(xn[:, v % 2], k.x_res[:, t], k.ln_scale[:, bass.ds(t, 1)], k.ln_shift[:, bass.ds(t, 1)],
                                  ALU.mult, ALU.add).then_inc(xn_ready, 1)

            def softmax(t, v):
                dve.wait_ge(s_made, t + 1)
                if late(t, 2):
                    dve.wait_ge(pt_made, t - 1)
                if cross:
                    dve.tensor_reduce(mx[:, v % 2], ps_s[:], AX.X, ALU.max).then_inc(mx_ready, 1)
                    dve.wait_ge(mx_ready, t + 1)
                    dve.tensor_tensor(sd[:, v % 2], ps_s[:], mx[:, v % 2].unsqueeze(2).to_broadcast([P, H0, SEQ]),
                                      ALU.subtract).then_inc(s_taken, 1)
                else:
                    dve.tensor_tensor(sd[:, v % 2], ps_s[:], bc(k.decay[:], 1, H0), ALU.mult).then_inc(s_taken, 1)
                    dve.wait_ge(s_taken, t + 1)
                    dve.tensor_reduce(mx[:, v % 2], sd[:, v % 2], AX.X, ALU.max).then_inc(mx_ready, 1)

            def divide(t, v):
                dve.wait_ge(o_made, t + 1)
                if late(t, 2):
                    dve.wait_ge(xb_ready if cross else ot_made, t - 1)
                dve.reciprocal(rec[:, v % 2], o_ps[:, :, D0]).then_inc(rec_ready, 1)
                dve.wait_ge(rec_ready, t + 1)
                dve.tensor_tensor(o_sb[:, v % 2], o_ps[:, :, 0:D0], rec[:, v % 2].unsqueeze(2).to_broadcast([P, H0, D0]),
                                  ALU.mult).then_inc(o_ready, 1)

            def residual(t, v):
                all_rows, all_stats = (k.o_all, k.o_mean_var) if cross else (k.x_res, k.mean_var)
                dve.wait_ge(xb_ready, t + 1)
                if late(t, 2):
                    dve.wait_ge(mv_kept, t - 1)
                if not cross:
                    dve.wait_ge(y_made, t + 1)
                    dve.tensor_tensor(row[:, v % 2], y_ps, xb[:, v % 2], ALU.add).then_inc(x_added, 1)
                    dve.wait_ge(x_added, t + 1)
                keep_with_stats(dve, row[:, v % 2], all_rows[:, t], st[:, v % 2], mv[:, v % 2], all_stats[:, t], t,
                                st_ready, mv_ready, mv_kept)

            def step(i, u):
                for stage, behind in ((softmax, 4), (residual, 6), (divide, 5), (normalise, 0)):
                    if has(i - behind, NT):
                        stage(i - behind, (u - behind) % UNROLL)

            pipeline(dve, NT, step, 6)


def project_cross(nc, k):
    NT = k.tiles
    with ExitStack() as c:
        def sb(n, shape, dt=F32):
            return c.enter_context(nc.sbuf_tensor(f"xp_{n}", shape, dt))

        new_sem = c.enter_context(stage_semaphores(nc))

        def sem(n):
            return new_sem(f"xp_{n}")

        on = sb("on", [P, 4, P])
        ot = sb("ot", [P, 4, P])
        xb = sb("xb", [P, 4, P])
        row = sb("row", [P, 4, P])
        st = sb("st", [P, 4, 6])
        mv = sb("mv", [P, 4, 2])
        ps_t = [c.enter_context(nc.psum_tensor(f"xp_t{n}", [P, 512], F32)) for n in range(4)]
        ps_y = [c.enter_context(nc.psum_tensor(f"xp_y{n}", [P, 512], F32)) for n in range(4)]
        on_ready, ot_made, ot_ready, y_made = sem("on_ready"), sem("ot_made"), sem("ot_ready"), sem("y_made")
        xb_ready, x_added, st_ready, mv_ready = sem("xb_ready"), sem("x_added"), sem("st_ready"), sem("mv_ready")
        stored = [sem(f"stored{n}") for n in range(4)]
        mv_kept, zeroed, zeros_stored = sem("mv_kept"), sem("zeroed"), sem("zeros_stored")
        zero_row = sb("zero_row", [P, P])
        block = c.enter_context(nc.Block())

        @block.gpsimd
        def _(pool):
            pool.memset(zero_row[:], 0.0).then_inc(zeroed, 1)

            def step(t, u):
                if late(t, 4):
                    pool.wait_ge(x_added, t - 3)
                pool.tensor_tensor(xb[:, u], k.x_res[:, t], k.x_bo[:], ALU.add).then_inc(xb_ready, 1)

            pipeline(pool, NT, step, 0)

        @block.tensor
        def _(pe):
            def step(i, u):
                if has(i, NT):
                    pe.wait_ge(on_ready, i + 1)
                    if late(i, 4):
                        pe.wait_ge(ot_ready, i - 3)
                    pe.transpose(ps_t[u][:, 0:P], on[:, u], k.ident[:]).then_inc(ot_made, 1)
                t, v = i - 2, (u - 2) % 4
                if late(t, 0):
                    pe.wait_ge(ot_ready, t + 1)
                    if late(t, 4):
                        pe.wait_ge(x_added, t - 3)
                    pe.matmul(ps_y[v][:, 0:P], ot[:, v], k.x_wo[:], start=True, stop=True).then_inc(y_made, 1)

            pipeline(pe, NT, step, 2)

        @block.scalar
        def _(act):
            def step(t, u):
                act.wait_ge(ot_made, t + 1)
                if late(t, 4):
                    act.wait_ge(y_made, t - 3)
                act.activation(ot[:, u], ps_t[u][:, 0:P], ACT.Identity, scale=k.x_ln_g[:], bias=k.x_ln_b[:])\
                   .then_inc(ot_ready, 1)

            pipeline(act, NT, step, 0)

        @block.sync
        def _(sp):
            def step(t, u):
                sp.wait_ge(x_added, t + 1)
                sp.dma_start(k.x_dram[t], row[:, u]).then_inc(stored[u], 16)

            sp.wait_ge(zeroed, 1)
            sp.dma_start(k.x_dram[NT:NT + NE * CAP // P].rearrange("n p c -> p n c"),
                         bc(zero_row[:], 1, NE * CAP // P)).then_inc(zeros_stored, 16)
            pipeline(sp, NT, step, 0)
            for n in range(4):
                sp.wait_ge(stored[n], 16 * len(range(n, NT, 4)))
            sp.wait_ge(zeros_stored, 16)

        @block.vector
        def _(dve):
            def step(i, u):
                if has(i, NT):
                    if late(i, 4):
                        dve.wait_ge(ot_made, i - 3)
                    dve.tensor_scalar(on[:, u], k.o_all[:, i], k.o_scale[:, bass.ds(i, 1)], k.o_shift[:, bass.ds(i, 1)],
                                      ALU.mult, ALU.add).then_inc(on_ready, 1)
                t, v = i - 3, (u - 3) % 4
                if late(t, 0):
                    dve.wait_ge(xb_ready, t + 1)
                    dve.wait_ge(y_made, t + 1)
                    if late(t, 4):
                        dve.wait_ge(mv_kept, t - 3)
                        dve.wait_ge(stored[v], 4 * (t - v))
                    dve.tensor_tensor(row[:, v], ps_y[v][:, 0:P], xb[:, v], ALU.add).then_inc(x_added, 1)
                    dve.wait_ge(x_added, t + 1)
                    keep_with_stats(dve, row[:, v], k.x_res[:, t], st[:, v], mv[:, v], k.mean_var[:, t], t,
                                    st_ready, mv_ready, mv_kept)

            pipeline(dve, NT, step, 3)


def set_up(nc, k):
    NT = k.tiles
    chunk = 4
    with ExitStack() as c:
        new_sem = c.enter_context(stage_semaphores(nc))

        def sem(n):
            return new_sem(f"su_{n}")

        dist = c.enter_context(nc.sbuf_tensor("su_dist", [P, SEQ], F32))
        dd = c.enter_context(nc.sbuf_tensor("su_dd", [P, 1], F32))
        dd_neg = c.enter_context(nc.sbuf_tensor("su_dd_neg", [P, 1], F32))
        dd_abs = c.enter_context(nc.sbuf_tensor("su_dd_abs", [P, 1], F32))
        mask_in = c.enter_context(nc.sbuf_tensor("su_mask", [P, NT, SEQ], I32))
        st = c.enter_context(nc.sbuf_tensor("su_st", [P, 2, 6], F32))
        x_loaded = [sem(f"x_loaded{n}") for n in range(NT // chunk)]
        loaded, mask_loaded, dd_loaded = sem("loaded"), sem("mask_loaded"), sem("dd_loaded")
        dd_ready, dec, st_ready, mv_ready = sem("dd_ready"), sem("dec"), sem("st_ready"), sem("mv_ready")
        mask_ready = sem("mask_ready")
        block = c.enter_context(nc.Block())

        @block.sync
        def _(sp):
            for n in range(NT // chunk):
                sp.dma_start(k.x_res[:, n * chunk:(n + 1) * chunk],
                             k.in_x[n * chunk:(n + 1) * chunk].rearrange("n p c -> p n c")).then_inc(x_loaded[n], 16)
            sp.dma_start(mask_in[:], k.in_mask.rearrange("n p s -> p n s")).then_inc(mask_loaded, 16)

        @block.scalar
        def _(act):
            act.dma_start(dist[:], k.in_dist).then_inc(dd_loaded, 16)
            act.dma_start(dd[:], k.in_dd.to_broadcast([P, 1])).then_inc(dd_loaded, 16)
            for tile, src in k.loads:
                act.dma_start(tile, src).then_inc(loaded, 16)
            act.wait_ge(dd_ready, 2)
            act.activation(k.decay[:], dist[:], ACT.Exp, scale=dd_abs[:]).then_inc(dec, 1)
            act.wait_ge(loaded, 16 * len(k.loads))

        @block.vector
        def _(dve):
            dve.wait_ge(dd_loaded, 32)
            dve.tensor_scalar(dd_neg[:], dd[:], -1.0, None, ALU.mult).then_inc(dd_ready, 1)
            dve.wait_ge(dd_ready, 1)
            dve.tensor_tensor(dd_abs[:], dd[:], dd_neg[:], ALU.min).then_inc(dd_ready, 1)
            for n in range(NT // chunk):
                dve.wait_ge(x_loaded[n], 16)
                for t in range(n * chunk, (n + 1) * chunk):
                    if t >= 2:
                        dve.wait_ge(mv_ready, t - 1)
                    dve.bn_stats(st[:, t % 2], k.x_res[:, t]).then_inc(st_ready, 1)
                    dve.wait_ge(st_ready, t + 1)
                    dve.bn_aggr(k.mean_var[:, t], st[:, t % 2]).then_inc(mv_ready, 1)
            dve.wait_ge(mask_loaded, 16)
            dve.wait_ge(loaded, 16 * len(k.loads))
            dve.tensor_scalar(k.mask_all[:], mask_in[:], 0.0, NEG, ALU.is_equal, ALU.mult).then_inc(mask_ready, 1)
            dve.wait_ge(mask_ready, 1)
            dve.tensor_tensor(k.mask_all[:], k.mask_all[:], bc(k.causal[:], 1, NT), ALU.min)


def router(nc, k, name, weight, bias, xn_dram, x_copy_dram):
    NT = k.tiles
    with ExitStack() as c:
        def sb(n, shape, dt=F32):
            return c.enter_context(nc.sbuf_tensor(f"{name}_{n}", shape, dt))

        new_sem = c.enter_context(stage_semaphores(nc))

        def sem(n):
            return new_sem(f"{name}_{n}")

        xn = sb("xn", [P, 4, P])
        xt = sb("xt", [P, 4, P])
        ps_t = [c.enter_context(nc.psum_tensor(f"{name}_t{n}", [P, 512], F32)) for n in range(4)]
        ps_l = [c.enter_context(nc.psum_tensor(f"{name}_l{n}", [P, 512], F32)) for n in range(4)]
        xn_ready, xt_made, xt_ready = sem("xn_ready"), sem("xt_made"), sem("xt_ready")
        l_made, l_ready, x_stored = sem("l_made"), sem("l_ready"), sem("x_stored")
        xn_stored = [sem(f"xn_stored{n}") for n in range(4)]
        block = c.enter_context(nc.Block())

        @block.sync
        def _(sp):
            def step(t, u):
                sp.wait_ge(xn_ready, t + 1)
                sp.dma_start(xn_dram[t], xn[:, u]).then_inc(xn_stored[u], 16)
                if x_copy_dram is not None:
                    sp.dma_start(x_copy_dram[t], k.x_res[:, t]).then_inc(x_stored, 16)

            pipeline(sp, NT, step, 0)
            for n in range(4):
                sp.wait_ge(xn_stored[n], 16 * len(range(n, NT, 4)))
            if x_copy_dram is not None:
                sp.wait_ge(x_stored, 16 * NT)

        @block.tensor
        def _(pe):
            def step(i, u):
                if has(i, NT):
                    pe.wait_ge(xn_ready, i + 1)
                    if late(i, 4):
                        pe.wait_ge(xt_ready, i - 3)
                    pe.transpose(ps_t[u][:, 0:P], xn[:, u], k.ident[:]).then_inc(xt_made, 1)
                t, v = i - 2, (u - 2) % 4
                if late(t, 0):
                    pe.wait_ge(xt_ready, t + 1)
                    if late(t, 4):
                        pe.wait_ge(l_ready, t - 3)
                    pe.matmul(ps_l[v][:, 0:NE], xt[:, v], weight[:], start=True, stop=True).then_inc(l_made, 1)

            pipeline(pe, NT, step, 2)

        @block.scalar
        def _(act):
            def step(t, u):
                act.wait_ge(xt_made, t + 1)
                if late(t, 4):
                    act.wait_ge(l_made, t - 3)
                act.copy(xt[:, u], ps_t[u][:, 0:P]).then_inc(xt_ready, 1)

            pipeline(act, NT, step, 0)

        @block.vector
        def _(dve):
            def step(i, u):
                if has(i, NT):
                    if late(i, 4):
                        dve.wait_ge(xt_made, i - 3)
                        dve.wait_ge(xn_stored[u], 4 * (i - u))
                    dve.tensor_scalar(xn[:, u], k.x_res[:, i], k.ln_scale[:, bass.ds(i, 1)], k.ln_shift[:, bass.ds(i, 1)],
                                      ALU.mult, ALU.add).then_inc(xn_ready, 1)
                t, v = i - 3, (u - 3) % 4
                if late(t, 0):
                    dve.wait_ge(l_made, t + 1)
                    dve.tensor_tensor(k.logits[:, t], ps_l[v][:, 0:NE], bias[:], ALU.add).then_inc(l_ready, 1)

            pipeline(dve, NT, step, 3)


def chosen_slots(nc, k, name, top, slots, w_slot):
    NT = k.tiles
    NS = slots
    with ExitStack() as c:
        def sb(n, shape, dt=F32):
            return c.enter_context(nc.sbuf_tensor(f"{name}_{n}", shape, dt))

        new_sem = c.enter_context(stage_semaphores(nc))

        def sem(n):
            return new_sem(f"{name}_{n}")

        E = [P, NT, NE]
        m = sb("m", [P, top, NT])
        key = sb("key", E)
        first = sb("first", [P, NT])
        oh = [sb(f"oh{n}", E) for n in range(top)]
        rest = sb("rest", E)
        sel_bf = sb("sel_bf", E, BF16)
        total = sb("total", E)
        rank = sb("rank", E)
        slot_e = sb("slot_e", E)
        keep = sb("keep", E)
        tmp = sb("tmp", E)
        slot = sb("slot", [P, top, NT])
        slot_i = sb("slot_i", [P, top, NT], I32)
        part_i = sb("part_i", [P, 2, top, NT], I32)
        part = sb("part", [P, 2, top, NT])
        zeros = sb("zeros", [P, NT])
        small = sb("small", [P, 6, NE])
        small_i = sb("small_i", [P, 2, NE], I32)
        lists = 5 if top == 2 else 2
        row_hot = sb("row_hot", [P, NT, P], BF16)
        tile_hot = sb("tile_hot", [P, NT, NS], BF16)
        listed = sb("listed", [P, NT, lists, NS], BF16)
        w = sb("w", [P, 4, NT])
        parts = sb("parts", [P, 2, 3, NT])
        parts_bf = sb("parts_bf", [P, 2, 3, NT], BF16)
        table = sb("table", [P, lists, NS])
        ids = sb("ids", [P, 5, NS])
        ge = sb("ge", [P, NS, NE]) if top == 1 else None
        ps_r = c.enter_context(nc.psum_tensor(f"{name}_r", [P, 512], F32))
        ps_n = c.enter_context(nc.psum_tensor(f"{name}_n", [P, 512], F32))
        ps_l = c.enter_context(nc.psum_tensor(f"{name}_l", [P, 512], F32))
        done = sem("done")
        e_ready = sem("e_ready")
        d_ready = sem("d_ready")
        sel_ready, ranks_made = sem("sel_ready"), sem("ranks_made")
        listed_ready, listed_made = sem("listed_ready"), sem("listed_made")
        block = c.enter_context(nc.Block())

        @block.scalar
        def _(act):
            if top == 2:
                act.wait_ge(d_ready, 1)
                act.activation(w[:, 1], w[:, 0], ACT.Exp).then_inc(e_ready, 1)

        @block.tensor
        def _(pe):
            flat = sel_bf[:].rearrange("p n e -> p (n e)")
            pe.wait_ge(sel_ready, 1)
            pe.matmul(ps_r[:, 0:NT * NE], k.before[:], flat, start=True, stop=True)
            pe.matmul(ps_n[:, 0:NT * NE], k.ones_bf[:], flat, start=True, stop=True).then_inc(ranks_made, 1)
            for n in range(top):
                pe.wait_ge(listed_ready, n + 1)
                for t in range(NT):
                    mm = pe.matmul(ps_l[:, 0:lists * NS], row_hot[:, t], listed[:, t].rearrange("p l s -> p (l s)"),
                                   start=(n == 0 and t == 0), stop=(n == top - 1 and t == NT - 1))
                mm.then_inc(listed_made, 1)

        @block.vector
        def _(dve):
            count = [0]

            def op(instruction):
                count[0] += 1
                instruction.then_inc(done, 1)
                dve.wait_ge(done, count[0])

            def all_e(ap):
                return ap.unsqueeze(2).to_broadcast(E)

            scores = k.logits
            for n in range(top):
                op(dve.tensor_reduce(m[:, n], scores[:], AX.X, ALU.max))
                op(dve.tensor_tensor(oh[n][:], scores[:], all_e(m[:, n]), ALU.is_equal))
                op(dve.scalar_tensor_tensor(out=key[:], in0=oh[n][:], scalar=-float(NE), in1=bc(k.iota_e[:], 1, NT),
                                            op0=ALU.mult, op1=ALU.add))
                op(dve.tensor_reduce(first[:], key[:], AX.X, ALU.min))
                op(dve.tensor_tensor(oh[n][:], key[:], all_e(first[:]), ALU.is_equal))
                if n == 0 and top == 2:
                    op(dve.scalar_tensor_tensor(out=rest[:], in0=oh[0][:], scalar=-3e38, in1=scores[:],
                                                op0=ALU.mult, op1=ALU.add))
                    scores = rest
            if top == 2:
                dve.tensor_tensor(w[:, 0], m[:, 1], m[:, 0], ALU.subtract).then_inc(d_ready, 1)
                op(dve.tensor_tensor(sel_bf[:], oh[0][:], oh[1][:], ALU.add))
            else:
                op(dve.tensor_copy(sel_bf[:], oh[0][:]))
            dve.memset(zeros[:], 0.0).then_inc(sel_ready, 1)

            dve.wait_ge(ranks_made, 1)
            op(dve.tensor_copy(total[:], ps_n[:, 0:NT * NE].rearrange("p (n e) -> p n e", e=NE)))
            for e in range(NE):
                op(dve.tensor_tensor_scan(rank[:, :, e], total[:, :, e], zeros[:], 0.0, ALU.add, ALU.add))
            if top == 1:
                op(dve.tensor_scalar(small_i[:, 0], rank[:, NT - 1], float(P - 1), None, ALU.add))
                op(dve.tensor_scalar(small_i[:, 1], small_i[:, 0], 7, None, ALU.arith_shift_right))
                op(dve.tensor_copy(small[:, 0], small_i[:, 1]))
                op(dve.tensor_tensor_scan(small[:, 1], small[:, 0], zeros[:, 0:NE], 0.0, ALU.add, ALU.add))
                op(dve.tensor_tensor(small[:, 2], small[:, 1], small[:, 0], ALU.subtract))
                op(dve.tensor_scalar(small[:, 3], small[:, 2], float(P), 1.0, ALU.mult, ALU.add))
                op(dve.tensor_tensor(ge[:], k.iota_s[:, 0:NS].unsqueeze(2).to_broadcast([P, NS, NE]),
                                     bc(small[:, 1], 1, NS), ALU.is_ge))
                op(dve.tensor_reduce(ids[:, 0], ge[:], AX.X, ALU.add))
                op(dve.tensor_scalar(k.tile_expert[:], ids[:, 0], float(NE - 1), None, ALU.min))
            op(dve.tensor_tensor(rank[:], rank[:], total[:], ALU.subtract))
            op(dve.tensor_tensor(rank[:], rank[:], ps_r[:, 0:NT * NE].rearrange("p (n e) -> p n e", e=NE), ALU.add))
            first_slot = k.iota_cap[:] if top == 2 else small[:, 3]
            op(dve.tensor_tensor(slot_e[:], rank[:], bc(first_slot, 1, NT), ALU.add))
            if top == 2:
                op(dve.tensor_scalar(keep[:], rank[:], float(CAP), None, ALU.is_lt))
                op(dve.tensor_tensor(slot_e[:], slot_e[:], keep[:], ALU.mult))
            for n in range(top):
                op(dve.tensor_tensor(tmp[:], slot_e[:], oh[n][:], ALU.mult))
                op(dve.tensor_reduce(slot[:, n], tmp[:], AX.X, ALU.add))
            op(dve.tensor_scalar(slot_i[:], slot[:], -1.0, None, ALU.add))
            op(dve.tensor_scalar(part_i[:, 0], slot_i[:], 7, None, ALU.arith_shift_right))
            op(dve.tensor_scalar(part_i[:, 1], slot_i[:], P - 1, None, ALU.bitwise_and))
            op(dve.tensor_copy(part[:], part_i[:]))

            if top == 2:
                dve.wait_ge(e_ready, 1)
                op(dve.tensor_scalar(w[:, 0], w[:, 1], 1.0, None, ALU.add))
                op(dve.reciprocal(w[:, 2], w[:, 0]))
                op(dve.tensor_tensor(w[:, 3], w[:, 1], w[:, 2], ALU.mult))
                op(dve.tensor_copy(parts[:, :, 0], w[:, 2:4]))
                for n in range(3):
                    op(dve.tensor_copy(parts_bf[:, :, n], parts[:, :, n]))
                    if n < 2:
                        op(dve.tensor_tensor(parts[:, :, n + 1], parts[:, :, n], parts_bf[:, :, n], ALU.subtract))

            for n in range(top):
                if n == 1:
                    dve.wait_ge(listed_made, 1)
                op(dve.tensor_tensor(row_hot[:], bc(k.iota_p[:], 1, NT),
                                     part[:, 1, n].unsqueeze(2).to_broadcast([P, NT, P]), ALU.is_equal))
                op(dve.tensor_tensor(tile_hot[:], bc(k.iota_s[:, 0:NS], 1, NT),
                                     part[:, 0, n].unsqueeze(2).to_broadcast([P, NT, NS]), ALU.is_equal))
                op(dve.tensor_tensor(listed[:, :, 0], tile_hot[:], k.iota_s1[:, 0:NT].unsqueeze(2).to_broadcast([P, NT, NS]),
                                     ALU.mult))
                op(dve.tensor_scalar(listed[:, :, 1], tile_hot[:], k.place[:], None, ALU.mult))
                for q in range(2, lists):
                    op(dve.tensor_tensor(listed[:, :, q], tile_hot[:],
                                         parts_bf[:, n, q - 2].unsqueeze(2).to_broadcast([P, NT, NS]), ALU.mult))
                dve.memset(zeros[:, 0:1], 0.0).then_inc(listed_ready, 1)
            dve.wait_ge(listed_made, top)
            op(dve.tensor_copy(table[:], ps_l[:, 0:lists * NS].rearrange("p (l s) -> p l s", s=NS)))
            op(dve.tensor_scalar(ids[:, 1], table[:, 0], float(P), -float(P), ALU.mult, ALU.add))
            op(dve.tensor_tensor(ids[:, 2], ids[:, 1], table[:, 1], ALU.add))
            op(dve.tensor_scalar(k.gather_idx[:, 0:NS], ids[:, 2], 0.0, None, ALU.max))
            op(dve.tensor_scalar(ids[:, 3], table[:, 0], 0.0, None, ALU.is_equal))
            op(dve.tensor_tensor(ids[:, 3], ids[:, 3], k.empty_id[:, 0:NS], ALU.mult))
            op(dve.tensor_tensor(k.scatter_idx[:, 0:NS], ids[:, 2], ids[:, 3], ALU.add))
            if top == 2:
                op(dve.tensor_tensor(w_slot[:], table[:, 4], table[:, 3], ALU.add))
                op(dve.tensor_tensor(w_slot[:], w_slot[:], table[:, 2], ALU.add))


def two_expert_ffn(nc, k):
    NT = k.tiles
    with ExitStack() as c:
        def sb(n, shape, dt=F32):
            return c.enter_context(nc.sbuf_tensor(f"m0_{n}", shape, dt))

        new_sem = c.enter_context(stage_semaphores(nc))

        def sem(n):
            return new_sem(f"m0_{n}")

        HALVES = CAP // P
        xg = sb("xg", [P, NE * HALVES, P])
        xgt = sb("xgt", [P, 2, CAP])
        gate = sb("gate", [P, 2, 2, CAP])
        hid = sb("hid", [P, 2, 2, CAP])
        y = sb("weighted", [P, NE * HALVES, P])
        st = sb("st", [P, 2, 6])
        ps_t = c.enter_context(nc.psum_tensor("m0_t", [P, 512], F32))
        ps_h = [c.enter_context(nc.psum_tensor(f"m0_h{n}", [P, 2, 2, CAP], F32)) for n in range(2)]
        ps_y = c.enter_context(nc.psum_tensor("m0_y", [P, 512], F32))
        gathered, added = k.gathered0, k.added0
        xt_made, xt_ready, h_made, gate_ready = sem("xt_made"), sem("xt_ready"), sem("h_made"), sem("gate_ready")
        hid_ready, y_made, y_ready = sem("hid_ready"), sem("y_made"), sem("y_ready")
        st_ready, mv_ready = sem("st_ready"), sem("mv_ready")
        chunk = 4
        x_loaded = [sem(f"x_loaded{n}") for n in range(4)]
        nc.scalar.preload_act_table(ACT.Silu)
        block = c.enter_context(nc.Block())

        @block.gpsimd
        def _(pool):
            for n in range(NE * HALVES):
                pool.indirect_dma_start(xg[:, n], None, k.xn_rows,
                                        bass.IndirectOffsetOnAxis(ap=k.gather_idx[:, n:n + 1], axis=0))\
                    .then_inc(gathered[n], 16)
            for e in range(NE):
                pool.wait_ge(y_ready, HALVES * (e + 1))
                if e:
                    pool.wait_ge(added[e - 1], 16 * HALVES)
                for half in range(HALVES):
                    n = HALVES * e + half
                    pool.indirect_dma_start(k.x_rows, bass.IndirectOffsetOnAxis(ap=k.scatter_idx[:, n:n + 1], axis=0),
                                            y[:, n], None, compute_op=ALU.add).then_inc(added[e], 16)

        @block.tensor
        def _(pe):
            def transposes(e):
                if e:
                    pe.wait_ge(xt_ready, e)
                for half in range(HALVES):
                    pe.wait_ge(gathered[HALVES * e + half], 16)
                    mm = pe.transpose(ps_t[:, half * P:(half + 1) * P], xg[:, HALVES * e + half], k.ident[:])
                mm.then_inc(xt_made, 1)

            def hidden(e):
                pe.wait_ge(xt_ready, e + 1)
                if e >= 2:
                    pe.wait_ge(hid_ready, e - 1)
                for n, weight in ((1, k.f0_v), (0, k.f0_w)):
                    for f in range(2):
                        mm = pe.matmul(ps_h[e % 2][:, n, f], weight[:, e, f * P:(f + 1) * P], xgt[:, e % 2],
                                       start=True, stop=True)
                mm.then_inc(h_made, 1)

            def output(e):
                pe.wait_ge(hid_ready, e + 1)
                if e:
                    pe.wait_ge(y_ready, HALVES * e)
                for half in range(HALVES):
                    for f in range(2):
                        mm = pe.matmul(ps_y[:, half * P:(half + 1) * P], hid[:, e % 2, f, half * P:(half + 1) * P],
                                       k.f0_out[:, e, f], start=(f == 0), stop=(f == 1))
                mm.then_inc(y_made, 1)

            for i in range(NE + 2):
                if i < NE:
                    transposes(i)
                if 1 <= i <= NE:
                    hidden(i - 1)
                if i >= 2:
                    output(i - 2)

        @block.scalar
        def _(act):
            for i in range(NE + 1):
                if i < NE:
                    act.wait_ge(xt_made, i + 1)
                    if i >= 2:
                        act.wait_ge(h_made, i - 1)
                    act.copy(xgt[:, i % 2], ps_t[:, 0:CAP]).then_inc(xt_ready, 1)
                if i >= 1:
                    e = i - 1
                    act.wait_ge(h_made, e + 1)
                    if e >= 2:
                        act.wait_ge(hid_ready, e - 1)
                    act.activation(gate[:, e % 2], ps_h[e % 2][:, 1], ACT.Silu).then_inc(gate_ready, 1)

        @block.sync
        def _(sp):
            for e in range(NE):
                sp.wait_ge(added[e], 16 * HALVES)
            for n in range(NT // chunk):
                if n >= 4:
                    sp.wait_ge(x_loaded[n % 4], 16 * (n // 4))
                sp.dma_start(k.x_res[:, n * chunk:(n + 1) * chunk],
                             k.x_dram[n * chunk:(n + 1) * chunk].rearrange("n p c -> p n c"))\
                    .then_inc(x_loaded[n % 4], 16)

        @block.vector
        def _(dve):
            for e in range(NE):
                dve.wait_ge(gate_ready, e + 1)
                if e >= 2:
                    dve.wait_ge(y_made, e - 1)
                dve.tensor_tensor(hid[:, e % 2], ps_h[e % 2][:, 0], gate[:, e % 2], ALU.mult).then_inc(hid_ready, 1)
                dve.wait_ge(y_made, e + 1)
                for half in range(HALVES):
                    n = HALVES * e + half
                    dve.tensor_scalar(y[:, n], ps_y[:, half * P:(half + 1) * P], k.w_slot[:, n:n + 1], None,
                                      ALU.mult).then_inc(y_ready, 1)
            for n in range(NT // chunk):
                dve.wait_ge(x_loaded[n % 4], 16 * (n // 4 + 1))
                for t in range(n * chunk, (n + 1) * chunk):
                    if t >= 2:
                        dve.wait_ge(mv_ready, t - 1)
                    dve.bn_stats(st[:, t % 2], k.x_res[:, t]).then_inc(st_ready, 1)
                    dve.wait_ge(st_ready, t + 1)
                    dve.bn_aggr(k.mean_var[:, t], st[:, t % 2]).then_inc(mv_ready, 1)


def wide_head_attention(nc, k):
    NT = k.tiles
    HALF = D1 // 2
    scale = float(D1) ** -0.5
    with ExitStack() as c:
        def sb(n, shape, dt=F32):
            return c.enter_context(nc.sbuf_tensor(f"wa_{n}", shape, dt))

        def ps(n, shape):
            return c.enter_context(nc.psum_tensor(f"wa_{n}", shape, F32))

        new_sem = c.enter_context(stage_semaphores(nc))

        def sem(n):
            return new_sem(f"wa_{n}")

        xn = sb("xn", [P, 2, P])
        xt = sb("xt", [P, 2, P])
        rot = [sb(f"rot{n}", [P, H1, 2, HALF]) for n in range(2)]
        cross = [sb(f"cross{n}", [P, H1, 2, HALF]) for n in range(2)]
        qt = sb("qt", [P, 2, PAIRS, P])
        kbd = sb("kbd", [P, 2, PAIRS, 2, P])
        vbd = sb("vbd", [P, 2, 2, PAIRS, 2, D1])
        sd = sb("sd", [P, 2, H1, SEQ])
        mx = sb("mx", [P, 2, H1])
        total = sb("total", [P, 2, H1])
        rec = sb("rec", [P, 2, H1])
        pt = sb("pt", [P, 2, PAIRS, P])
        o_sb = sb("o", [P, 2, H1, D1])
        ot = sb("ot", [P, 2, PAIRS, P])
        xb = sb("xb", [P, 2, P])
        row = sb("row", [P, 2, P])
        st = sb("st", [P, 2, 6])
        mv = sb("mv", [P, 2, 2])

        ps_p = ps("ps_p", [P, 2, 512])
        ps_t = ps("ps_t", [P, PAIRS, P])
        ps_s = ps("ps_s", [P, H1, SEQ])
        ps_o = ps("ps_o", [P, 2, 512])

        setup = sem("setup")
        xn_ready, xt_made, xt_ready = sem("xn_ready"), sem("xt_made"), sem("xt_ready")
        qk_made = [sem("q_made"), sem("k_made")]
        crossed = [sem("q_crossed"), sem("k_crossed")]
        rotated = [sem("q_rotated"), sem("k_rotated")]
        qk_t_made = [sem("qt_made"), sem("kt_made")]
        qk_t_ready = [sem("qt_ready"), sem("kt_ready")]
        v_made, v_ready = sem("v_made"), sem("v_ready")
        s_made, mx_ready, s_taken, p_ready = sem("s_made"), sem("mx_ready"), sem("s_taken"), sem("p_ready")
        total_ready, rec_ready = sem("total_ready"), sem("rec_ready")
        pt_made, pt_ready = sem("pt_made"), sem("pt_ready")
        o_made, o_ready, ot_made, ot_ready = sem("o_made"), sem("o_ready"), sem("ot_made"), sem("ot_ready")
        y_made, xb_ready, x_added = sem("y_made"), sem("xb_ready"), sem("x_added")
        st_ready, mv_ready, mv_kept = sem("st_ready"), sem("mv_ready"), sem("mv_kept")

        TURNS = [("o", 3, ot_ready), ("q", 1, qk_t_ready[0]), ("p", 2, pt_ready),
                 ("k", 1, qk_t_ready[1])]

        def wait_for_turn(pe, user, i):
            at = [n for n, _, _ in TURNS].index(user)
            for back in range(1, 4 * len(TURNS)):
                steps, n = divmod(at - back, len(TURNS))
                _, behind, copied = TURNS[n]
                t = i + steps - behind
                if has(t, NT):
                    pe.wait_ge(copied, t + 1)
                    return

        nc.scalar.preload_act_table(ACT.Exp)
        block = c.enter_context(nc.Block())

        @block.gpsimd
        def _(pool):
            pool.memset(kbd[:], 0.0)
            pool.memset(vbd[:], 0.0).then_inc(setup, 1)

            def step(i, u):
                t, v = i - 3, (u - 3) % 2
                if has(t, NT):
                    if late(t, 2):
                        pool.wait_ge(x_added, t - 1)
                    pool.tensor_tensor(xb[:, v], k.x_res[:, t], k.l1_bo[:], ALU.add).then_inc(xb_ready, 1)
                t = i - 1
                if has(t, NT):
                    for n in range(2):
                        pool.wait_ge(crossed[n], t + 1)
                        pool.tensor_tensor(rot[n][:], rot[n][:], cross[n][:], ALU.add).then_inc(rotated[n], 1)

            pipeline(pool, NT, step, 3, 2, 6)

        @block.tensor
        def _(pe):
            pe.wait_ge(setup, 1)

            def x_transpose(i, t, v):
                pe.wait_ge(xn_ready, t + 1)
                pe.transpose(ps_o[:, 1, 0:P], xn[:, v], k.ident[:]).then_inc(xt_made, 1)

            def project(n):
                def stage(i, t, v):
                    if n == 0:
                        pe.wait_ge(xt_ready, t + 1)
                        if late(t, 1):
                            pe.wait_ge(v_ready, t)
                    else:
                        pe.wait_ge(crossed[0], t + 1)
                    weight = (k.l1_wq, k.l1_wk)[n]
                    for half in range(2):
                        mm = pe.matmul(ps_p[:, half], xt[:, v], weight[:, half * 512:(half + 1) * 512],
                                       start=True, stop=True)
                    mm.then_inc(qk_made[n], 1)
                return stage

            def project_v(i, t, v):
                pe.wait_ge(crossed[1], t + 1)
                for b in range(2):
                    for half in range(2):
                        mm = pe.matmul(ps_p[half * SEQ:(half + 1) * SEQ, b], xt[:, v, b * SEQ:(b + 1) * SEQ],
                                       k.l1_wv[:, half], start=True, stop=True)
                mm.then_inc(v_made, 1)

            def qk_transpose(n):
                def stage(i, t, v):
                    pe.wait_ge(rotated[n], t + 1)
                    wait_for_turn(pe, "qk"[n], i)
                    flat = rot[n][:].rearrange("p (n h) s d -> p n (h s d)", h=2)
                    for m in range(PAIRS):
                        mm = pe.transpose(ps_t[:, m], flat[:, m], k.ident[:])
                    mm.then_inc(qk_t_made[n], 1)
                return stage

            def scores(i, t, v):
                pe.wait_ge(qk_t_ready[0], t + 1)
                pe.wait_ge(qk_t_ready[1], t + 1)
                if late(t, 1):
                    pe.wait_ge(s_taken, t)
                for half in range(2):
                    pe.matmul(ps_s[:, 8 * half:8 * half + 8], k.ident_bf[:], bc(k.causal[:], 1, 8),
                              start=True, stop=True)
                for m in range(PAIRS):
                    for b in range(2):
                        rows = slice(b * SEQ, (b + 1) * SEQ)
                        mm = pe.matmul(ps_s[rows, 2 * m:2 * m + 2], qt[:, v, m, rows], kbd[:, v, m, :, rows],
                                       start=False, stop=True, skip_group_check=True)
                mm.then_inc(s_made, 1)

            def p_transpose(i, t, v):
                pe.wait_ge(p_ready, t + 1)
                wait_for_turn(pe, "p", i)
                flat = sd[:, v].rearrange("p (n h) s -> p n (h s)", h=2)
                for m in range(PAIRS):
                    mm = pe.transpose(ps_t[:, m], flat[:, m], k.ident[:])
                mm.then_inc(pt_made, 1)

            def values(i, t, v):
                pe.wait_ge(pt_ready, t + 1)
                pe.wait_ge(v_ready, t + 1)
                if late(t, 1):
                    pe.wait_ge(x_added, t)
                if has(i, NT):
                    pe.wait_ge(xt_ready, i + 1)
                for m in range(PAIRS):
                    for b in range(2):
                        rows = slice(b * SEQ, (b + 1) * SEQ)
                        mm = pe.matmul(ps_o[rows, m // 4, m % 4 * P:(m % 4 + 1) * P], pt[:, v, m, rows], vbd[:, v, b, m],
                                       start=True, stop=True)
                mm.then_inc(o_made, 1)

            def o_transpose(i, t, v):
                pe.wait_ge(o_ready, t + 1)
                wait_for_turn(pe, "o", i)
                flat = o_sb[:, v].rearrange("p (n h) d -> p n (h d)", h=2)
                for m in range(PAIRS):
                    mm = pe.transpose(ps_t[:, m], flat[:, m], k.ident[:])
                mm.then_inc(ot_made, 1)

            def out_project(i, t, v):
                pe.wait_ge(ot_ready, t + 1)
                for m in range(PAIRS):
                    mm = pe.matmul(ps_o[:, 0, 0:P], ot[:, v, m], k.l1_wo[:, m], start=(m == 0), stop=(m == PAIRS - 1))
                mm.then_inc(y_made, 1)

            def step(i, u):
                for stage, behind in ((project(0), 1), (o_transpose, 3), (scores, 2), (project(1), 1),
                                      (qk_transpose(0), 1), (out_project, 3), (x_transpose, 0), (p_transpose, 2),
                                      (project_v, 1), (qk_transpose(1), 1), (values, 2)):
                    if has(i - behind, NT):
                        stage(i, i - behind, (u - behind) % 2)

            pipeline(pe, NT, step, 3, 2, 6)

        @block.scalar
        def _(act):
            act.wait_ge(setup, 1)

            def x_copy(t, v):
                act.wait_ge(xt_made, t + 1)
                if late(t, 2):
                    act.wait_ge(v_made, t - 1)
                act.copy(xt[:, v], ps_o[:, 1, 0:P]).then_inc(xt_ready, 1)

            def q_copy(t, v):
                act.wait_ge(qk_t_made[0], t + 1)
                if late(t, 2):
                    act.wait_ge(s_made, t - 1)
                act.copy(qt[:, v], ps_t[:]).then_inc(qk_t_ready[0], 1)

            def k_copy(t, v):
                act.wait_ge(qk_t_made[1], t + 1)
                act.copy(kbd[0:SEQ, v, :, 0], ps_t[0:SEQ])
                act.copy(kbd[SEQ:P, v, :, 1], ps_t[SEQ:P]).then_inc(qk_t_ready[1], 1)

            def v_copy(t, v):
                act.wait_ge(v_made, t + 1)
                if late(t, 2):
                    act.wait_ge(o_made, t - 1)
                for half in range(2):
                    rows = slice(half * SEQ, (half + 1) * SEQ)
                    op = act.copy(vbd[rows, v, :, :, half], ps_p[rows].rearrange("p b (n d) -> p b n d", d=D1))
                op.then_inc(v_ready, 1)

            def exponential(t, v):
                act.wait_ge(s_taken, t + 1)
                act.activation(sd[:, v], sd[:, v], ACT.Exp, scale=scale).then_inc(p_ready, 1)

            def p_copy(t, v):
                act.wait_ge(pt_made, t + 1)
                if late(t, 2):
                    act.wait_ge(o_made, t - 1)
                act.copy(pt[:, v], ps_t[:]).then_inc(pt_ready, 1)

            def o_copy(t, v):
                act.wait_ge(ot_made, t + 1)
                if late(t, 2):
                    act.wait_ge(y_made, t - 1)
                act.copy(ot[:, v], ps_t[:]).then_inc(ot_ready, 1)

            def step(i, u):
                for stage, behind in ((o_copy, 3), (exponential, 2), (q_copy, 1), (x_copy, 0), (p_copy, 2),
                                      (v_copy, 1), (k_copy, 1)):
                    if has(i - behind, NT):
                        stage(i - behind, (u - behind) % 2)

            pipeline(act, NT, step, 3, 2, 6)

        @block.vector
        def _(dve):
            def normalise(t, v):
                if late(t, 2):
                    dve.wait_ge(xt_made, t - 1)
                dve.tensor_scalar(xn[:, v], k.x_res[:, t], k.ln_scale[:, bass.ds(t, 1)], k.ln_shift[:, bass.ds(t, 1)],
                                  ALU.mult, ALU.add).then_inc(xn_ready, 1)

            def rotate(n):
                def stage(t, v):
                    dve.wait_ge(qk_made[n], t + 1)
                    if late(t, 1):
                        dve.wait_ge(qk_t_made[n], t)
                    src = ps_p[:].rearrange("p b (h s d) -> p (b h) s d", s=2, d=HALF)
                    dve.tensor_tensor(rot[n][:].rearrange("p h s d -> p (h s) d"), src.rearrange("p h s d -> p (h s) d"),
                                      bc(k.cos[:], 1, 2 * H1), ALU.mult)
                    dve.tensor_tensor(cross[n][:, :, 0], src[:, :, 1], bc(k.neg_sin[:], 1, H1), ALU.mult)
                    dve.tensor_tensor(cross[n][:, :, 1], src[:, :, 0], bc(k.sin[:], 1, H1), ALU.mult)\
                        .then_inc(crossed[n], 1)
                return stage

            def subtract_max(t, v):
                dve.wait_ge(s_made, t + 1)
                if late(t, 2):
                    dve.wait_ge(pt_made, t - 1)
                    dve.wait_ge(total_ready, t - 1)
                dve.tensor_reduce(mx[:, v], ps_s[:], AX.X, ALU.max).then_inc(mx_ready, 1)
                dve.wait_ge(mx_ready, t + 1)
                dve.tensor_tensor(sd[:, v], ps_s[:], mx[:, v].unsqueeze(2).to_broadcast([P, H1, SEQ]),
                                  ALU.subtract).then_inc(s_taken, 1)

            def add_up(t, v):
                dve.wait_ge(p_ready, t + 1)
                if late(t, 2):
                    dve.wait_ge(rec_ready, t - 1)
                dve.tensor_reduce(total[:, v], sd[:, v], AX.X, ALU.add).then_inc(total_ready, 1)
                dve.wait_ge(total_ready, t + 1)
                if late(t, 2):
                    dve.wait_ge(o_ready, t - 1)
                dve.reciprocal(rec[:, v], total[:, v]).then_inc(rec_ready, 1)

            def divide(t, v):
                dve.wait_ge(o_made, t + 1)
                dve.wait_ge(rec_ready, t + 1)
                if late(t, 2):
                    dve.wait_ge(ot_made, t - 1)
                dve.tensor_tensor(o_sb[:, v], ps_o[:].rearrange("p b (h d) -> p (b h) d", d=D1),
                                  rec[:, v].unsqueeze(2).to_broadcast([P, H1, D1]), ALU.mult).then_inc(o_ready, 1)

            def residual(t, v):
                dve.wait_ge(xb_ready, t + 1)
                dve.wait_ge(y_made, t + 1)
                if late(t, 2):
                    dve.wait_ge(mv_kept, t - 1)
                dve.tensor_tensor(row[:, v], ps_o[:, 0, 0:P], xb[:, v], ALU.add).then_inc(x_added, 1)
                dve.wait_ge(x_added, t + 1)
                keep_with_stats(dve, row[:, v], k.x_res[:, t], st[:, v], mv[:, v], k.mean_var[:, t], t,
                                st_ready, mv_ready, mv_kept)

            def step(i, u):
                for stage, behind in ((rotate(0), 1), (normalise, 0), (subtract_max, 2), (rotate(1), 1),
                                      (add_up, 2), (residual, 3), (divide, 2)):
                    if has(i - behind, NT):
                        stage(i - behind, (u - behind) % 2)

            pipeline(dve, NT, step, 3, 2, 6)


def context_scores(nc, k):
    NT = k.tiles
    with ExitStack() as c:
        def sb(n, shape, dt=F32):
            return c.enter_context(nc.sbuf_tensor(f"cs_{n}", shape, dt))

        new_sem = c.enter_context(stage_semaphores(nc))

        def sem(n):
            return new_sem(f"cs_{n}")

        xn = sb("xn", [P, 4, P])
        cs = sb("cs", [P, 4, P])
        ctx_t = sb("ctx_t", [P, 4, P])
        prod = sb("prod", [P, 4, P])
        own = sb("own", [P, 4])
        mx = sb("mx", [P, 4])
        neg_mx = sb("neg_mx", [P, 4])
        e = sb("e", [P, 4, P])
        total = sb("total", [P, 4])
        rec = sb("rec", [P, 4])
        att = sb("att", [P, 4, P])
        ps_x = [c.enter_context(nc.psum_tensor(f"cs_x{n}", [P, 512], F32)) for n in range(2)]
        ps_s = [c.enter_context(nc.psum_tensor(f"cs_s{n}", [P, 512], F32)) for n in range(4)]
        ps_a = [c.enter_context(nc.psum_tensor(f"cs_a{n}", [P, 512], F32)) for n in range(2)]
        ctx_loaded = [sem(f"ctx_loaded{n}") for n in range(4)]
        xn_ready, own_ready, xt_made, cs_ready, s_made = (sem(n) for n in ("xn_ready", "own_ready", "xt_made", "cs_ready", "s_made"))
        mx_ready, e_ready, rec_ready, att_ready = (sem(n) for n in ("mx_ready", "e_ready", "rec_ready", "att_ready"))
        at_made, at_ready, max_kept = sem("at_made"), sem("at_ready"), sem("max_kept")
        nc.scalar.preload_act_table(ACT.Exp)
        block = c.enter_context(nc.Block())

        @block.sync
        def _(sp):
            def step(t, u):
                if late(t, 4):
                    sp.wait_ge(s_made, t - 3)
                sp.dma_start(ctx_t[:, u], k.in_ctx_t[t]).then_inc(ctx_loaded[u], 16)

            pipeline(sp, NT, step, 0)

        @block.tensor
        def _(pe):
            def step(i, u):
                if has(i, NT):
                    pe.wait_ge(xn_ready, i + 1)
                    if late(i, 2):
                        pe.wait_ge(cs_ready, i - 1)
                    pe.transpose(ps_x[u % 2][:, 0:P], xn[:, u], k.ident[:]).then_inc(xt_made, 1)
                t, v = i - 1, (u - 1) % 4
                if has(t, NT):
                    pe.wait_ge(cs_ready, t + 1)
                    pe.wait_ge(ctx_loaded[v], 16 + 4 * (t - v))
                    if late(t, 4):
                        pe.wait_ge(e_ready, t - 3)
                    pe.matmul(ps_s[v][:, 0:P], k.ident_bf[:], k.other_seq[:], start=True, stop=True)
                    pe.matmul(ps_s[v][:, 0:P], cs[:, v], ctx_t[:, v], start=False, stop=True,
                              skip_group_check=True).then_inc(s_made, 1)
                t, v = i - 3, (u - 3) % 4
                if has(t, NT):
                    pe.wait_ge(att_ready, t + 1)
                    if late(t, 2):
                        pe.wait_ge(at_ready, t - 1)
                    pe.transpose(ps_a[v % 2][:, 0:P], att[:, v], k.ident[:]).then_inc(at_made, 1)

            pipeline(pe, NT, step, 3)

        @block.scalar
        def _(act):
            def step(i, u):
                if has(i, NT):
                    act.wait_ge(xt_made, i + 1)
                    if late(i, 4):
                        act.wait_ge(s_made, i - 3)
                    act.activation(cs[:, u], ps_x[u % 2][:, 0:P], ACT.Identity, scale=k.l1_wcq[:], bias=k.l1_wq_col[:])\
                        .then_inc(cs_ready, 1)
                t, v = i - 3, (u - 3) % 4
                if has(t, NT):
                    act.wait_ge(at_made, t + 1)
                    act.copy(k.at_all[:, t], ps_a[v % 2][:, 0:P]).then_inc(at_ready, 1)
                t, v = i - 2, (u - 2) % 4
                if has(t, NT):
                    act.wait_ge(mx_ready, t + 1)
                    if late(t, 4):
                        act.wait_ge(att_ready, t - 3)
                    act.activation(e[:, v], ps_s[v][:, 0:P], ACT.Exp, bias=neg_mx[:, v:v + 1],
                                   accum_out=total[:, v:v + 1]).then_inc(e_ready, 1)

            pipeline(act, NT, step, 3)

        @block.vector
        def _(dve):
            def step(i, u):
                if has(i, NT):
                    if late(i, 4):
                        dve.wait_ge(xt_made, i - 3)
                        dve.wait_ge(max_kept, i - 3)
                    dve.tensor_scalar(xn[:, u], k.x_res[:, i], k.ln_scale[:, bass.ds(i, 1)], k.ln_shift[:, bass.ds(i, 1)],
                                      ALU.mult, ALU.add).then_inc(xn_ready, 1)
                    dve.wait_ge(xn_ready, i + 1)
                    dve.tensor_tensor_reduce(prod[:, u], xn[:, u], k.l1_wc[:], 1.0, 0.0, ALU.mult, ALU.add,
                                             own[:, u:u + 1]).then_inc(own_ready, 1)
                t, v = i - 2, (u - 2) % 4
                if has(t, NT):
                    dve.wait_ge(s_made, t + 1)
                    dve.tensor_reduce(mx[:, v:v + 1], ps_s[v][:, 0:P], AX.X, ALU.max)
                    dve.tensor_reduce(neg_mx[:, v:v + 1], ps_s[v][:, 0:P], AX.X, ALU.max, negate=True)\
                        .then_inc(mx_ready, 1)
                    dve.wait_ge(mx_ready, t + 1)
                    dve.wait_ge(own_ready, t + 1)
                    dve.scalar_tensor_tensor(out=k.row_max[:, bass.ds(t, 1)], in0=mx[:, v:v + 1], scalar=k.l1_b3[:],
                                             in1=own[:, v:v + 1], op0=ALU.add, op1=ALU.add).then_inc(max_kept, 1)
                t, v = i - 3, (u - 3) % 4
                if has(t, NT):
                    dve.wait_ge(e_ready, t + 1)
                    if late(t, 4):
                        dve.wait_ge(at_made, t - 3)
                    dve.reciprocal(rec[:, v:v + 1], total[:, v:v + 1]).then_inc(rec_ready, 1)
                    dve.wait_ge(rec_ready, t + 1)
                    dve.tensor_scalar(att[:, v], e[:, v], rec[:, v:v + 1], None, ALU.mult).then_inc(att_ready, 1)

            pipeline(dve, NT, step, 3)


def token_weights(nc, k):
    NT = k.tiles
    with ExitStack() as c:
        def sb(n, shape):
            return c.enter_context(nc.sbuf_tensor(f"tw_{n}", shape, F32))

        new_sem = c.enter_context(stage_semaphores(nc))

        def sem(n):
            return new_sem(f"tw_{n}")

        e = sb("e", [NT, 2, SEQ])
        mx = sb("mx", [NT, 2])
        rec = sb("rec", [NT, 2])
        ps_m = c.enter_context(nc.psum_tensor("tw_m", [P, 512], F32))
        ps_w = c.enter_context(nc.psum_tensor("tw_w", [P, 512], F32))
        m_made, sub_ready, e_ready, w_ready, w_made, op_done = (sem(n) for n in ("m_made", "sub_ready", "e_ready", "w_ready",
                                                                              "w_made", "op_done"))
        block = c.enter_context(nc.Block())

        @block.tensor
        def _(pe):
            pe.transpose(ps_m[0:NT, 0:P], k.row_max[:], k.ident[:]).then_inc(m_made, 1)
            pe.wait_ge(w_ready, 1)
            pe.transpose(ps_w[:, 0:NT], e[:].rearrange("n b s -> n (b s)"), k.ident[0:NT, 0:NT]).then_inc(w_made, 1)

        @block.scalar
        def _(act):
            act.wait_ge(sub_ready, 1)
            act.activation(e[:], e[:], ACT.Exp).then_inc(e_ready, 1)

        @block.vector
        def _(dve):
            rows = ps_m[0:NT, 0:P].rearrange("n (b s) -> n b s", b=2)
            dve.wait_ge(m_made, 1)
            dve.tensor_reduce(mx[:], rows, AX.X, ALU.max).then_inc(op_done, 1)
            dve.wait_ge(op_done, 1)
            dve.tensor_tensor(e[:], rows, mx[:].unsqueeze(2).to_broadcast([NT, 2, SEQ]), ALU.subtract)\
                .then_inc(sub_ready, 1)
            dve.wait_ge(e_ready, 1)
            dve.tensor_reduce(mx[:], e[:], AX.X, ALU.add).then_inc(op_done, 1)
            dve.wait_ge(op_done, 2)
            dve.reciprocal(rec[:], mx[:]).then_inc(op_done, 1)
            dve.wait_ge(op_done, 3)
            dve.tensor_tensor(e[:], e[:], rec[:].unsqueeze(2).to_broadcast([NT, 2, SEQ]), ALU.mult).then_inc(w_ready, 1)
            dve.wait_ge(w_made, 1)
            dve.tensor_copy(k.token_w[:], ps_w[:, 0:NT])


def context_mix(nc, k):
    NT = k.tiles
    with ExitStack() as c:
        def sb(n, shape, dt=F32):
            return c.enter_context(nc.sbuf_tensor(f"cm_{n}", shape, dt))

        new_sem = c.enter_context(stage_semaphores(nc))

        def sem(n):
            return new_sem(f"cm_{n}")

        ctx = sb("ctx", [P, 4, P])
        xn = sb("xn", [P, 4, P])
        wb = sb("wb", [P, 4, P])
        feat = sb("feat", [P, 4, 4, P])
        xb = sb("xb", [P, 4, P])
        row = sb("row", [P, 4, P])
        st = sb("st", [P, 4, 6])
        mv = sb("mv", [P, 4, 2])
        ps_x = [c.enter_context(nc.psum_tensor(f"cm_x{n}", [P, 512], F32)) for n in range(2)]
        ps_c = [c.enter_context(nc.psum_tensor(f"cm_c{n}", [P, 512], F32)) for n in range(2)]
        ps_q = [c.enter_context(nc.psum_tensor(f"cm_q{n}", [P, 512], F32)) for n in range(2)]
        ps_z = [c.enter_context(nc.psum_tensor(f"cm_z{n}", [P, 512], F32)) for n in range(2)]
        ctx_loaded = [sem(f"ctx_loaded{n}") for n in range(4)]
        xn_ready, wb_ready, xt_made, c_ready = (sem(n) for n in ("xn_ready", "wb_ready", "xt_made", "c_ready"))
        c2q_made, c2q_ready, q2c_made, feat_ready = (sem(n) for n in ("c2q_made", "c2q_ready", "q2c_made", "feat_ready"))
        z_made, xb_ready, x_added = (sem(n) for n in ("z_made", "xb_ready", "x_added"))
        st_ready, mv_ready, mv_kept = (sem(n) for n in ("st_ready", "mv_ready", "mv_kept"))
        block = c.enter_context(nc.Block())

        @block.sync
        def _(sp):
            def step(t, u):
                if late(t, 4):
                    sp.wait_ge(c2q_made, t - 3)
                sp.dma_start(ctx[:, u], k.in_ctx[t]).then_inc(ctx_loaded[u], 16)

            pipeline(sp, NT, step, 0)

        @block.gpsimd
        def _(pool):
            def step(t, u):
                if late(t, 4):
                    pool.wait_ge(q2c_made, t - 3)
                pool.tensor_tensor(wb[:, u], k.same_seq[:], k.token_w[:, bass.ds(t, 1)].to_broadcast([P, P]), ALU.mult)\
                    .then_inc(wb_ready, 1)
                if late(t, 4):
                    pool.wait_ge(x_added, t - 3)
                pool.tensor_tensor(xb[:, u], k.x_res[:, t], k.l1_bl[:], ALU.add).then_inc(xb_ready, 1)

            pipeline(pool, NT, step, 0)

        @block.tensor
        def _(pe):
            def step(i, u):
                if has(i, NT):
                    pe.wait_ge(xn_ready, i + 1)
                    if late(i, 2):
                        pe.wait_ge(c_ready, i - 1)
                    pe.transpose(ps_x[u % 2][:, 0:P], xn[:, u], k.ident[:]).then_inc(xt_made, 1)
                    pe.wait_ge(ctx_loaded[u], 16 + 4 * (i - u))
                    if late(i, 2):
                        pe.wait_ge(feat_ready, i - 1)
                    pe.matmul(ps_c[u % 2][:, 0:P], ctx[:, u], k.at_all[:, i], start=True, stop=True).then_inc(c2q_made, 1)
                    pe.wait_ge(wb_ready, i + 1)
                    pe.matmul(ps_q[u % 2][:, 0:P], xn[:, u], wb[:, u], start=True, stop=True).then_inc(q2c_made, 1)
                t, v = i - 2, (u - 2) % 4
                if has(t, NT):
                    pe.wait_ge(feat_ready, t + 1)
                    if late(t, 2):
                        pe.wait_ge(x_added, t - 1)
                    for n in range(4):
                        mm = pe.matmul(ps_z[v % 2][:, 0:P], feat[:, v, n], k.l1_wl[:, n], start=(n == 0), stop=(n == 3))
                    mm.then_inc(z_made, 1)

            pipeline(pe, NT, step, 2)

        @block.scalar
        def _(act):
            def step(t, u):
                act.wait_ge(xt_made, t + 1)
                if late(t, 4):
                    act.wait_ge(z_made, t - 3)
                act.copy(feat[:, u, 0], ps_x[u % 2][:, 0:P]).then_inc(c_ready, 1)
                act.wait_ge(c2q_made, t + 1)
                act.copy(feat[:, u, 1], ps_c[u % 2][:, 0:P]).then_inc(c2q_ready, 1)

            pipeline(act, NT, step, 0)

        @block.vector
        def _(dve):
            def step(i, u):
                if has(i, NT):
                    if late(i, 4):
                        dve.wait_ge(q2c_made, i - 3)
                    dve.tensor_scalar(xn[:, u], k.x_res[:, i], k.ln_scale[:, bass.ds(i, 1)], k.ln_shift[:, bass.ds(i, 1)],
                                      ALU.mult, ALU.add).then_inc(xn_ready, 1)
                t, v = i - 1, (u - 1) % 4
                if has(t, NT):
                    dve.wait_ge(c2q_ready, t + 1)
                    dve.wait_ge(q2c_made, t + 1)
                    dve.tensor_tensor(feat[:, v, 2], feat[:, v, 1], feat[:, v, 0], ALU.mult)
                    dve.tensor_tensor(feat[:, v, 3], ps_q[v % 2][:, 0:P], feat[:, v, 0], ALU.mult).then_inc(feat_ready, 1)
                t, v = i - 3, (u - 3) % 4
                if has(t, NT):
                    dve.wait_ge(xb_ready, t + 1)
                    dve.wait_ge(z_made, t + 1)
                    if late(t, 4):
                        dve.wait_ge(mv_kept, t - 3)
                    dve.tensor_tensor(row[:, v], ps_z[v % 2][:, 0:P], xb[:, v], ALU.add).then_inc(x_added, 1)
                    dve.wait_ge(x_added, t + 1)
                    keep_with_stats(dve, row[:, v], k.x_res[:, t], st[:, v], mv[:, v], k.mean_var[:, t], t,
                                    st_ready, mv_ready, mv_kept)

            pipeline(dve, NT, step, 3)


def one_expert_ffn(nc, k, out_rows):
    NT = k.tiles
    NS = NT + NE - 1
    FF = 4
    with ExitStack() as c:
        def sb(n, shape, dt=F32):
            return c.enter_context(nc.sbuf_tensor(f"m1_{n}", shape, dt))

        new_sem = c.enter_context(stage_semaphores(nc))

        def sem(n):
            return new_sem(f"m1_{n}")

        WIDTH = k.l1_ffn.shape[2]
        from_row = sb("from_row", [P, 4, 1], U32)
        no_shift = sb("no_shift", [P, 1], U32)
        to_row = sb("to_row", [P, 4, 1], U32)
        xg = sb("xg", [P, 4, 2 * P])
        wt = sb("wt", [P, 2, WIDTH])
        xt = sb("xt", [P, 2, P])
        hid = sb("hid", [P, 2, FF, P])
        xb = sb("xb", [P, 4, P])
        y = sb("y", [P, 4, P])
        w1, b1 = wt[:, :, 0:FF * P], wt[:, :, FF * P:FF * P + FF]
        w2 = wt[:, :, FF * P + FF:2 * FF * P + FF].rearrange("p b (f c) -> p b f c", c=P)
        b2 = wt[:, :, 2 * FF * P + FF:WIDTH]
        ps_x = [c.enter_context(nc.psum_tensor(f"m1_x{n}", [P, 512], F32)) for n in range(2)]
        ps_h = [c.enter_context(nc.psum_tensor(f"m1_h{n}", [P, FF, P], F32)) for n in range(2)]
        ps_y = [c.enter_context(nc.psum_tensor(f"m1_y{n}", [P, 512], F32)) for n in range(2)]
        gathered, scattered = k.gathered1, k.scattered1
        setup = sem("setup")
        from_ready, to_ready, wt_ready, xt_made, xt_ready = (sem(n) for n in ("from_ready", "to_ready", "wt_ready", "xt_made", "xt_ready"))
        h_made, hid_ready, y_made, xb_ready, y_ready = (sem(n) for n in ("h_made", "hid_ready", "y_made", "xb_ready",
                                                                          "y_ready"))
        nc.scalar.preload_act_table(ACT.Gelu)
        block = c.enter_context(nc.Block())

        @block.gpsimd
        def _(pool):
            def copy_idx(t, v, of_all, to):
                column = of_all[:, bass.ds(t, 1)] if not isinstance(t, int) else of_all[:, t:t + 1]
                return pool.tensor_tensor(to[:, v], column, no_shift[:], ALU.add)

            pool.memset(no_shift[:], 0).then_inc(setup, 1)
            pool.wait_ge(setup, 1)
            copy_idx(0, 0, k.gather_idx, from_row).then_inc(from_ready, 1)

            def step(i, u):
                g, gv = i + 1, (u + 1) % 4
                s, sv = i - 3, (u - 3) % 4
                if has(i, NS):
                    pool.wait_ge(from_ready, i + 1)
                if has(i - 4, NS):
                    pool.wait_ge(y_ready, i - 3)
                    pool.wait_ge(to_ready, i - 3)
                if has(g, NS):
                    if late(g, 4):
                        pool.wait_ge(xb_ready, g - 3)
                    copy_idx(g, gv, k.gather_idx, from_row).then_inc(from_ready, 1)
                if has(s, NS):
                    if late(s, 4):
                        pool.wait_ge(scattered[sv], 4 * (s - sv))
                    copy_idx(s, sv, k.scatter_idx, to_row).then_inc(to_ready, 1)
                if has(i, NS):
                    pool.indirect_dma_start(xg[:, u], None, k.xx_rows,
                                            bass.IndirectOffsetOnAxis(ap=from_row[:, u], axis=0)).then_inc(gathered[u], 16)
                if has(i - 4, NS):
                    pool.indirect_dma_start(out_rows, bass.IndirectOffsetOnAxis(ap=to_row[:, u], axis=0),
                                            y[:, u], None, bounds_check=NT * P - 1, oob_is_err=False)\
                        .then_inc(scattered[u], 16)

            pipeline(pool, NS, step, 4)
            for n in range(4):
                pool.wait_ge(scattered[n], 16 * len(range(n, NS, 4)))

        @block.tensor
        def _(pe):
            def step(i, u):
                t, v = i - 1, (u - 1) % 4
                if has(t, NS):
                    pe.wait_ge(gathered[v], 16 + 4 * (t - v))
                    if late(t, 2):
                        pe.wait_ge(xt_ready, t - 1)
                    pe.transpose(ps_x[v % 2][:, 0:P], xg[:, v, P:2 * P], k.ident[:]).then_inc(xt_made, 1)
                t, v = i - 3, (u - 3) % 4
                if has(t, NS):
                    pe.wait_ge(hid_ready, t + 1)
                    if late(t, 2):
                        pe.wait_ge(y_ready, t - 1)
                    for f in range(FF):
                        mm = pe.matmul(ps_y[v % 2][:, 0:P], hid[:, v % 2, f], w2[:, v % 2, f], start=(f == 0), stop=(f == FF - 1))
                    mm.then_inc(y_made, 1)
                t, v = i - 2, (u - 2) % 4
                if has(t, NS):
                    pe.wait_ge(xt_ready, t + 1)
                    pe.wait_ge(wt_ready, t + 1)
                    if late(t, 2):
                        pe.wait_ge(hid_ready, t - 1)
                    for f in range(FF):
                        mm = pe.matmul(ps_h[v % 2][:, f], w1[:, v % 2, f * P:(f + 1) * P], xt[:, v % 2], start=True, stop=True)
                    mm.then_inc(h_made, 1)

            pipeline(pe, NS, step, 3)

        @block.scalar
        def _(act):
            def step(i, u):
                t, v = i - 1, (u - 1) % 4
                if has(t, NS):
                    act.wait_ge(xt_made, t + 1)
                    if late(t, 2):
                        act.wait_ge(h_made, t - 1)
                    act.copy(xt[:, v % 2], ps_x[v % 2][:, 0:P]).then_inc(xt_ready, 1)
                t, v = i - 2, (u - 2) % 4
                if has(t, NS):
                    act.wait_ge(h_made, t + 1)
                    if late(t, 2):
                        act.wait_ge(y_made, t - 1)
                    for f in range(FF):
                        op = act.activation(hid[:, v % 2, f], ps_h[v % 2][:, f], ACT.Gelu, bias=b1[:, v % 2, f:f + 1])
                    op.then_inc(hid_ready, 1)

            pipeline(act, NS, step, 2)

        @block.vector
        def _(dve):
            def step(i, u):
                t, v = i - 3, (u - 3) % 4
                if has(t, NS):
                    dve.wait_ge(xb_ready, t + 1)
                    if late(t, 4):
                        dve.wait_ge(scattered[v], 4 * (t - v))
                    dve.wait_ge(y_made, t + 1)
                    dve.tensor_tensor(y[:, v], ps_y[v % 2][:, 0:P], xb[:, v], ALU.add).then_inc(y_ready, 1)
                t, v = i - 1, (u - 1) % 4
                if has(t, NS):
                    if late(t, 2):
                        dve.wait_ge(y_ready, t - 1)
                        dve.wait_ge(hid_ready, t - 1)
                        dve.wait_ge(y_made, t - 1)
                    expert = dve.value_load(k.tile_expert[0:1, bass.ds(t, 1)], min_val=0, max_val=NE - 1)
                    dve.tensor_scalar(wt[:, v % 2], k.l1_ffn[:, expert], 1.0, None, ALU.mult).then_inc(wt_ready, 1)
                    dve.wait_ge(wt_ready, t + 1)
                    dve.wait_ge(gathered[v], 16 + 4 * (t - v))
                    dve.tensor_tensor(xb[:, v], xg[:, v, 0:P], b2[:, v % 2], ALU.add).then_inc(xb_ready, 1)

            pipeline(dve, NS, step, 3)


def load(nc, k, name):
    with ExitStack() as c:
        loaded = c.enter_context(stage_semaphores(nc))(f"{name}_loaded")
        block = c.enter_context(nc.Block())

        @block.sync
        def _(sp):
            for tile, src in k.loads:
                sp.dma_start(tile, src).then_inc(loaded, 16)
            sp.wait_ge(loaded, 16 * len(k.loads))
    k.loads = []


def route_constants(nc, k, a, rm, slots):
    NT = k.tiles
    k.logits = rm("logits", [P, NT, NE])
    k.iota_e = rm("iota_e", [P, NE], src=a["iota"][:, 0:NE].to_broadcast([P, NE]))
    k.iota_cap = rm("iota_cap", [P, NE], src=a["iota_cap"].to_broadcast([P, NE]))
    k.iota_s = rm("iota_s", [P, P], src=a["iota"][:, 0:P].to_broadcast([P, P]))
    k.iota_s1 = rm("iota_s1", [P, NT], src=a["iota"][:, 1:NT + 1].to_broadcast([P, NT]))
    k.iota_p = k.iota_s
    k.place = rm("place", [P, 1], src=a["place"])
    k.empty_id = rm("empty_id", [P, slots], src=a["empty_id"][:, 0:slots])
    k.before = rm("before", [P, P], BF16, src=a["before"])
    k.ones_bf = rm("ones_bf", [P, P], BF16, src=a["ones_bf"])
    k.gather_idx = rm("gather_idx", [P, slots], U32)
    k.scatter_idx = rm("scatter_idx", [P, slots], U32)


def build(nc, a):
    NT = a["x"].shape[0]
    k = Kept(NT)
    with ExitStack() as outer:
        k.loads = []
        new_sem = outer.enter_context(stage_semaphores(nc))
        k.gathered0 = [new_sem(f"gathered0_{n}") for n in range(NE * CAP // P)]
        k.added0 = [new_sem(f"added0_{e}") for e in range(NE)]
        k.gathered1 = [new_sem(f"gathered1_{n}") for n in range(4)]
        k.scattered1 = [new_sem(f"scattered1_{n}") for n in range(4)]

        def res(n, shape, dt=F32, src=None, stack=outer):
            t = stack.enter_context(nc.sbuf_tensor(n, shape, dt))
            if src is not None:
                k.loads.append((t[:], src))
            return t

        def rows(n):
            return a[n].to_broadcast([P, a[n].shape[1]])

        k.in_x, k.in_mask, k.in_ctx_t, k.in_dist, k.in_dd = a["x"], a["mask"], a["ctx_t"], a["dist"], a["dd"]
        k.x_dram, k.xn_dram = a["x_dram"], a["xn_dram"]
        k.in_ctx, k.xx_dram = a["ctx"], a["xx_dram"]
        k.xx_rows = k.xx_dram.rearrange("n p c -> (n p) c")
        k.x_rows = k.x_dram.rearrange("n p c -> (n p) c")
        k.xn_rows = k.xn_dram.rearrange("n p c -> (n p) c")
        k.x_res = res("x_res", [P, NT, P])
        k.mean_var = res("mean_var", [P, NT, 2])
        k.ln_scale = res("ln_scale", [P, NT])
        k.ln_shift = res("ln_shift", [P, NT])
        k.ident = res("ident", [P, P], src=a["ident"])
        k.ident_bf = res("ident_bf", [P, P], BF16, src=a["ident_bf"])
        k.causal = res("causal", [P, SEQ], BF16, src=a["causal"])
        with ExitStack() as layer0:
            def r0(n, shape, dt=F32, src=None):
                return res(n, shape, dt, src, layer0)
            k.head_mask = r0("head_mask", [P, GRP, 1], src=a["head_mask"])
            k.group_mask = r0("group_mask", [P, GRP, 1], src=a["group_mask"])
            k.a_wq, k.a_wk, k.a_wv, k.a_wo, k.x_wq, k.x_wk, k.x_wv, k.x_wo = (
                r0(n, [P, P], src=a[n]) for n in ("a_wq", "a_wk", "a_wv", "a_wo", "x_wq", "x_wk", "x_wv", "x_wo"))
            k.a_bq, k.a_bk, k.a_bv, k.x_bq, k.x_bk, k.x_ln_g, k.x_ln_b = (
                r0(n, [P, 1], src=a[n]) for n in ("a_bq", "a_bk", "a_bv", "x_bq", "x_bk", "x_ln_g", "x_ln_b"))
            k.a_bo = r0("a_bo_rows", [P, P], src=rows("a_bo"))
            k.x_bo = r0("x_bo_rows", [P, P], src=rows("x_bo"))
            k.x_bv_rows = r0("x_bv_rows", [P, P], src=rows("x_bv"))
            k.decay = r0("decay", [P, SEQ])
            k.mask_all = r0("mask_all", [P, NT, SEQ], BF16)
            set_up(nc, k)
            k.loads = []
            layer_norm_scales(nc, k, k.mean_var, k.ln_scale[:], k.ln_shift[:], "ln0")
            small_head_attention(nc, k, "sa", cross=False)
            with ExitStack() as cross:
                k.o_all = res("o_all", [P, NT, P], stack=cross)
                k.o_mean_var = res("o_mean_var", [P, NT, 2], stack=cross)
                k.o_scale = res("o_scale", [P, NT], stack=cross)
                k.o_shift = res("o_shift", [P, NT], stack=cross)
                layer_norm_scales(nc, k, k.mean_var, k.ln_scale[:], k.ln_shift[:], "ln1")
                small_head_attention(nc, k, "ca", cross=True)
                layer_norm_scales(nc, k, k.o_mean_var, k.o_scale[:], k.o_shift[:], "lno")
                project_cross(nc, k)
        with ExitStack() as moe0:
            layer_norm_scales(nc, k, k.mean_var, k.ln_scale[:], k.ln_shift[:], "ln2")

            def rm(n, shape, dt=F32, src=None):
                return res(f"moe0_{n}", shape, dt, src, moe0)

            route_constants(nc, k, a, rm, NE * CAP // P)
            rw = rm("f0_rw", [P, NE], src=a["f0_rw"])
            rb = rm("f0_rb", [P, NE], src=rows("f0_rb"))
            k.f0_w = rm("f0_w", [P, NE, 2 * P], src=a["f0_w"])
            k.f0_v = rm("f0_v", [P, NE, 2 * P], src=a["f0_v"])
            k.f0_out = rm("f0_out", [P, NE, 2, P], src=a["f0_out"])
            k.w_slot = rm("w_slot", [P, NE * CAP // P])
            load(nc, k, "ld2")
            router(nc, k, "r0", rw, rb, k.xn_dram, None)
            chosen_slots(nc, k, "c0", 2, NE * CAP // P, k.w_slot)
            two_expert_ffn(nc, k)
        with ExitStack() as wide:
            layer_norm_scales(nc, k, k.mean_var, k.ln_scale[:], k.ln_shift[:], "ln3")

            def rw1(n, shape, dt=F32, src=None):
                return res(n, shape, dt, src, wide)

            k.l1_wq = rw1("l1_wq", [P, H1 * D1], src=a["l1_wq"])
            k.l1_wk = rw1("l1_wk", [P, H1 * D1], src=a["l1_wk"])
            k.l1_wv = rw1("l1_wv", [P, 2, PAIRS * D1], src=a["l1_wv"])
            k.l1_wo = rw1("l1_wo", [P, PAIRS, P], src=a["l1_wo"])
            k.l1_bo = rw1("l1_bo", [P, P], src=rows("l1_bo"))
            k.cos = rw1("cos", [P, D1 // 2], src=a["cos"])
            k.sin = rw1("sin", [P, D1 // 2], src=a["sin"])
            k.neg_sin = rw1("neg_sin", [P, D1 // 2], src=a["neg_sin"])
            load(nc, k, "ld3")
            wide_head_attention(nc, k)
        with ExitStack() as context:
            layer_norm_scales(nc, k, k.mean_var, k.ln_scale[:], k.ln_shift[:], "ln4")

            def rc(n, shape, dt=F32, src=None):
                return res(n, shape, dt, src, context)

            k.l1_wcq = rc("l1_wcq", [P, 1], src=a["l1_wcq"])
            k.l1_wq_col = rc("l1_w_q", [P, 1], src=a["l1_w_q"])
            k.l1_wc = rc("l1_wc", [P, P], src=rows("l1_wc"))
            k.l1_b3 = rc("l1_b3", [P, 1])
            b3 = rc("l1_b3_parts", [P, 3])
            for n, part in enumerate(("l1_b_cq", "l1_b_c", "l1_b_q")):
                k.loads.append((b3[:, n:n + 1], rows(part)))
            k.l1_wl = rc("l1_wl", [P, 4, P], src=a["l1_wl"])
            k.l1_bl = rc("l1_bl", [P, P], src=rows("l1_bl"))
            k.same_seq = rc("same_seq", [P, P], src=a["same_seq"])
            k.other_seq = rc("other_seq", [P, P], BF16, src=a["other_seq"])
            k.at_all = rc("at_all", [P, NT, P])
            k.row_max = rc("row_max", [P, NT])
            k.token_w = rc("token_w", [P, NT])
            load(nc, k, "ld4")
            with nc.Block() as block:
                @block.vector
                def _(dve):
                    dve.tensor_reduce(k.l1_b3[:], b3[:], AX.X, ALU.add)
            context_scores(nc, k)
            token_weights(nc, k)
            context_mix(nc, k)
        with ExitStack() as moe1:
            layer_norm_scales(nc, k, k.mean_var, k.ln_scale[:], k.ln_shift[:], "ln5")

            def rm1(n, shape, dt=F32, src=None):
                return res(f"moe1_{n}", shape, dt, src, moe1)

            slots = NT + NE - 1
            FF = a["f1_w1"].shape[2]
            route_constants(nc, k, a, rm1, slots)
            rw = rm1("f1_rw", [P, NE], src=a["f1_rw"])
            rb = rm1("f1_rb", [P, NE], src=rows("f1_rb"))
            k.tile_expert = rm1("tile_expert", [P, slots], I32)
            k.l1_ffn = rm1("l1_ffn", [P, NE, 2 * FF + FF // P + P])
            at = 0
            for n in ("f1_w1", "f1_b1", "f1_w2", "f1_b2"):
                w = a[n].shape[-1]
                k.loads.append((k.l1_ffn[:, :, at:at + w], bc(a[n], 0, P) if n == "f1_b2" else a[n]))
                at += w
            load(nc, k, "ld5")
            router(nc, k, "r1", rw, rb, k.xx_dram[:, :, P:2 * P], k.xx_dram[:, :, 0:P])
            chosen_slots(nc, k, "c1", 1, slots, None)
            one_expert_ffn(nc, k, a["out"].rearrange("n p c -> (n p) c"))


def _layout(v):
    c, f, bf = np.ascontiguousarray, np.float32, mybir.dt.np(BF16)
    B = v["x"].shape[0]
    NT = B * SEQ // P
    i, s = np.arange(P), np.arange(SEQ)
    same = (i // SEQ)[:, None] == (i // SEQ)[None]
    o = {}
    o["dist"] = np.abs((i % SEQ)[:, None] - s[None]).astype(f)
    o["ident"] = np.eye(P, dtype=f)
    o["ident_bf"] = np.eye(P).astype(bf)
    o["causal"] = np.where(s[None] <= (i % SEQ)[:, None], 0, NEG).astype(bf)
    o["head_mask"] = ((i // D0) % GRP == np.arange(GRP)[:, None]).T.astype(f)[:, :, None]
    o["group_mask"] = (i // (GRP * D0) == np.arange(GRP)[:, None]).T.astype(f)[:, :, None]
    o["iota"] = np.arange(256, dtype=f).reshape(1, 256)
    o["iota_cap"] = (CAP * np.arange(NE) + 1).astype(f).reshape(1, NE)
    o["place"] = i.astype(f).reshape(P, 1)
    o["empty_id"] = (P + NT * P + i[:, None] + P * np.arange(NT + NE)[None]).astype(f)
    o["before"] = (i[:, None] < i[None]).astype(bf)
    o["ones_bf"] = np.ones((P, P), bf)
    o["same_seq"] = same.astype(f)
    o["other_seq"] = np.where(same, 0, NEG).astype(bf)
    freq = (f(1.0) / f(10000.0) ** (np.arange(0, D1, 2, dtype=f) / f(D1))).astype(f)
    angle = (i % SEQ).astype(f)[:, None] * freq[None]
    o["cos"], o["sin"] = np.cos(angle).astype(f), np.sin(angle).astype(f)
    o["neg_sin"] = -o["sin"]
    o["x"] = v["x"].reshape(NT, P, P)
    o["mask"] = v["mask_BxSxS2_ik1"].reshape(NT, P, SEQ)
    o["ctx"] = v["ctx_1024"].reshape(NT, P, P)
    o["ctx_t"] = o["ctx"].transpose(0, 2, 1)
    W, b = v["L0_attn_Wqkv_w"], v["L0_attn_Wqkv_b"]
    for n, q in enumerate("qkv"):
        o["a_w" + q], o["a_b" + q] = W[n * P:(n + 1) * P].T, b[n * P:(n + 1) * P].reshape(P, 1)
    o["dd"] = v["L0_attn_distance_decay"].reshape(1, 1)
    o["a_wo"], o["a_bo"] = v["L0_attn_out_w"].T, v["L0_attn_out_b"].reshape(1, P)

    def repeated(w):
        return np.repeat(w.reshape(H0 // GRP, 1, D0, -1), GRP, axis=1).reshape(P, -1)

    o["x_wq"], o["x_bq"] = v["L0_xattn_Wq"].T, v["L0_xattn_bq"].reshape(P, 1)
    o["x_wk"], o["x_bk"] = repeated(v["L0_xattn_Wk"]).T, repeated(v["L0_xattn_bk"])
    o["x_wv"], o["x_bv"] = repeated(v["L0_xattn_Wv"]).T, repeated(v["L0_xattn_bv"]).reshape(1, P)
    o["x_wo"], o["x_bo"] = v["L0_xattn_Wo"].T, v["L0_xattn_bo"].reshape(1, P)
    o["x_ln_g"], o["x_ln_b"] = v["L0_xattn_ln_g"].reshape(P, 1), v["L0_xattn_ln_b"].reshape(P, 1)
    o["f0_rw"], o["f0_rb"] = v["L0_ffn_router_w"].T, v["L0_ffn_router_b"].reshape(1, NE)
    o["f0_w"], o["f0_v"] = v["L0_ffn_W"].transpose(1, 0, 2), v["L0_ffn_V"].transpose(1, 0, 2)
    o["f0_out"] = v["L0_ffn_W_out"].reshape(NE, 2, P, P).transpose(2, 0, 1, 3)
    halves = np.concatenate([np.arange(0, D1, 2), np.arange(1, D1, 2)])
    for q in "qk":
        o["l1_w" + q] = v["L1_attn_W" + q].reshape(P, H1, D1)[:, :, halves].reshape(P, H1 * D1)
    o["l1_wv"] = v["L1_attn_Wv"].reshape(P, PAIRS, 2, D1).transpose(0, 2, 1, 3).reshape(P, 2, PAIRS * D1)
    o["l1_wo"] = v["L1_attn_Wo"].reshape(PAIRS, P, P).transpose(1, 0, 2)
    o["l1_bo"] = v["L1_attn_bo"].reshape(1, P)
    o["l1_wcq"], o["l1_w_q"] = v["L1_xattn_w_cq"].reshape(P, 1), v["L1_xattn_w_q"].reshape(P, 1)
    o["l1_wc"] = v["L1_xattn_w_c"].reshape(1, P)
    for n in ("b_cq", "b_c", "b_q"):
        o["l1_" + n] = v["L1_xattn_" + n].reshape(1, 1)
    o["l1_wl"] = v["L1_xattn_W_l"].T.reshape(4, P, P).transpose(1, 0, 2)
    o["l1_bl"] = v["L1_xattn_b_l"].reshape(1, P)
    o["f1_rw"], o["f1_rb"] = v["L1_ffn_wr"], v["L1_ffn_br"].reshape(1, NE)
    o["f1_w1"] = v["L1_ffn_w1"].transpose(1, 0, 2)
    o["f1_b1"] = v["L1_ffn_b1"].reshape(NE, -1, P).transpose(2, 0, 1)
    o["f1_w2"] = v["L1_ffn_w2"].reshape(NE, -1, P, P).transpose(2, 0, 1, 3).reshape(P, NE, -1)
    o["f1_b2"] = v["L1_ffn_b2"]
    return {n: c(x) for n, x in o.items()}


def kernel(**inputs):
    import numpy as _np
    import concourse.bacc as _bacc
    from concourse import mybir as _mybir
    from concourse.bass_utils import run_bass_kernel_spmd as _run

    nc = _bacc.Bacc("TRN2", target_bir_lowering=False, num_devices=1)
    tensors = _layout({n: _np.asarray(x) for n, x in inputs.items()})
    arrays, a = {}, {}
    for n, x in tensors.items():
        x = _np.ascontiguousarray(x)
        arrays[f"in_{n}_dram"] = x
        a[n] = nc.dram_tensor(f"in_{n}_dram", x.shape, _mybir.dt.from_np(x.dtype), kind="ExternalInput").ap()
    NT = a["x"].shape[0]
    a["out"] = nc.dram_tensor("out_0_dram", [NT, P, P], F32, kind="ExternalOutput").ap()
    a["x_dram"] = nc.dram_tensor("x_dram", [NT + NE * CAP // P, P, P], F32).ap()
    a["xn_dram"] = nc.dram_tensor("xn_dram", [NT, P, P], F32).ap()
    a["xx_dram"] = nc.dram_tensor("xx_dram", [NT, P, 2 * P], F32).ap()
    build(nc, a)
    r = _run(nc, [arrays], core_ids=[0])
    return r.results[0]["out_0_dram"].reshape(inputs["x"].shape)
```

```python
from contextlib import ExitStack, contextmanager

import numpy as np

import concourse.bass as bass
from concourse import mybir

F32 = mybir.dt.float32
BF16 = mybir.dt.bfloat16
I32 = mybir.dt.int32
U32 = mybir.dt.uint32
ALU = mybir.AluOpType
ACT = mybir.ActivationFunctionType
AX = mybir.AxisListType

P = 128
SEQ = 64
LN_EPS = 1e-5
NEG = -1e30

H0, D0 = 16, 8
GRP = 4
H1, D1 = 16, 64
NE = 8
CAP = 256
PAIRS = 8
UNROLL = 4
GROUP = 4
PEEL = 8


class Kept:

    def __init__(self, tiles):
        self.tiles = tiles


@contextmanager
def stage_semaphores(nc):
    made = []

    def new(name):
        made.append(nc.alloc_semaphore(name))
        return made[-1]

    yield new
    numbers = sorted(s.num for s in made)
    while numbers:
        n = next((n for n in range(1, len(numbers)) if numbers[n] != numbers[0] + n), len(numbers))
        nc.gpsimd.sem_clear(range(numbers[0], numbers[0] + n))
        numbers = numbers[n:]
    for s in made:
        nc.release_semaphore(s)


def pipeline(eng, tiles, step, lag, unroll=UNROLL, peel=PEEL):
    body = (tiles - peel) // unroll
    for i in range(peel):
        step(i, i % unroll)
    with eng.Fori(0, body) as j:
        for u in range(unroll):
            step(j * unroll + (peel + u), u)
    for i in range(peel + body * unroll, tiles + lag):
        step(i, i % unroll)


def late(t, n):
    return not isinstance(t, int) or t >= n


def has(t, tiles):
    return not isinstance(t, int) or 0 <= t < tiles


def bc(ap, axis, n):
    return ap.unsqueeze(axis).to_broadcast([*ap.shape[:axis], n, *ap.shape[axis:]])


def keep_with_stats(dve, row, kept, st, mv, kept_mv, t, st_ready, mv_ready, mv_kept):
    dve.bn_stats(st, row).then_inc(st_ready, 1)
    dve.wait_ge(st_ready, t + 1)
    dve.tensor_scalar(kept, row, 1.0, None, ALU.mult)
    dve.bn_aggr(mv, st).then_inc(mv_ready, 1)
    dve.wait_ge(mv_ready, t + 1)
    dve.tensor_scalar(kept_mv, mv, 1.0, None, ALU.mult).then_inc(mv_kept, 1)


def group_pipeline(eng, tiles, step, lag):
    pipeline(eng, tiles // GROUP, step, lag, 2, 6)


def group(g):
    return bass.ds(g * GROUP, GROUP)


def normalise_group(dve, k, g, to):
    for n in range(GROUP):
        t = g * GROUP + n
        op = dve.tensor_scalar(to[:, n], k.x_res[:, t], k.ln_scale[:, bass.ds(t, 1)], k.ln_shift[:, bass.ds(t, 1)],
                               ALU.mult, ALU.add)
    return op


class GroupStats:

    def __init__(self, dve, tiles, row, all_stats, st, mv, st_ready, mv_ready, mv_kept):
        self.dve, self.groups, self.row, self.all_stats, self.st, self.mv = dve, tiles // GROUP, row, all_stats, st, mv
        self.st_ready, self.mv_ready, self.mv_kept = st_ready, mv_ready, mv_kept

    def by_row(self, g, v):
        for n in range(GROUP):
            op = self.dve.bn_stats(self.st[:, v, n], self.row[:, v, n])
        op.then_inc(self.st_ready, 1)

    def keep_and_aggregate(self, made, v):
        kept = made - 1
        if has(made, self.groups):
            self.dve.wait_ge(self.st_ready, made + 1)
            if late(made, 2):
                self.dve.wait_ge(self.mv_kept, made - 1)
        if has(kept, self.groups):
            self.dve.wait_ge(self.mv_ready, kept + 1)
            self.dve.tensor_scalar(self.all_stats[:, group(kept)], self.mv[:, 1 - v], 1.0, None, ALU.mult)\
                .then_inc(self.mv_kept, 1)
        if has(made, self.groups):
            for n in range(GROUP):
                op = self.dve.bn_aggr(self.mv[:, v, n], self.st[:, v, n])
            op.then_inc(self.mv_ready, 1)


def layer_norm_scales(nc, k, mean_var, scale, shift, name):
    with ExitStack() as c:
        tiles = mean_var.shape[1]
        ve = c.enter_context(nc.sbuf_tensor(f"{name}_ve", [P, tiles], F32))
        root = c.enter_context(nc.sbuf_tensor(f"{name}_root", [P, tiles], F32))
        guess = c.enter_context(nc.sbuf_tensor(f"{name}_guess", [P, tiles], F32))
        corr = c.enter_context(nc.sbuf_tensor(f"{name}_corr", [P, tiles], F32))
        new_sem = c.enter_context(stage_semaphores(nc))
        var_done, root_done, newton = (new_sem(f"{name}_{n}") for n in ("var_done", "root_done", "newton"))
        block = c.enter_context(nc.Block())

        @block.vector
        def _(dve):
            dve.tensor_scalar(ve[:], mean_var[:, :, 1], LN_EPS, None, ALU.add).then_inc(var_done, 1)
            dve.wait_ge(root_done, 1)
            dve.reciprocal(guess[:], root[:]).then_inc(newton, 1)
            dve.wait_ge(newton, 1)
            dve.tensor_tensor(corr[:], guess[:], guess[:], ALU.mult).then_inc(newton, 1)
            dve.wait_ge(newton, 2)
            dve.tensor_tensor(corr[:], corr[:], ve[:], ALU.mult).then_inc(newton, 1)
            dve.wait_ge(newton, 3)
            dve.tensor_scalar(corr[:], corr[:], -0.5, 1.5, ALU.mult, ALU.add).then_inc(newton, 1)
            dve.wait_ge(newton, 4)
            dve.tensor_tensor(scale, guess[:], corr[:], ALU.mult).then_inc(newton, 1)
            dve.wait_ge(newton, 5)
            dve.scalar_tensor_tensor(out=shift, in0=mean_var[:, :, 0], scalar=-1.0, in1=scale,
                                     op0=ALU.mult, op1=ALU.mult)

        @block.scalar
        def _(act):
            act.wait_ge(var_done, 1)
            act.activation(root[:], ve[:], ACT.Sqrt).then_inc(root_done, 1)


def small_head_attention(nc, k, name, cross):
    NT = k.tiles
    scale = float(1.0 / np.sqrt(D0))
    wq, wk, wv, bq, bk, bv = ((k.x_wq, k.x_wk, k.x_wv, k.x_bq, k.x_bk, k.x_bv_rows) if cross else
                              (k.a_wq, k.a_wk, k.a_wv, k.a_bq, k.a_bk, k.a_bv))
    with ExitStack() as c:
        def sb(n, shape, dt=F32):
            return c.enter_context(nc.sbuf_tensor(f"{name}_{n}", shape, dt))

        def ps(n, shape):
            return c.enter_context(nc.psum_tensor(f"{name}_{n}", shape, F32))

        new_sem = c.enter_context(stage_semaphores(nc))

        def sem(n):
            return new_sem(f"{name}_{n}")

        xn = sb("xn", [P, 2, P])
        xt = sb("xt", [P, 2, P])
        q_sb = sb("q", [P, 2, P])
        k_sb = sb("k", [P, 2, P])
        qm = sb("qm", [P, 2, GRP, P])
        km = sb("km", [P, 2, GRP, P])
        vbd = sb("vbd", [P, 4, 2, PAIRS, 2, D0 + 1])
        sd = sb("sd", [P, 2, H0, SEQ])
        mx = sb("mx", [P, 2, H0])
        pt = sb("pt", [P, 2, PAIRS, P])
        rec = sb("rec", [P, 2, H0])
        o_sb = sb("o", [P, 2, H0, D0])
        ctx_t = sb("ctx_t", [P, 4, P]) if cross else None
        ot_sb = sb("ot", [P, 2, P])
        xb = sb("xb", [P, 2, P])
        row = sb("row", [P, 2, P])
        st = sb("st", [P, 2, 6])
        mv = sb("mv", [P, 2, 2])

        ps_xt = ps("ps_xt", [P, 512])
        ps_qkv = ps("ps_qkv", [P, 4, P])
        ps_s = ps("ps_s", [P, H0, SEQ])
        ps_pt = ps("ps_pt", [P, PAIRS, P])
        ps_o = ps("ps_o", [P, 512])
        ps_y = ps("ps_y", [P, 512])
        o_ps = ps_o[:, 0:H0 * (D0 + 1)].rearrange("p (h d) -> p h d", d=D0 + 1)
        ot_ps, y_ps = ps_y[:, 0:P], ps_y[:, P:2 * P]

        setup = sem("setup")
        ctx_loaded = [sem(f"ctx_loaded{n}") for n in range(4)]
        xn_ready = sem("xn_ready")
        xt_made = sem("xt_made")
        xt_ready = sem("xt_ready")
        qkv_made = sem("qkv_made")
        qkv_ready = sem("qkv_ready")
        masked = sem("masked")
        s_made = sem("s_made")
        s_taken = sem("s_taken")
        mx_ready = sem("mx_ready")
        sub_ready = sem("sub_ready")
        p_ready = sem("p_ready")
        pt_made = sem("pt_made")
        pt_ready = sem("pt_ready")
        o_made = sem("o_made")
        rec_ready = sem("rec_ready")
        o_ready = sem("o_ready")
        ot_made = sem("ot_made")
        ot_ready = sem("ot_ready")
        y_made = sem("y_made")
        xb_ready = sem("xb_ready")
        x_added = sem("x_added")
        st_ready = sem("st_ready")
        mv_ready = sem("mv_ready")
        mv_kept = sem("mv_kept")

        nc.scalar.preload_act_table(ACT.Exp)
        block = c.enter_context(nc.Block())

        @block.sync
        def _(sp):
            if not cross:
                return

            def load_ctx(t, u):
                if late(t, 4):
                    sp.wait_ge(qkv_made, t - 3)
                sp.dma_start(ctx_t[:, u, :], k.in_ctx_t[t]).then_inc(ctx_loaded[u], 16)

            pipeline(sp, NT, load_ctx, 0)

        @block.gpsimd
        def _(pool):
            pool.memset(vbd[:], 0.0).then_inc(setup, 1)
            pool.wait_ge(setup, 1)
            pool.memset(vbd[0:SEQ, :, :, :, 0, D0:D0 + 1], 1.0)
            pool.memset(vbd[SEQ:P, :, :, :, 1, D0:D0 + 1], 1.0).then_inc(setup, 1)

            def subtract_max(t, v):
                pool.wait_ge(mx_ready, t + 1)
                pool.tensor_tensor(sd[:, v % 2], sd[:, v % 2], mx[:, v % 2].unsqueeze(2).to_broadcast([P, H0, SEQ]),
                                   ALU.subtract).then_inc(sub_ready, 1)

            def split_heads(t, v):
                pool.wait_ge(qkv_ready, t + 1)
                if late(t, 2):
                    pool.wait_ge(s_made, t - 1)
                pool.tensor_tensor(km[:, v % 2], bc(k_sb[:, v % 2], 1, GRP), k.head_mask[:].to_broadcast([P, GRP, P]),
                                   ALU.mult)
                pool.tensor_tensor(qm[:, v % 2], bc(q_sb[:, v % 2], 1, GRP), k.group_mask[:].to_broadcast([P, GRP, P]),
                                   ALU.mult).then_inc(masked, 1)

            def add_bias(t, v):
                if cross:
                    pool.wait_ge(o_ready, t + 1)
                    if late(t, 2):
                        pool.wait_ge(mv_kept, t - 1)
                    pool.tensor_tensor(row[:, v % 2], o_sb[:, v % 2].rearrange("p h d -> p (h d)"), bv[:],
                                       ALU.add).then_inc(xb_ready, 1)
                else:
                    if late(t, 2):
                        pool.wait_ge(x_added, t - 1)
                    pool.tensor_tensor(xb[:, v % 2], k.x_res[:, t], k.a_bo[:], ALU.add).then_inc(xb_ready, 1)

            def step(i, u):
                for stage, behind in ((subtract_max, 4), (split_heads, 2), (add_bias, 5)):
                    if cross and stage is subtract_max:
                        continue
                    if has(i - behind, NT):
                        stage(i - behind, (u - behind) % UNROLL)

            pipeline(pool, NT, step, 5)

        @block.tensor
        def _(pe):
            pe.wait_ge(setup, 2)

            def x_transpose(t, v):
                pe.wait_ge(xn_ready, t + 1)
                if late(t, 1):
                    pe.wait_ge(xt_ready, t)
                pe.transpose(ps_xt[:, 0:P], xn[:, v % 2], k.ident[:]).then_inc(xt_made, 1)

            def project(t, v):
                pe.wait_ge(xt_ready, t + 1)
                if late(t, 1):
                    pe.wait_ge(qkv_ready, t)
                if cross:
                    pe.wait_ge(ctx_loaded[v], 16 + 4 * (t - v))
                kv = ctx_t[:, v] if cross else xt[:, v % 2]
                pe.matmul(ps_qkv[:, 0], wq[:], xt[:, v % 2], start=True, stop=True)
                pe.matmul(ps_qkv[:, 1], wk[:], kv, start=True, stop=True)
                for b in range(2):
                    for half in range(2):
                        mm = pe.matmul(ps_qkv[half * SEQ:(half + 1) * SEQ, 2 + b], kv[:, b * SEQ:(b + 1) * SEQ],
                                       wv[:], start=True, stop=True)
                mm.then_inc(qkv_made, 1)

            def scores(t, v):
                pe.wait_ge(masked, t + 1)
                if late(t, 1):
                    pe.wait_ge(s_taken, t)
                if cross:
                    for half in range(2):
                        pe.matmul(ps_s[:, 8 * half:8 * half + 8], k.ident_bf[:], bc(k.mask_all[:, t], 1, 8),
                                  start=True, stop=True)
                for g in range(GRP):
                    for b in range(2):
                        rows = slice(b * SEQ, (b + 1) * SEQ)
                        mm = pe.matmul(ps_s[rows, GRP * g:GRP * g + GRP], qm[:, v % 2, g, rows],
                                       km[:, v % 2, :, rows], start=not cross, stop=True, skip_group_check=cross)
                mm.then_inc(s_made, 1)

            def p_transpose(t, v):
                pe.wait_ge(p_ready, t + 1)
                if late(t, 1):
                    pe.wait_ge(pt_ready, t)
                flat = sd[:, v % 2].rearrange("p (n h) s -> p n (h s)", h=2)
                for n in range(PAIRS):
                    mm = pe.transpose(ps_pt[:, n], flat[:, n], k.ident[:])
                mm.then_inc(pt_made, 1)

            def values(t, v):
                pe.wait_ge(pt_ready, t + 1)
                if late(t, 1):
                    pe.wait_ge(o_ready, t)
                for n in range(PAIRS):
                    for b in range(2):
                        rows = slice(b * SEQ, (b + 1) * SEQ)
                        mm = pe.matmul(o_ps[rows, 2 * n:2 * n + 2], pt[:, v % 2, n, rows], vbd[:, v, b, n],
                                       start=True, stop=True)
                mm.then_inc(o_made, 1)

            def o_transpose(t, v):
                pe.wait_ge(o_ready, t + 1)
                if late(t, 1):
                    pe.wait_ge(x_added, t)
                pe.transpose(ot_ps, o_sb[:, v % 2].rearrange("p h d -> p (h d)"), k.ident[:]).then_inc(ot_made, 1)

            def out_project(t, v):
                pe.wait_ge(ot_ready, t + 1)
                pe.matmul(y_ps, ot_sb[:, v % 2], k.a_wo[:], start=True, stop=True).then_inc(y_made, 1)

            def step(i, u):
                for stage, behind in ((x_transpose, 1), (o_transpose, 6), (p_transpose, 5), (project, 2),
                                      (out_project, 6), (values, 5), (scores, 3)):
                    if cross and stage in (o_transpose, out_project):
                        continue
                    if has(i - behind, NT):
                        stage(i - behind, (u - behind) % UNROLL)

            pipeline(pe, NT, step, 6)

        @block.scalar
        def _(act):
            act.wait_ge(setup, 2)

            def x_copy(t, v):
                act.wait_ge(xt_made, t + 1)
                if late(t, 2):
                    act.wait_ge(qkv_made, t - 1)
                act.copy(xt[:, v % 2], ps_xt[:, 0:P]).then_inc(xt_ready, 1)

            def qkv_copy(t, v):
                act.wait_ge(qkv_made, t + 1)
                if late(t, 2):
                    act.wait_ge(masked, t - 1)
                act.activation(k_sb[:, v % 2], ps_qkv[:, 1], ACT.Identity, bias=bk[:])
                act.activation(q_sb[:, v % 2], ps_qkv[:, 0], ACT.Identity, bias=bq[:])
                if late(t, 4):
                    act.wait_ge(o_made, t - 3)
                for half in range(2):
                    rows = slice(half * SEQ, (half + 1) * SEQ)
                    src = ps_qkv[rows, 2:4].rearrange("p b (n h d) -> p b n h d", h=2, d=D0)
                    op = act.copy(vbd[rows, v, :, :, half, 0:D0], src[:, :, :, half])
                op.then_inc(qkv_ready, 1)

            def exponential(t, v):
                act.wait_ge(s_taken if cross else sub_ready, t + 1)
                act.activation(sd[:, v % 2], sd[:, v % 2], ACT.Exp, scale=scale).then_inc(p_ready, 1)

            def p_copy(t, v):
                act.wait_ge(pt_made, t + 1)
                if late(t, 2):
                    act.wait_ge(o_made, t - 1)
                act.copy(pt[:, v % 2], ps_pt[:]).then_inc(pt_ready, 1)

            def o_copy(t, v):
                act.wait_ge(ot_made, t + 1)
                if late(t, 2):
                    act.wait_ge(y_made, t - 1)
                act.activation(ot_sb[:, v % 2], ot_ps, ACT.Identity, bias=bv[:]).then_inc(ot_ready, 1)

            def step(i, u):
                for stage, behind in ((x_copy, 1), (o_copy, 6), (p_copy, 5), (qkv_copy, 2), (exponential, 4)):
                    if cross and stage is o_copy:
                        continue
                    if has(i - behind, NT):
                        stage(i - behind, (u - behind) % UNROLL)

            pipeline(act, NT, step, 6)

        @block.vector
        def _(dve):
            def normalise(t, v):
                if late(t, 2):
                    dve.wait_ge(xt_made, t - 1)
                dve.tensor_scalar(xn[:, v % 2], k.x_res[:, t], k.ln_scale[:, bass.ds(t, 1)], k.ln_shift[:, bass.ds(t, 1)],
                                  ALU.mult, ALU.add).then_inc(xn_ready, 1)

            def softmax(t, v):
                dve.wait_ge(s_made, t + 1)
                if late(t, 2):
                    dve.wait_ge(pt_made, t - 1)
                if cross:
                    dve.tensor_reduce(mx[:, v % 2], ps_s[:], AX.X, ALU.max).then_inc(mx_ready, 1)
                    dve.wait_ge(mx_ready, t + 1)
                    dve.tensor_tensor(sd[:, v % 2], ps_s[:], mx[:, v % 2].unsqueeze(2).to_broadcast([P, H0, SEQ]),
                                      ALU.subtract).then_inc(s_taken, 1)
                else:
                    dve.tensor_tensor(sd[:, v % 2], ps_s[:], bc(k.decay[:], 1, H0), ALU.mult).then_inc(s_taken, 1)
                    dve.wait_ge(s_taken, t + 1)
                    dve.tensor_reduce(mx[:, v % 2], sd[:, v % 2], AX.X, ALU.max).then_inc(mx_ready, 1)

            def divide(t, v):
                dve.wait_ge(o_made, t + 1)
                if late(t, 2):
                    dve.wait_ge(xb_ready if cross else ot_made, t - 1)
                dve.reciprocal(rec[:, v % 2], o_ps[:, :, D0]).then_inc(rec_ready, 1)
                dve.wait_ge(rec_ready, t + 1)
                dve.tensor_tensor(o_sb[:, v % 2], o_ps[:, :, 0:D0], rec[:, v % 2].unsqueeze(2).to_broadcast([P, H0, D0]),
                                  ALU.mult).then_inc(o_ready, 1)

            def residual(t, v):
                all_rows, all_stats = (k.o_all, k.o_mean_var) if cross else (k.x_res, k.mean_var)
                dve.wait_ge(xb_ready, t + 1)
                if late(t, 2):
                    dve.wait_ge(mv_kept, t - 1)
                if not cross:
                    dve.wait_ge(y_made, t + 1)
                    dve.tensor_tensor(row[:, v % 2], y_ps, xb[:, v % 2], ALU.add).then_inc(x_added, 1)
                    dve.wait_ge(x_added, t + 1)
                keep_with_stats(dve, row[:, v % 2], all_rows[:, t], st[:, v % 2], mv[:, v % 2], all_stats[:, t], t,
                                st_ready, mv_ready, mv_kept)

            def step(i, u):
                for stage, behind in ((softmax, 4), (residual, 6), (divide, 5), (normalise, 0)):
                    if has(i - behind, NT):
                        stage(i - behind, (u - behind) % UNROLL)

            pipeline(dve, NT, step, 6)


def project_cross(nc, k):
    NT = k.tiles
    with ExitStack() as c:
        def sb(n, shape, dt=F32):
            return c.enter_context(nc.sbuf_tensor(f"xp_{n}", shape, dt))

        new_sem = c.enter_context(stage_semaphores(nc))

        def sem(n):
            return new_sem(f"xp_{n}")

        ROWS = [P, 2, GROUP, P]
        on, ot, xb, row = sb("on", ROWS), sb("ot", ROWS), sb("xb", ROWS), sb("row", ROWS)
        st = sb("st", [P, 2, GROUP, 6])
        mv = sb("mv", [P, 2, GROUP, 2])
        zero_row = sb("zero_row", [P, P])
        ps_t = [c.enter_context(nc.psum_tensor(f"xp_t{n}", [P, GROUP, P], F32)) for n in range(2)]
        ps_y = [c.enter_context(nc.psum_tensor(f"xp_y{n}", [P, GROUP, P], F32)) for n in range(2)]
        on_ready, ot_made, ot_ready, y_made = sem("on_ready"), sem("ot_made"), sem("ot_ready"), sem("y_made")
        xb_ready, x_added, row_kept = sem("xb_ready"), sem("x_added"), sem("row_kept")
        stored = [sem(f"stored{n}") for n in range(2)]
        st_ready, mv_ready, mv_kept = sem("st_ready"), sem("mv_ready"), sem("mv_kept")
        zeroed, zeros_stored = sem("zeroed"), sem("zeros_stored")
        block = c.enter_context(nc.Block())

        @block.gpsimd
        def _(pool):
            pool.memset(zero_row[:], 0.0).then_inc(zeroed, 1)

            def step(g, u):
                if late(g, 2):
                    pool.wait_ge(x_added, g - 1)
                pool.tensor_tensor(xb[:, u], k.x_res[:, group(g)], bc(k.x_bo[:], 1, GROUP), ALU.add).then_inc(xb_ready, 1)

            group_pipeline(pool, NT, step, 0)

        @block.tensor
        def _(pe):
            def step(i, u):
                if has(i, NT // GROUP):
                    pe.wait_ge(on_ready, i + 1)
                    if late(i, 2):
                        pe.wait_ge(ot_ready, i - 1)
                    for n in range(GROUP):
                        mm = pe.transpose(ps_t[u][:, n], on[:, u, n], k.ident[:])
                    mm.then_inc(ot_made, 1)
                g, v = i - 1, 1 - u
                if has(g, NT // GROUP):
                    pe.wait_ge(ot_ready, g + 1)
                    if late(g, 2):
                        pe.wait_ge(x_added, g - 1)
                    for n in range(GROUP):
                        mm = pe.matmul(ps_y[v][:, n], ot[:, v, n], k.x_wo[:], start=True, stop=True)
                    mm.then_inc(y_made, 1)

            group_pipeline(pe, NT, step, 1)

        @block.scalar
        def _(act):
            def step(i, u):
                if has(i, NT // GROUP):
                    act.wait_ge(ot_made, i + 1)
                    if late(i, 2):
                        act.wait_ge(y_made, i - 1)
                    act.activation(ot[:, u], ps_t[u][:], ACT.Identity, scale=k.x_ln_g[:], bias=k.x_ln_b[:])\
                       .then_inc(ot_ready, 1)
                g, v = i - 2, u
                if has(g, NT // GROUP):
                    act.wait_ge(x_added, g + 1)
                    act.copy(k.x_res[:, group(g)], row[:, v]).then_inc(row_kept, 1)

            group_pipeline(act, NT, step, 2)

        @block.sync
        def _(sp):
            def step(g, u):
                sp.wait_ge(x_added, g + 1)
                sp.dma_start(k.x_dram[group(g)].rearrange("n p c -> p n c"), row[:, u]).then_inc(stored[u], 16)

            sp.wait_ge(zeroed, 1)
            sp.dma_start(k.x_dram[NT:NT + NE * CAP // P].rearrange("n p c -> p n c"),
                         bc(zero_row[:], 1, NE * CAP // P)).then_inc(zeros_stored, 16)
            group_pipeline(sp, NT, step, 0)
            for n in range(2):
                sp.wait_ge(stored[n], 16 * len(range(n, NT // GROUP, 2)))
            sp.wait_ge(zeros_stored, 16)

        @block.vector
        def _(dve):
            stats = GroupStats(dve, NT, row, k.mean_var, st, mv, st_ready, mv_ready, mv_kept)

            def step(i, u):
                if has(i, NT // GROUP):
                    if late(i, 2):
                        dve.wait_ge(ot_made, i - 1)
                    for n in range(GROUP):
                        op = dve.tensor_scalar(on[:, u, n], k.o_all[:, i * GROUP + n],
                                               k.o_scale[:, bass.ds(i * GROUP + n, 1)],
                                               k.o_shift[:, bass.ds(i * GROUP + n, 1)], ALU.mult, ALU.add)
                    op.then_inc(on_ready, 1)
                g, v = i - 2, u
                if has(g, NT // GROUP):
                    dve.wait_ge(xb_ready, g + 1)
                    dve.wait_ge(y_made, g + 1)
                    if late(g, 2):
                        dve.wait_ge(row_kept, g - 1)
                        dve.wait_ge(stored[v], 8 * (g - v))
                    dve.tensor_tensor(row[:, v], ps_y[v][:], xb[:, v], ALU.add).then_inc(x_added, 1)
                stats.keep_and_aggregate(i - 3, 1 - u)
                if has(g, NT // GROUP):
                    dve.wait_ge(x_added, g + 1)
                    stats.by_row(g, v)

            group_pipeline(dve, NT, step, 4)


def set_up(nc, k):
    NT = k.tiles
    chunk = 4
    with ExitStack() as c:
        new_sem = c.enter_context(stage_semaphores(nc))

        def sem(n):
            return new_sem(f"su_{n}")

        dist = c.enter_context(nc.sbuf_tensor("su_dist", [P, SEQ], F32))
        dd = c.enter_context(nc.sbuf_tensor("su_dd", [P, 1], F32))
        dd_neg = c.enter_context(nc.sbuf_tensor("su_dd_neg", [P, 1], F32))
        dd_abs = c.enter_context(nc.sbuf_tensor("su_dd_abs", [P, 1], F32))
        mask_in = c.enter_context(nc.sbuf_tensor("su_mask", [P, NT, SEQ], I32))
        st = c.enter_context(nc.sbuf_tensor("su_st", [P, 2, 6], F32))
        x_loaded = [sem(f"x_loaded{n}") for n in range(NT // chunk)]
        loaded, mask_loaded, dd_loaded = sem("loaded"), sem("mask_loaded"), sem("dd_loaded")
        dd_ready, dec, st_ready, mv_ready = sem("dd_ready"), sem("dec"), sem("st_ready"), sem("mv_ready")
        mask_ready = sem("mask_ready")
        block = c.enter_context(nc.Block())

        @block.sync
        def _(sp):
            for n in range(NT // chunk):
                sp.dma_start(k.x_res[:, n * chunk:(n + 1) * chunk],
                             k.in_x[n * chunk:(n + 1) * chunk].rearrange("n p c -> p n c")).then_inc(x_loaded[n], 16)
            sp.dma_start(mask_in[:], k.in_mask.rearrange("n p s -> p n s")).then_inc(mask_loaded, 16)

        @block.scalar
        def _(act):
            act.dma_start(dist[:], k.in_dist).then_inc(dd_loaded, 16)
            act.dma_start(dd[:], k.in_dd.to_broadcast([P, 1])).then_inc(dd_loaded, 16)
            for tile, src in k.loads:
                act.dma_start(tile, src).then_inc(loaded, 16)
            act.wait_ge(dd_ready, 2)
            act.activation(k.decay[:], dist[:], ACT.Exp, scale=dd_abs[:]).then_inc(dec, 1)
            act.wait_ge(loaded, 16 * len(k.loads))

        @block.vector
        def _(dve):
            dve.wait_ge(dd_loaded, 32)
            dve.tensor_scalar(dd_neg[:], dd[:], -1.0, None, ALU.mult).then_inc(dd_ready, 1)
            dve.wait_ge(dd_ready, 1)
            dve.tensor_tensor(dd_abs[:], dd[:], dd_neg[:], ALU.min).then_inc(dd_ready, 1)
            for n in range(NT // chunk):
                dve.wait_ge(x_loaded[n], 16)
                for t in range(n * chunk, (n + 1) * chunk):
                    if t >= 2:
                        dve.wait_ge(mv_ready, t - 1)
                    dve.bn_stats(st[:, t % 2], k.x_res[:, t]).then_inc(st_ready, 1)
                    dve.wait_ge(st_ready, t + 1)
                    dve.bn_aggr(k.mean_var[:, t], st[:, t % 2]).then_inc(mv_ready, 1)
            dve.wait_ge(mask_loaded, 16)
            dve.wait_ge(loaded, 16 * len(k.loads))
            dve.tensor_scalar(k.mask_all[:], mask_in[:], 0.0, NEG, ALU.is_equal, ALU.mult).then_inc(mask_ready, 1)
            dve.wait_ge(mask_ready, 1)
            dve.tensor_tensor(k.mask_all[:], k.mask_all[:], bc(k.causal[:], 1, NT), ALU.min)


def router(nc, k, name, weight, bias, xn_dram, x_copy_dram):
    NT = k.tiles
    NG = NT // GROUP
    with ExitStack() as c:
        def sb(n, shape, dt=F32):
            return c.enter_context(nc.sbuf_tensor(f"{name}_{n}", shape, dt))

        new_sem = c.enter_context(stage_semaphores(nc))

        def sem(n):
            return new_sem(f"{name}_{n}")

        BUFS = 4
        xn = sb("xn", [P, BUFS, GROUP, P])
        xt = sb("xt", [P, BUFS, GROUP, P])
        ps_t = [c.enter_context(nc.psum_tensor(f"{name}_t{n}", [P, GROUP, P], F32)) for n in range(BUFS)]
        ps_l = [c.enter_context(nc.psum_tensor(f"{name}_l{n}", [P, 512], F32)) for n in range(BUFS)]
        xn_ready, xt_made, xt_ready = sem("xn_ready"), sem("xt_made"), sem("xt_ready")
        l_made, l_ready, x_stored = sem("l_made"), sem("l_ready"), sem("x_stored")
        xn_stored = [sem(f"xn_stored{n}") for n in range(BUFS)]
        block = c.enter_context(nc.Block())

        @block.sync
        def _(sp):
            def step(g, u):
                sp.wait_ge(xn_ready, g + 1)
                sp.dma_start(xn_dram[group(g)].rearrange("n p c -> p n c"), xn[:, u]).then_inc(xn_stored[u], 16)
                if x_copy_dram is not None:
                    sp.dma_start(x_copy_dram[group(g)].rearrange("n p c -> p n c"), k.x_res[:, group(g)])\
                        .then_inc(x_stored, 16)

            pipeline(sp, NG, step, 0, BUFS, BUFS)
            for n in range(BUFS):
                sp.wait_ge(xn_stored[n], 16 * len(range(n, NG, BUFS)))
            if x_copy_dram is not None:
                sp.wait_ge(x_stored, 16 * NG)

        @block.tensor
        def _(pe):
            def step(i, u):
                if has(i, NG):
                    pe.wait_ge(xn_ready, i + 1)
                    if late(i, BUFS):
                        pe.wait_ge(xt_ready, i - BUFS + 1)
                    for n in range(GROUP):
                        mm = pe.transpose(ps_t[u][:, n], xn[:, u, n], k.ident[:])
                    mm.then_inc(xt_made, 1)
                g, v = i - 1, (u - 1) % BUFS
                if has(g, NG):
                    pe.wait_ge(xt_ready, g + 1)
                    if late(g, BUFS):
                        pe.wait_ge(l_ready, g - BUFS + 1)
                    for n in range(GROUP):
                        mm = pe.matmul(ps_l[v][:, n * NE:(n + 1) * NE], xt[:, v, n], weight[:], start=True, stop=True)
                    mm.then_inc(l_made, 1)

            pipeline(pe, NG, step, 1, BUFS, 2 * BUFS)

        @block.scalar
        def _(act):
            def step(g, u):
                act.wait_ge(xt_made, g + 1)
                if late(g, BUFS):
                    act.wait_ge(l_made, g - BUFS + 1)
                act.copy(xt[:, u], ps_t[u][:]).then_inc(xt_ready, 1)

            pipeline(act, NG, step, 0, BUFS, BUFS)

        @block.vector
        def _(dve):
            def step(i, u):
                if has(i, NG):
                    if late(i, BUFS):
                        dve.wait_ge(xt_made, i - BUFS + 1)
                        dve.wait_ge(xn_stored[u], 16 // BUFS * (i - u))
                    normalise_group(dve, k, i, xn[:, u]).then_inc(xn_ready, 1)
                g, v = i - 2, (u - 2) % BUFS
                if has(g, NG):
                    dve.wait_ge(l_made, g + 1)
                    dve.tensor_tensor(k.logits[:, group(g)],
                                      ps_l[v][:, 0:GROUP * NE].rearrange("p (n e) -> p n e", e=NE),
                                      bc(bias[:], 1, GROUP), ALU.add).then_inc(l_ready, 1)

            pipeline(dve, NG, step, 2, BUFS, BUFS)


def chosen_slots(nc, k, name, top, slots, w_slot):
    NT = k.tiles
    NS = slots
    with ExitStack() as c:
        def sb(n, shape, dt=F32):
            return c.enter_context(nc.sbuf_tensor(f"{name}_{n}", shape, dt))

        new_sem = c.enter_context(stage_semaphores(nc))

        def sem(n):
            return new_sem(f"{name}_{n}")

        E = [P, NT, NE]
        m = sb("m", [P, top, NT])
        key = sb("key", E)
        first = sb("first", [P, NT])
        oh = [sb(f"oh{n}", E) for n in range(top)]
        rest = sb("rest", E)
        sel_bf = sb("sel_bf", E, BF16)
        total = sb("total", E)
        rank = sb("rank", E)
        slot_e = sb("slot_e", E)
        keep = sb("keep", E)
        tmp = sb("tmp", E)
        slot = sb("slot", [P, top, NT])
        slot_i = sb("slot_i", [P, top, NT], I32)
        part_i = sb("part_i", [P, 2, top, NT], I32)
        part = sb("part", [P, 2, top, NT])
        zeros = sb("zeros", [P, NT])
        small = sb("small", [P, 6, NE])
        small_i = sb("small_i", [P, 2, NE], I32)
        lists = 5 if top == 2 else 2
        row_hot = sb("row_hot", [P, NT, P], BF16)
        tile_hot = sb("tile_hot", [P, NT, NS], BF16)
        listed = sb("listed", [P, NT, lists, NS], BF16)
        w = sb("w", [P, 4, NT])
        parts = sb("parts", [P, 2, 3, NT])
        parts_bf = sb("parts_bf", [P, 2, 3, NT], BF16)
        table = sb("table", [P, lists, NS])
        ids = sb("ids", [P, 5, NS])
        ge = sb("ge", [P, NS, NE]) if top == 1 else None
        ps_r = c.enter_context(nc.psum_tensor(f"{name}_r", [P, 512], F32))
        ps_n = c.enter_context(nc.psum_tensor(f"{name}_n", [P, 512], F32))
        ps_l = c.enter_context(nc.psum_tensor(f"{name}_l", [P, 512], F32))
        done = sem("done")
        e_ready = sem("e_ready")
        d_ready = sem("d_ready")
        sel_ready, ranks_made = sem("sel_ready"), sem("ranks_made")
        listed_ready, listed_made = sem("listed_ready"), sem("listed_made")
        block = c.enter_context(nc.Block())

        @block.scalar
        def _(act):
            if top == 2:
                act.wait_ge(d_ready, 1)
                act.activation(w[:, 1], w[:, 0], ACT.Exp).then_inc(e_ready, 1)

        @block.tensor
        def _(pe):
            flat = sel_bf[:].rearrange("p n e -> p (n e)")
            pe.wait_ge(sel_ready, 1)
            pe.matmul(ps_r[:, 0:NT * NE], k.before[:], flat, start=True, stop=True)
            pe.matmul(ps_n[:, 0:NT * NE], k.ones_bf[:], flat, start=True, stop=True).then_inc(ranks_made, 1)
            for n in range(top):
                pe.wait_ge(listed_ready, n + 1)
                for t in range(NT):
                    mm = pe.matmul(ps_l[:, 0:lists * NS], row_hot[:, t], listed[:, t].rearrange("p l s -> p (l s)"),
                                   start=(n == 0 and t == 0), stop=(n == top - 1 and t == NT - 1))
                mm.then_inc(listed_made, 1)

        @block.vector
        def _(dve):
            count = [0]

            def op(instruction):
                count[0] += 1
                instruction.then_inc(done, 1)
                dve.wait_ge(done, count[0])

            def all_e(ap):
                return ap.unsqueeze(2).to_broadcast(E)

            scores = k.logits
            for n in range(top):
                op(dve.tensor_reduce(m[:, n], scores[:], AX.X, ALU.max))
                op(dve.tensor_tensor(oh[n][:], scores[:], all_e(m[:, n]), ALU.is_equal))
                op(dve.scalar_tensor_tensor(out=key[:], in0=oh[n][:], scalar=-float(NE), in1=bc(k.iota_e[:], 1, NT),
                                            op0=ALU.mult, op1=ALU.add))
                op(dve.tensor_reduce(first[:], key[:], AX.X, ALU.min))
                op(dve.tensor_tensor(oh[n][:], key[:], all_e(first[:]), ALU.is_equal))
                if n == 0 and top == 2:
                    op(dve.scalar_tensor_tensor(out=rest[:], in0=oh[0][:], scalar=-3e38, in1=scores[:],
                                                op0=ALU.mult, op1=ALU.add))
                    scores = rest
            if top == 2:
                dve.tensor_tensor(w[:, 0], m[:, 1], m[:, 0], ALU.subtract).then_inc(d_ready, 1)
                op(dve.tensor_tensor(sel_bf[:], oh[0][:], oh[1][:], ALU.add))
            else:
                op(dve.tensor_copy(sel_bf[:], oh[0][:]))
            dve.memset(zeros[:], 0.0).then_inc(sel_ready, 1)

            dve.wait_ge(ranks_made, 1)
            op(dve.tensor_copy(total[:], ps_n[:, 0:NT * NE].rearrange("p (n e) -> p n e", e=NE)))
            for e in range(NE):
                op(dve.tensor_tensor_scan(rank[:, :, e], total[:, :, e], zeros[:], 0.0, ALU.add, ALU.add))
            if top == 1:
                op(dve.tensor_scalar(small_i[:, 0], rank[:, NT - 1], float(P - 1), None, ALU.add))
                op(dve.tensor_scalar(small_i[:, 1], small_i[:, 0], 7, None, ALU.arith_shift_right))
                op(dve.tensor_copy(small[:, 0], small_i[:, 1]))
                op(dve.tensor_tensor_scan(small[:, 1], small[:, 0], zeros[:, 0:NE], 0.0, ALU.add, ALU.add))
                op(dve.tensor_tensor(small[:, 2], small[:, 1], small[:, 0], ALU.subtract))
                op(dve.tensor_scalar(small[:, 3], small[:, 2], float(P), 1.0, ALU.mult, ALU.add))
                op(dve.tensor_tensor(ge[:], k.iota_s[:, 0:NS].unsqueeze(2).to_broadcast([P, NS, NE]),
                                     bc(small[:, 1], 1, NS), ALU.is_ge))
                op(dve.tensor_reduce(ids[:, 0], ge[:], AX.X, ALU.add))
                op(dve.tensor_scalar(k.tile_expert[:], ids[:, 0], float(NE - 1), None, ALU.min))
            op(dve.tensor_tensor(rank[:], rank[:], total[:], ALU.subtract))
            op(dve.tensor_tensor(rank[:], rank[:], ps_r[:, 0:NT * NE].rearrange("p (n e) -> p n e", e=NE), ALU.add))
            first_slot = k.iota_cap[:] if top == 2 else small[:, 3]
            op(dve.tensor_tensor(slot_e[:], rank[:], bc(first_slot, 1, NT), ALU.add))
            if top == 2:
                op(dve.tensor_scalar(keep[:], rank[:], float(CAP), None, ALU.is_lt))
                op(dve.tensor_tensor(slot_e[:], slot_e[:], keep[:], ALU.mult))
            for n in range(top):
                op(dve.tensor_tensor(tmp[:], slot_e[:], oh[n][:], ALU.mult))
                op(dve.tensor_reduce(slot[:, n], tmp[:], AX.X, ALU.add))
            op(dve.tensor_scalar(slot_i[:], slot[:], -1.0, None, ALU.add))
            op(dve.tensor_scalar(part_i[:, 0], slot_i[:], 7, None, ALU.arith_shift_right))
            op(dve.tensor_scalar(part_i[:, 1], slot_i[:], P - 1, None, ALU.bitwise_and))
            op(dve.tensor_copy(part[:], part_i[:]))

            if top == 2:
                dve.wait_ge(e_ready, 1)
                op(dve.tensor_scalar(w[:, 0], w[:, 1], 1.0, None, ALU.add))
                op(dve.reciprocal(w[:, 2], w[:, 0]))
                op(dve.tensor_tensor(w[:, 3], w[:, 1], w[:, 2], ALU.mult))
                op(dve.tensor_copy(parts[:, :, 0], w[:, 2:4]))
                for n in range(3):
                    op(dve.tensor_copy(parts_bf[:, :, n], parts[:, :, n]))
                    if n < 2:
                        op(dve.tensor_tensor(parts[:, :, n + 1], parts[:, :, n], parts_bf[:, :, n], ALU.subtract))

            for n in range(top):
                if n == 1:
                    dve.wait_ge(listed_made, 1)
                op(dve.tensor_tensor(row_hot[:], bc(k.iota_p[:], 1, NT),
                                     part[:, 1, n].unsqueeze(2).to_broadcast([P, NT, P]), ALU.is_equal))
                op(dve.tensor_tensor(tile_hot[:], bc(k.iota_s[:, 0:NS], 1, NT),
                                     part[:, 0, n].unsqueeze(2).to_broadcast([P, NT, NS]), ALU.is_equal))
                op(dve.tensor_tensor(listed[:, :, 0], tile_hot[:], k.iota_s1[:, 0:NT].unsqueeze(2).to_broadcast([P, NT, NS]),
                                     ALU.mult))
                op(dve.tensor_scalar(listed[:, :, 1], tile_hot[:], k.place[:], None, ALU.mult))
                for q in range(2, lists):
                    op(dve.tensor_tensor(listed[:, :, q], tile_hot[:],
                                         parts_bf[:, n, q - 2].unsqueeze(2).to_broadcast([P, NT, NS]), ALU.mult))
                dve.memset(zeros[:, 0:1], 0.0).then_inc(listed_ready, 1)
            dve.wait_ge(listed_made, top)
            op(dve.tensor_copy(table[:], ps_l[:, 0:lists * NS].rearrange("p (l s) -> p l s", s=NS)))
            op(dve.tensor_scalar(ids[:, 1], table[:, 0], float(P), -float(P), ALU.mult, ALU.add))
            op(dve.tensor_tensor(ids[:, 2], ids[:, 1], table[:, 1], ALU.add))
            op(dve.tensor_scalar(k.gather_idx[:, 0:NS], ids[:, 2], 0.0, None, ALU.max))
            op(dve.tensor_scalar(ids[:, 3], table[:, 0], 0.0, None, ALU.is_equal))
            op(dve.tensor_tensor(ids[:, 3], ids[:, 3], k.empty_id[:, 0:NS], ALU.mult))
            op(dve.tensor_tensor(k.scatter_idx[:, 0:NS], ids[:, 2], ids[:, 3], ALU.add))
            if top == 2:
                op(dve.tensor_tensor(w_slot[:], table[:, 4], table[:, 3], ALU.add))
                op(dve.tensor_tensor(w_slot[:], w_slot[:], table[:, 2], ALU.add))


def two_expert_ffn(nc, k):
    NT = k.tiles
    with ExitStack() as c:
        def sb(n, shape, dt=F32):
            return c.enter_context(nc.sbuf_tensor(f"m0_{n}", shape, dt))

        new_sem = c.enter_context(stage_semaphores(nc))

        def sem(n):
            return new_sem(f"m0_{n}")

        HALVES = CAP // P
        xg = sb("xg", [P, NE * HALVES, P])
        xgt = sb("xgt", [P, 2, CAP])
        gate = sb("gate", [P, 2, 2, CAP])
        hid = sb("hid", [P, 2, 2, CAP])
        y = sb("weighted", [P, NE * HALVES, P])
        st = sb("st", [P, 2, 6])
        ps_t = c.enter_context(nc.psum_tensor("m0_t", [P, 512], F32))
        ps_h = [c.enter_context(nc.psum_tensor(f"m0_h{n}", [P, 2, 2, CAP], F32)) for n in range(2)]
        ps_y = c.enter_context(nc.psum_tensor("m0_y", [P, 512], F32))
        gathered, added = k.gathered0, k.added0
        xt_made, xt_ready, h_made, gate_ready = sem("xt_made"), sem("xt_ready"), sem("h_made"), sem("gate_ready")
        hid_ready, y_made, y_ready = sem("hid_ready"), sem("y_made"), sem("y_ready")
        st_ready, mv_ready = sem("st_ready"), sem("mv_ready")
        chunk = 4
        x_loaded = [sem(f"x_loaded{n}") for n in range(4)]
        nc.scalar.preload_act_table(ACT.Silu)
        block = c.enter_context(nc.Block())

        @block.gpsimd
        def _(pool):
            for n in range(NE * HALVES):
                pool.indirect_dma_start(xg[:, n], None, k.xn_rows,
                                        bass.IndirectOffsetOnAxis(ap=k.gather_idx[:, n:n + 1], axis=0))\
                    .then_inc(gathered[n], 16)
            for e in range(NE):
                pool.wait_ge(y_ready, HALVES * (e + 1))
                if e:
                    pool.wait_ge(added[e - 1], 16 * HALVES)
                for half in range(HALVES):
                    n = HALVES * e + half
                    pool.indirect_dma_start(k.x_rows, bass.IndirectOffsetOnAxis(ap=k.scatter_idx[:, n:n + 1], axis=0),
                                            y[:, n], None, compute_op=ALU.add).then_inc(added[e], 16)

        @block.tensor
        def _(pe):
            def transposes(e):
                if e:
                    pe.wait_ge(xt_ready, e)
                for half in range(HALVES):
                    pe.wait_ge(gathered[HALVES * e + half], 16)
                    mm = pe.transpose(ps_t[:, half * P:(half + 1) * P], xg[:, HALVES * e + half], k.ident[:])
                mm.then_inc(xt_made, 1)

            def hidden(e):
                pe.wait_ge(xt_ready, e + 1)
                if e >= 2:
                    pe.wait_ge(hid_ready, e - 1)
                for n, weight in ((1, k.f0_v), (0, k.f0_w)):
                    for f in range(2):
                        mm = pe.matmul(ps_h[e % 2][:, n, f], weight[:, e, f * P:(f + 1) * P], xgt[:, e % 2],
                                       start=True, stop=True)
                mm.then_inc(h_made, 1)

            def output(e):
                pe.wait_ge(hid_ready, e + 1)
                if e:
                    pe.wait_ge(y_ready, HALVES * e)
                for half in range(HALVES):
                    for f in range(2):
                        mm = pe.matmul(ps_y[:, half * P:(half + 1) * P], hid[:, e % 2, f, half * P:(half + 1) * P],
                                       k.f0_out[:, e, f], start=(f == 0), stop=(f == 1))
                mm.then_inc(y_made, 1)

            for i in range(NE + 2):
                if i < NE:
                    transposes(i)
                if 1 <= i <= NE:
                    hidden(i - 1)
                if i >= 2:
                    output(i - 2)

        @block.scalar
        def _(act):
            for i in range(NE + 1):
                if i < NE:
                    act.wait_ge(xt_made, i + 1)
                    if i >= 2:
                        act.wait_ge(h_made, i - 1)
                    act.copy(xgt[:, i % 2], ps_t[:, 0:CAP]).then_inc(xt_ready, 1)
                if i >= 1:
                    e = i - 1
                    act.wait_ge(h_made, e + 1)
                    if e >= 2:
                        act.wait_ge(hid_ready, e - 1)
                    act.activation(gate[:, e % 2], ps_h[e % 2][:, 1], ACT.Silu).then_inc(gate_ready, 1)

        @block.sync
        def _(sp):
            for e in range(NE):
                sp.wait_ge(added[e], 16 * HALVES)
            for n in range(NT // chunk):
                if n >= 4:
                    sp.wait_ge(x_loaded[n % 4], 16 * (n // 4))
                sp.dma_start(k.x_res[:, n * chunk:(n + 1) * chunk],
                             k.x_dram[n * chunk:(n + 1) * chunk].rearrange("n p c -> p n c"))\
                    .then_inc(x_loaded[n % 4], 16)

        @block.vector
        def _(dve):
            for e in range(NE):
                dve.wait_ge(gate_ready, e + 1)
                if e >= 2:
                    dve.wait_ge(y_made, e - 1)
                dve.tensor_tensor(hid[:, e % 2], ps_h[e % 2][:, 0], gate[:, e % 2], ALU.mult).then_inc(hid_ready, 1)
                dve.wait_ge(y_made, e + 1)
                for half in range(HALVES):
                    n = HALVES * e + half
                    dve.tensor_scalar(y[:, n], ps_y[:, half * P:(half + 1) * P], k.w_slot[:, n:n + 1], None,
                                      ALU.mult).then_inc(y_ready, 1)
            for n in range(NT // chunk):
                dve.wait_ge(x_loaded[n % 4], 16 * (n // 4 + 1))
                for t in range(n * chunk, (n + 1) * chunk):
                    if t >= 2:
                        dve.wait_ge(mv_ready, t - 1)
                    dve.bn_stats(st[:, t % 2], k.x_res[:, t]).then_inc(st_ready, 1)
                    dve.wait_ge(st_ready, t + 1)
                    dve.bn_aggr(k.mean_var[:, t], st[:, t % 2]).then_inc(mv_ready, 1)


def wide_head_attention(nc, k):
    NT = k.tiles
    HALF = D1 // 2
    scale = float(D1) ** -0.5
    with ExitStack() as c:
        def sb(n, shape, dt=F32):
            return c.enter_context(nc.sbuf_tensor(f"wa_{n}", shape, dt))

        def ps(n, shape):
            return c.enter_context(nc.psum_tensor(f"wa_{n}", shape, F32))

        new_sem = c.enter_context(stage_semaphores(nc))

        def sem(n):
            return new_sem(f"wa_{n}")

        xn = sb("xn", [P, 2, P])
        xt = sb("xt", [P, 2, P])
        rot = [sb(f"rot{n}", [P, H1, 2, HALF]) for n in range(2)]
        cross = [sb(f"cross{n}", [P, H1, 2, HALF]) for n in range(2)]
        qt = sb("qt", [P, 2, PAIRS, P])
        kbd = sb("kbd", [P, 2, PAIRS, 2, P])
        vbd = sb("vbd", [P, 2, 2, PAIRS, 2, D1])
        sd = sb("sd", [P, 2, H1, SEQ])
        mx = sb("mx", [P, 2, H1])
        total = sb("total", [P, 2, H1])
        rec = sb("rec", [P, 2, H1])
        pt = sb("pt", [P, 2, PAIRS, P])
        o_sb = sb("o", [P, 2, H1, D1])
        ot = sb("ot", [P, 2, PAIRS, P])
        xb = sb("xb", [P, 2, P])
        row = sb("row", [P, 2, P])
        st = sb("st", [P, 2, 6])
        mv = sb("mv", [P, 2, 2])

        ps_p = ps("ps_p", [P, 2, 512])
        ps_t = ps("ps_t", [P, PAIRS, P])
        ps_s = ps("ps_s", [P, H1, SEQ])
        ps_o = ps("ps_o", [P, 2, 512])

        setup = sem("setup")
        xn_ready, xt_made, xt_ready = sem("xn_ready"), sem("xt_made"), sem("xt_ready")
        qk_made = [sem("q_made"), sem("k_made")]
        crossed = [sem("q_crossed"), sem("k_crossed")]
        rotated = [sem("q_rotated"), sem("k_rotated")]
        qk_t_made = [sem("qt_made"), sem("kt_made")]
        qk_t_ready = [sem("qt_ready"), sem("kt_ready")]
        v_made, v_ready = sem("v_made"), sem("v_ready")
        s_made, mx_ready, s_taken, p_ready = sem("s_made"), sem("mx_ready"), sem("s_taken"), sem("p_ready")
        total_ready, rec_ready = sem("total_ready"), sem("rec_ready")
        pt_made, pt_ready = sem("pt_made"), sem("pt_ready")
        o_made, o_ready, ot_made, ot_ready = sem("o_made"), sem("o_ready"), sem("ot_made"), sem("ot_ready")
        y_made, xb_ready, x_added = sem("y_made"), sem("xb_ready"), sem("x_added")
        st_ready, mv_ready, mv_kept = sem("st_ready"), sem("mv_ready"), sem("mv_kept")

        TURNS = [("o", 3, ot_ready), ("q", 1, qk_t_ready[0]), ("p", 2, pt_ready),
                 ("k", 1, qk_t_ready[1])]

        def wait_for_turn(pe, user, i):
            at = [n for n, _, _ in TURNS].index(user)
            for back in range(1, 4 * len(TURNS)):
                steps, n = divmod(at - back, len(TURNS))
                _, behind, copied = TURNS[n]
                t = i + steps - behind
                if has(t, NT):
                    pe.wait_ge(copied, t + 1)
                    return

        nc.scalar.preload_act_table(ACT.Exp)
        block = c.enter_context(nc.Block())

        @block.gpsimd
        def _(pool):
            pool.memset(kbd[:], 0.0)
            pool.memset(vbd[:], 0.0).then_inc(setup, 1)

            def step(i, u):
                t, v = i - 3, (u - 3) % 2
                if has(t, NT):
                    if late(t, 2):
                        pool.wait_ge(x_added, t - 1)
                    pool.tensor_tensor(xb[:, v], k.x_res[:, t], k.l1_bo[:], ALU.add).then_inc(xb_ready, 1)
                t = i - 1
                if has(t, NT):
                    for n in range(2):
                        pool.wait_ge(crossed[n], t + 1)
                        pool.tensor_tensor(rot[n][:], rot[n][:], cross[n][:], ALU.add).then_inc(rotated[n], 1)

            pipeline(pool, NT, step, 3, 2, 6)

        @block.tensor
        def _(pe):
            pe.wait_ge(setup, 1)

            def x_transpose(i, t, v):
                pe.wait_ge(xn_ready, t + 1)
                pe.transpose(ps_o[:, 1, 0:P], xn[:, v], k.ident[:]).then_inc(xt_made, 1)

            def project(n):
                def stage(i, t, v):
                    if n == 0:
                        pe.wait_ge(xt_ready, t + 1)
                        if late(t, 1):
                            pe.wait_ge(v_ready, t)
                    else:
                        pe.wait_ge(crossed[0], t + 1)
                    weight = (k.l1_wq, k.l1_wk)[n]
                    for half in range(2):
                        mm = pe.matmul(ps_p[:, half], xt[:, v], weight[:, half * 512:(half + 1) * 512],
                                       start=True, stop=True)
                    mm.then_inc(qk_made[n], 1)
                return stage

            def project_v(i, t, v):
                pe.wait_ge(crossed[1], t + 1)
                for b in range(2):
                    for half in range(2):
                        mm = pe.matmul(ps_p[half * SEQ:(half + 1) * SEQ, b], xt[:, v, b * SEQ:(b + 1) * SEQ],
                                       k.l1_wv[:, half], start=True, stop=True)
                mm.then_inc(v_made, 1)

            def qk_transpose(n):
                def stage(i, t, v):
                    pe.wait_ge(rotated[n], t + 1)
                    wait_for_turn(pe, "qk"[n], i)
                    flat = rot[n][:].rearrange("p (n h) s d -> p n (h s d)", h=2)
                    for m in range(PAIRS):
                        mm = pe.transpose(ps_t[:, m], flat[:, m], k.ident[:])
                    mm.then_inc(qk_t_made[n], 1)
                return stage

            def scores(i, t, v):
                pe.wait_ge(qk_t_ready[0], t + 1)
                pe.wait_ge(qk_t_ready[1], t + 1)
                if late(t, 1):
                    pe.wait_ge(s_taken, t)
                for half in range(2):
                    pe.matmul(ps_s[:, 8 * half:8 * half + 8], k.ident_bf[:], bc(k.causal[:], 1, 8),
                              start=True, stop=True)
                for m in range(PAIRS):
                    for b in range(2):
                        rows = slice(b * SEQ, (b + 1) * SEQ)
                        mm = pe.matmul(ps_s[rows, 2 * m:2 * m + 2], qt[:, v, m, rows], kbd[:, v, m, :, rows],
                                       start=False, stop=True, skip_group_check=True)
                mm.then_inc(s_made, 1)

            def p_transpose(i, t, v):
                pe.wait_ge(p_ready, t + 1)
                wait_for_turn(pe, "p", i)
                flat = sd[:, v].rearrange("p (n h) s -> p n (h s)", h=2)
                for m in range(PAIRS):
                    mm = pe.transpose(ps_t[:, m], flat[:, m], k.ident[:])
                mm.then_inc(pt_made, 1)

            def values(i, t, v):
                pe.wait_ge(pt_ready, t + 1)
                pe.wait_ge(v_ready, t + 1)
                if late(t, 1):
                    pe.wait_ge(x_added, t)
                if has(i, NT):
                    pe.wait_ge(xt_ready, i + 1)
                for m in range(PAIRS):
                    for b in range(2):
                        rows = slice(b * SEQ, (b + 1) * SEQ)
                        mm = pe.matmul(ps_o[rows, m // 4, m % 4 * P:(m % 4 + 1) * P], pt[:, v, m, rows], vbd[:, v, b, m],
                                       start=True, stop=True)
                mm.then_inc(o_made, 1)

            def o_transpose(i, t, v):
                pe.wait_ge(o_ready, t + 1)
                wait_for_turn(pe, "o", i)
                flat = o_sb[:, v].rearrange("p (n h) d -> p n (h d)", h=2)
                for m in range(PAIRS):
                    mm = pe.transpose(ps_t[:, m], flat[:, m], k.ident[:])
                mm.then_inc(ot_made, 1)

            def out_project(i, t, v):
                pe.wait_ge(ot_ready, t + 1)
                for m in range(PAIRS):
                    mm = pe.matmul(ps_o[:, 0, 0:P], ot[:, v, m], k.l1_wo[:, m], start=(m == 0), stop=(m == PAIRS - 1))
                mm.then_inc(y_made, 1)

            def step(i, u):
                for stage, behind in ((project(0), 1), (o_transpose, 3), (scores, 2), (project(1), 1),
                                      (qk_transpose(0), 1), (out_project, 3), (x_transpose, 0), (p_transpose, 2),
                                      (project_v, 1), (qk_transpose(1), 1), (values, 2)):
                    if has(i - behind, NT):
                        stage(i, i - behind, (u - behind) % 2)

            pipeline(pe, NT, step, 3, 2, 6)

        @block.scalar
        def _(act):
            act.wait_ge(setup, 1)

            def x_copy(t, v):
                act.wait_ge(xt_made, t + 1)
                if late(t, 2):
                    act.wait_ge(v_made, t - 1)
                act.copy(xt[:, v], ps_o[:, 1, 0:P]).then_inc(xt_ready, 1)

            def q_copy(t, v):
                act.wait_ge(qk_t_made[0], t + 1)
                if late(t, 2):
                    act.wait_ge(s_made, t - 1)
                act.copy(qt[:, v], ps_t[:]).then_inc(qk_t_ready[0], 1)

            def k_copy(t, v):
                act.wait_ge(qk_t_made[1], t + 1)
                act.copy(kbd[0:SEQ, v, :, 0], ps_t[0:SEQ])
                act.copy(kbd[SEQ:P, v, :, 1], ps_t[SEQ:P]).then_inc(qk_t_ready[1], 1)

            def v_copy(t, v):
                act.wait_ge(v_made, t + 1)
                if late(t, 2):
                    act.wait_ge(o_made, t - 1)
                for half in range(2):
                    rows = slice(half * SEQ, (half + 1) * SEQ)
                    op = act.copy(vbd[rows, v, :, :, half], ps_p[rows].rearrange("p b (n d) -> p b n d", d=D1))
                op.then_inc(v_ready, 1)

            def exponential(t, v):
                act.wait_ge(s_taken, t + 1)
                act.activation(sd[:, v], sd[:, v], ACT.Exp, scale=scale).then_inc(p_ready, 1)

            def p_copy(t, v):
                act.wait_ge(pt_made, t + 1)
                if late(t, 2):
                    act.wait_ge(o_made, t - 1)
                act.copy(pt[:, v], ps_t[:]).then_inc(pt_ready, 1)

            def o_copy(t, v):
                act.wait_ge(ot_made, t + 1)
                if late(t, 2):
                    act.wait_ge(y_made, t - 1)
                act.copy(ot[:, v], ps_t[:]).then_inc(ot_ready, 1)

            def step(i, u):
                for stage, behind in ((o_copy, 3), (exponential, 2), (q_copy, 1), (x_copy, 0), (p_copy, 2),
                                      (v_copy, 1), (k_copy, 1)):
                    if has(i - behind, NT):
                        stage(i - behind, (u - behind) % 2)

            pipeline(act, NT, step, 3, 2, 6)

        @block.vector
        def _(dve):
            def normalise(t, v):
                if late(t, 2):
                    dve.wait_ge(xt_made, t - 1)
                dve.tensor_scalar(xn[:, v], k.x_res[:, t], k.ln_scale[:, bass.ds(t, 1)], k.ln_shift[:, bass.ds(t, 1)],
                                  ALU.mult, ALU.add).then_inc(xn_ready, 1)

            def rotate(n):
                def stage(t, v):
                    dve.wait_ge(qk_made[n], t + 1)
                    if late(t, 1):
                        dve.wait_ge(qk_t_made[n], t)
                    src = ps_p[:].rearrange("p b (h s d) -> p (b h) s d", s=2, d=HALF)
                    dve.tensor_tensor(rot[n][:].rearrange("p h s d -> p (h s) d"), src.rearrange("p h s d -> p (h s) d"),
                                      bc(k.cos[:], 1, 2 * H1), ALU.mult)
                    dve.tensor_tensor(cross[n][:, :, 0], src[:, :, 1], bc(k.neg_sin[:], 1, H1), ALU.mult)
                    dve.tensor_tensor(cross[n][:, :, 1], src[:, :, 0], bc(k.sin[:], 1, H1), ALU.mult)\
                        .then_inc(crossed[n], 1)
                return stage

            def subtract_max(t, v):
                dve.wait_ge(s_made, t + 1)
                if late(t, 2):
                    dve.wait_ge(pt_made, t - 1)
                    dve.wait_ge(total_ready, t - 1)
                dve.tensor_reduce(mx[:, v], ps_s[:], AX.X, ALU.max).then_inc(mx_ready, 1)
                dve.wait_ge(mx_ready, t + 1)
                dve.tensor_tensor(sd[:, v], ps_s[:], mx[:, v].unsqueeze(2).to_broadcast([P, H1, SEQ]),
                                  ALU.subtract).then_inc(s_taken, 1)

            def add_up(t, v):
                dve.wait_ge(p_ready, t + 1)
                if late(t, 2):
                    dve.wait_ge(rec_ready, t - 1)
                dve.tensor_reduce(total[:, v], sd[:, v], AX.X, ALU.add).then_inc(total_ready, 1)
                dve.wait_ge(total_ready, t + 1)
                if late(t, 2):
                    dve.wait_ge(o_ready, t - 1)
                dve.reciprocal(rec[:, v], total[:, v]).then_inc(rec_ready, 1)

            def divide(t, v):
                dve.wait_ge(o_made, t + 1)
                dve.wait_ge(rec_ready, t + 1)
                if late(t, 2):
                    dve.wait_ge(ot_made, t - 1)
                dve.tensor_tensor(o_sb[:, v], ps_o[:].rearrange("p b (h d) -> p (b h) d", d=D1),
                                  rec[:, v].unsqueeze(2).to_broadcast([P, H1, D1]), ALU.mult).then_inc(o_ready, 1)

            def residual(t, v):
                dve.wait_ge(xb_ready, t + 1)
                dve.wait_ge(y_made, t + 1)
                if late(t, 2):
                    dve.wait_ge(mv_kept, t - 1)
                dve.tensor_tensor(row[:, v], ps_o[:, 0, 0:P], xb[:, v], ALU.add).then_inc(x_added, 1)
                dve.wait_ge(x_added, t + 1)
                keep_with_stats(dve, row[:, v], k.x_res[:, t], st[:, v], mv[:, v], k.mean_var[:, t], t,
                                st_ready, mv_ready, mv_kept)

            def step(i, u):
                for stage, behind in ((rotate(0), 1), (normalise, 0), (subtract_max, 2), (rotate(1), 1),
                                      (add_up, 2), (residual, 3), (divide, 2)):
                    if has(i - behind, NT):
                        stage(i - behind, (u - behind) % 2)

            pipeline(dve, NT, step, 3, 2, 6)


def context_scores(nc, k):
    NT = k.tiles
    NG = NT // GROUP
    with ExitStack() as c:
        def sb(n, shape, dt=F32):
            return c.enter_context(nc.sbuf_tensor(f"cs_{n}", shape, dt))

        new_sem = c.enter_context(stage_semaphores(nc))

        def sem(n):
            return new_sem(f"cs_{n}")

        ROWS = [P, 2, GROUP, P]
        xn, prod, att, e = sb("xn", ROWS), sb("prod", ROWS), sb("att", ROWS), sb("e", ROWS)
        cs = sb("cs", ROWS)
        ctx_t = sb("ctx_t", ROWS)
        COLUMN = [P, 2, GROUP]
        own = sb("own", COLUMN)
        neg_mx, total, rec = sb("neg_mx", COLUMN), sb("total", COLUMN), sb("rec", COLUMN)
        ps_x = [c.enter_context(nc.psum_tensor(f"cs_x{n}", [P, GROUP, P], F32)) for n in range(2)]
        ps_s = [c.enter_context(nc.psum_tensor(f"cs_s{n}", [P, GROUP, P], F32)) for n in range(2)]
        ps_a = [c.enter_context(nc.psum_tensor(f"cs_a{n}", [P, GROUP, P], F32)) for n in range(2)]
        ctx_loaded = [sem(f"ctx_loaded{n}") for n in range(2)]
        xn_ready, prod_ready, own_ready, xt_made = sem("xn_ready"), sem("prod_ready"), sem("own_ready"), sem("xt_made")
        cs_ready, s_made, mx_ready, e_ready = sem("cs_ready"), sem("s_made"), sem("mx_ready"), sem("e_ready")
        rec_ready, att_ready, at_made, at_ready = sem("rec_ready"), sem("att_ready"), sem("at_made"), sem("at_ready")
        max_kept = sem("max_kept")
        nc.scalar.preload_act_table(ACT.Exp)
        block = c.enter_context(nc.Block())

        @block.sync
        def _(sp):
            def step(g, u):
                if late(g, 2):
                    sp.wait_ge(s_made, g - 1)
                sp.dma_start(ctx_t[:, u], k.in_ctx_t[group(g)].rearrange("n p c -> p n c")).then_inc(ctx_loaded[u], 16)

            group_pipeline(sp, NT, step, 0)

        @block.gpsimd
        def _(pool):
            def step(g, u):
                pool.wait_ge(xn_ready, g + 1)
                if late(g, 2):
                    pool.wait_ge(own_ready, g - 1)
                pool.tensor_tensor(prod[:, u], xn[:, u], bc(k.l1_wc[:], 1, GROUP), ALU.mult).then_inc(prod_ready, 1)

            group_pipeline(pool, NT, step, 0)

        @block.tensor
        def _(pe):
            def step(i, u):
                if has(i, NG):
                    pe.wait_ge(xn_ready, i + 1)
                    if late(i, 2):
                        pe.wait_ge(cs_ready, i - 1)
                    for n in range(GROUP):
                        mm = pe.transpose(ps_x[u][:, n], xn[:, u, n], k.ident[:])
                    mm.then_inc(xt_made, 1)
                g, v = i - 3, 1 - u
                if has(g, NG):
                    pe.wait_ge(att_ready, g + 1)
                    if late(g, 2):
                        pe.wait_ge(at_ready, g - 1)
                    for n in range(GROUP):
                        mm = pe.transpose(ps_a[v][:, n], att[:, v, n], k.ident[:])
                    mm.then_inc(at_made, 1)
                g, v = i - 1, 1 - u
                if has(g, NG):
                    pe.wait_ge(cs_ready, g + 1)
                    pe.wait_ge(ctx_loaded[v], 16 + 8 * (g - v))
                    if late(g, 2):
                        pe.wait_ge(e_ready, g - 1)
                    pe.matmul(ps_s[v][:], k.ident_bf[:], bc(k.other_seq[:], 1, GROUP), start=True, stop=True)
                    for n in range(GROUP):
                        mm = pe.matmul(ps_s[v][:, n], cs[:, v, n], ctx_t[:, v, n], start=False, stop=True,
                                       skip_group_check=True)
                    mm.then_inc(s_made, 1)

            group_pipeline(pe, NT, step, 3)

        @block.scalar
        def _(act):
            def step(i, u):
                if has(i, NG):
                    act.wait_ge(xt_made, i + 1)
                    if late(i, 2):
                        act.wait_ge(s_made, i - 1)
                    act.activation(cs[:, u], ps_x[u][:], ACT.Identity, scale=k.l1_wcq[:], bias=k.l1_wq_col[:])\
                        .then_inc(cs_ready, 1)
                g, v = i - 3, 1 - u
                if has(g, NG):
                    act.wait_ge(at_made, g + 1)
                    act.copy(k.at_all[:, group(g)], ps_a[v][:]).then_inc(at_ready, 1)
                g, v = i - 2, u
                if has(g, NG):
                    act.wait_ge(mx_ready, g + 1)
                    if late(g, 2):
                        act.wait_ge(att_ready, g - 1)
                    for n in range(GROUP):
                        op = act.activation(e[:, v, n], ps_s[v][:, n], ACT.Exp, bias=neg_mx[:, v, n:n + 1],
                                            accum_out=total[:, v, n:n + 1])
                    op.then_inc(e_ready, 1)

            group_pipeline(act, NT, step, 3)

        @block.vector
        def _(dve):
            def step(i, u):
                g, v = i - 3, 1 - u
                if has(g, NG):
                    dve.wait_ge(e_ready, g + 1)
                    dve.reciprocal(rec[:, v], total[:, v]).then_inc(rec_ready, 1)
                g, v = i - 2, u
                if has(g, NG):
                    dve.wait_ge(s_made, g + 1)
                    if late(g, 2):
                        dve.wait_ge(max_kept, g - 1)
                    dve.tensor_reduce(neg_mx[:, v], ps_s[v][:], AX.X, ALU.max, negate=True).then_inc(mx_ready, 1)
                if has(i, NG):
                    if late(i, 2):
                        dve.wait_ge(xt_made, i - 1)
                        dve.wait_ge(prod_ready, i - 1)
                    normalise_group(dve, k, i, xn[:, u]).then_inc(xn_ready, 1)
                g, v = i - 3, 1 - u
                if has(g, NG):
                    dve.wait_ge(rec_ready, g + 1)
                    if late(g, 2):
                        dve.wait_ge(at_made, g - 1)
                    dve.tensor_tensor(att[:, v], e[:, v], rec[:, v].unsqueeze(2).to_broadcast([P, GROUP, P]),
                                      ALU.mult).then_inc(att_ready, 1)
                g, v = i - 2, u
                if has(g, NG):
                    dve.wait_ge(prod_ready, g + 1)
                    dve.tensor_reduce(own[:, v], prod[:, v], AX.X, ALU.add).then_inc(own_ready, 1)
                g, v = i - 2, u
                if has(g, NG):
                    dve.wait_ge(mx_ready, g + 1)
                    dve.wait_ge(own_ready, g + 1)
                    dve.scalar_tensor_tensor(out=k.row_max[:, group(g)], in0=own[:, v], scalar=k.l1_b3[:],
                                             in1=neg_mx[:, v], op0=ALU.add, op1=ALU.subtract).then_inc(max_kept, 1)

            group_pipeline(dve, NT, step, 3)


def token_weights(nc, k):
    NT = k.tiles
    with ExitStack() as c:
        def sb(n, shape):
            return c.enter_context(nc.sbuf_tensor(f"tw_{n}", shape, F32))

        new_sem = c.enter_context(stage_semaphores(nc))

        def sem(n):
            return new_sem(f"tw_{n}")

        e = sb("e", [NT, 2, SEQ])
        mx = sb("mx", [NT, 2])
        rec = sb("rec", [NT, 2])
        ps_m = c.enter_context(nc.psum_tensor("tw_m", [P, 512], F32))
        ps_w = c.enter_context(nc.psum_tensor("tw_w", [P, 512], F32))
        m_made, sub_ready, e_ready, w_ready, w_made, op_done = (sem(n) for n in ("m_made", "sub_ready", "e_ready", "w_ready",
                                                                              "w_made", "op_done"))
        block = c.enter_context(nc.Block())

        @block.tensor
        def _(pe):
            pe.transpose(ps_m[0:NT, 0:P], k.row_max[:], k.ident[:]).then_inc(m_made, 1)
            pe.wait_ge(w_ready, 1)
            pe.transpose(ps_w[:, 0:NT], e[:].rearrange("n b s -> n (b s)"), k.ident[0:NT, 0:NT]).then_inc(w_made, 1)

        @block.scalar
        def _(act):
            act.wait_ge(sub_ready, 1)
            act.activation(e[:], e[:], ACT.Exp).then_inc(e_ready, 1)

        @block.vector
        def _(dve):
            rows = ps_m[0:NT, 0:P].rearrange("n (b s) -> n b s", b=2)
            dve.wait_ge(m_made, 1)
            dve.tensor_reduce(mx[:], rows, AX.X, ALU.max).then_inc(op_done, 1)
            dve.wait_ge(op_done, 1)
            dve.tensor_tensor(e[:], rows, mx[:].unsqueeze(2).to_broadcast([NT, 2, SEQ]), ALU.subtract)\
                .then_inc(sub_ready, 1)
            dve.wait_ge(e_ready, 1)
            dve.tensor_reduce(mx[:], e[:], AX.X, ALU.add).then_inc(op_done, 1)
            dve.wait_ge(op_done, 2)
            dve.reciprocal(rec[:], mx[:]).then_inc(op_done, 1)
            dve.wait_ge(op_done, 3)
            dve.tensor_tensor(e[:], e[:], rec[:].unsqueeze(2).to_broadcast([NT, 2, SEQ]), ALU.mult).then_inc(w_ready, 1)
            dve.wait_ge(w_made, 1)
            dve.tensor_copy(k.token_w[:], ps_w[:, 0:NT])


def context_mix(nc, k):
    NT = k.tiles
    NG = NT // GROUP
    with ExitStack() as c:
        def sb(n, shape, dt=F32):
            return c.enter_context(nc.sbuf_tensor(f"cm_{n}", shape, dt))

        new_sem = c.enter_context(stage_semaphores(nc))

        def sem(n):
            return new_sem(f"cm_{n}")

        ROWS = [P, 2, GROUP, P]
        ctx, xn, xb, row = sb("ctx", ROWS), sb("xn", ROWS), sb("xb", ROWS), sb("row", ROWS)
        wb = sb("wb", ROWS)
        feat = sb("feat", [P, 2, 4, GROUP, P])
        st = sb("st", [P, 2, GROUP, 6])
        mv = sb("mv", [P, 2, GROUP, 2])
        ps_x, ps_c, ps_q, ps_z = ([c.enter_context(nc.psum_tensor(f"cm_{q}{n}", [P, GROUP, P], F32)) for n in range(2)]
                                  for q in "xcqz")
        ctx_loaded = [sem(f"ctx_loaded{n}") for n in range(2)]
        xn_ready, wb_ready, xt_made, c_ready = sem("xn_ready"), sem("wb_ready"), sem("xt_made"), sem("c_ready")
        c2q_made, c2q_ready, q2c_made = sem("c2q_made"), sem("c2q_ready"), sem("q2c_made")
        c_c2q_ready, c_q2c_ready, z_made = sem("c_c2q_ready"), sem("c_q2c_ready"), sem("z_made")
        xb_ready, x_added, row_kept = sem("xb_ready"), sem("x_added"), sem("row_kept")
        st_ready, mv_ready, mv_kept = sem("st_ready"), sem("mv_ready"), sem("mv_kept")
        block = c.enter_context(nc.Block())

        @block.sync
        def _(sp):
            def step(g, u):
                if late(g, 2):
                    sp.wait_ge(c2q_made, g - 1)
                sp.dma_start(ctx[:, u], k.in_ctx[group(g)].rearrange("n p c -> p n c")).then_inc(ctx_loaded[u], 16)

            group_pipeline(sp, NT, step, 0)

        @block.gpsimd
        def _(pool):
            def step(i, u):
                if has(i, NG):
                    if late(i, 2):
                        pool.wait_ge(q2c_made, i - 1)
                    pool.tensor_tensor(wb[:, u], bc(k.same_seq[:], 1, GROUP),
                                       k.token_w[:, group(i)].unsqueeze(2).to_broadcast([P, GROUP, P]), ALU.mult)\
                        .then_inc(wb_ready, 1)
                g, v = i - 1, 1 - u
                if has(g, NG):
                    pool.wait_ge(c2q_ready, g + 1)
                    pool.tensor_tensor(feat[:, v, 2], feat[:, v, 1], feat[:, v, 0], ALU.mult).then_inc(c_c2q_ready, 1)
                    if late(g, 2):
                        pool.wait_ge(x_added, g - 1)
                    pool.tensor_tensor(xb[:, v], k.x_res[:, group(g)], bc(k.l1_bl[:], 1, GROUP), ALU.add)\
                        .then_inc(xb_ready, 1)

            group_pipeline(pool, NT, step, 1)

        @block.tensor
        def _(pe):
            def step(i, u):
                if has(i, NG):
                    pe.wait_ge(xn_ready, i + 1)
                    if late(i, 2):
                        pe.wait_ge(c_ready, i - 1)
                    for n in range(GROUP):
                        mm = pe.transpose(ps_x[u][:, n], xn[:, u, n], k.ident[:])
                    mm.then_inc(xt_made, 1)
                    pe.wait_ge(ctx_loaded[u], 16 + 8 * (i - u))
                    if late(i, 2):
                        pe.wait_ge(c2q_ready, i - 1)
                    for n in range(GROUP):
                        mm = pe.matmul(ps_c[u][:, n], ctx[:, u, n], k.at_all[:, i * GROUP + n], start=True, stop=True)
                    mm.then_inc(c2q_made, 1)
                    pe.wait_ge(wb_ready, i + 1)
                    if late(i, 2):
                        pe.wait_ge(c_q2c_ready, i - 1)
                    for n in range(GROUP):
                        mm = pe.matmul(ps_q[u][:, n], xn[:, u, n], wb[:, u, n], start=True, stop=True)
                    mm.then_inc(q2c_made, 1)
                g, v = i - 2, u
                if has(g, NG):
                    pe.wait_ge(c_c2q_ready, g + 1)
                    pe.wait_ge(c_q2c_ready, g + 1)
                    if late(g, 2):
                        pe.wait_ge(x_added, g - 1)
                    for n in range(GROUP):
                        for f in range(4):
                            mm = pe.matmul(ps_z[v][:, n], feat[:, v, f, n], k.l1_wl[:, f], start=(f == 0), stop=(f == 3))
                    mm.then_inc(z_made, 1)

            group_pipeline(pe, NT, step, 2)

        @block.scalar
        def _(act):
            def step(i, u):
                if has(i, NG):
                    act.wait_ge(xt_made, i + 1)
                    if late(i, 2):
                        act.wait_ge(z_made, i - 1)
                    act.copy(feat[:, u, 0], ps_x[u][:]).then_inc(c_ready, 1)
                    act.wait_ge(c2q_made, i + 1)
                    act.copy(feat[:, u, 1], ps_c[u][:]).then_inc(c2q_ready, 1)
                g, v = i - 3, 1 - u
                if has(g, NG):
                    act.wait_ge(x_added, g + 1)
                    act.copy(k.x_res[:, group(g)], row[:, v]).then_inc(row_kept, 1)

            group_pipeline(act, NT, step, 3)

        @block.vector
        def _(dve):
            stats = GroupStats(dve, NT, row, k.mean_var, st, mv, st_ready, mv_ready, mv_kept)

            def step(i, u):
                if has(i, NG):
                    if late(i, 2):
                        dve.wait_ge(q2c_made, i - 1)
                    normalise_group(dve, k, i, xn[:, u]).then_inc(xn_ready, 1)
                g, v = i - 1, 1 - u
                if has(g, NG):
                    dve.wait_ge(c_ready, g + 1)
                    dve.wait_ge(q2c_made, g + 1)
                    if late(g, 2):
                        dve.wait_ge(z_made, g - 1)
                    dve.tensor_tensor(feat[:, v, 3], ps_q[v][:], feat[:, v, 0], ALU.mult).then_inc(c_q2c_ready, 1)
                g, v = i - 3, 1 - u
                if has(g, NG):
                    dve.wait_ge(xb_ready, g + 1)
                    dve.wait_ge(z_made, g + 1)
                    if late(g, 2):
                        dve.wait_ge(row_kept, g - 1)
                    dve.tensor_tensor(row[:, v], ps_z[v][:], xb[:, v], ALU.add).then_inc(x_added, 1)
                stats.keep_and_aggregate(i - 4, u)
                if has(g, NG):
                    dve.wait_ge(x_added, g + 1)
                    stats.by_row(g, v)

            group_pipeline(dve, NT, step, 5)


def one_expert_ffn(nc, k, out_rows):
    NT = k.tiles
    NS = NT + NE - 1
    FF = 4
    with ExitStack() as c:
        def sb(n, shape, dt=F32):
            return c.enter_context(nc.sbuf_tensor(f"m1_{n}", shape, dt))

        new_sem = c.enter_context(stage_semaphores(nc))

        def sem(n):
            return new_sem(f"m1_{n}")

        WIDTH = k.l1_ffn.shape[2]
        from_row = sb("from_row", [P, 4, 1], U32)
        no_shift = sb("no_shift", [P, 1], U32)
        to_row = sb("to_row", [P, 4, 1], U32)
        xg = sb("xg", [P, 4, 2 * P])
        wt = sb("wt", [P, 4, WIDTH])
        xt = sb("xt", [P, 2, P])
        hid = sb("hid", [P, 2, FF, P])
        xb = sb("xb", [P, 4, P])
        y = sb("y", [P, 4, P])
        w1, b1 = wt[:, :, 0:FF * P], wt[:, :, FF * P:FF * P + FF]
        w2 = wt[:, :, FF * P + FF:2 * FF * P + FF].rearrange("p b (f c) -> p b f c", c=P)
        b2 = wt[:, :, 2 * FF * P + FF:WIDTH]
        ps_x = [c.enter_context(nc.psum_tensor(f"m1_x{n}", [P, 512], F32)) for n in range(2)]
        ps_h = [c.enter_context(nc.psum_tensor(f"m1_h{n}", [P, FF, P], F32)) for n in range(2)]
        ps_y = [c.enter_context(nc.psum_tensor(f"m1_y{n}", [P, 512], F32)) for n in range(2)]
        gathered, scattered = k.gathered1, k.scattered1
        setup = sem("setup")
        from_ready, to_ready, wt_ready, xt_made, xt_ready = (sem(n) for n in ("from_ready", "to_ready", "wt_ready", "xt_made", "xt_ready"))
        h_made, hid_ready, y_made, xb_ready, y_ready = (sem(n) for n in ("h_made", "hid_ready", "y_made", "xb_ready",
                                                                          "y_ready"))
        nc.scalar.preload_act_table(ACT.Gelu)
        block = c.enter_context(nc.Block())

        @block.gpsimd
        def _(pool):
            def copy_idx(t, v, of_all, to):
                column = of_all[:, bass.ds(t, 1)] if not isinstance(t, int) else of_all[:, t:t + 1]
                return pool.tensor_tensor(to[:, v], column, no_shift[:], ALU.add)

            pool.memset(no_shift[:], 0).then_inc(setup, 1)
            pool.wait_ge(setup, 1)
            copy_idx(0, 0, k.gather_idx, from_row).then_inc(from_ready, 1)

            def step(i, u):
                g, gv = i + 1, (u + 1) % 4
                s, sv = i - 4, u
                if has(i, NS):
                    pool.wait_ge(from_ready, i + 1)
                    if late(i, 4):
                        pool.wait_ge(xt_made, i - 3)
                if has(i - 5, NS):
                    pool.wait_ge(y_ready, i - 4)
                    pool.wait_ge(to_ready, i - 4)
                if has(g, NS):
                    if late(g, 4):
                        pool.wait_ge(xb_ready, g - 3)
                    copy_idx(g, gv, k.gather_idx, from_row).then_inc(from_ready, 1)
                if has(s, NS):
                    if late(s, 4):
                        pool.wait_ge(scattered[sv], 4 * (s - sv))
                    copy_idx(s, sv, k.scatter_idx, to_row).then_inc(to_ready, 1)
                if has(i, NS):
                    pool.indirect_dma_start(xg[:, u], None, k.xx_rows,
                                            bass.IndirectOffsetOnAxis(ap=from_row[:, u], axis=0)).then_inc(gathered[u], 16)
                if has(i - 5, NS):
                    pool.indirect_dma_start(out_rows, bass.IndirectOffsetOnAxis(ap=to_row[:, (u - 1) % 4], axis=0),
                                            y[:, (u - 1) % 4], None, bounds_check=NT * P - 1, oob_is_err=False)\
                        .then_inc(scattered[(u - 1) % 4], 16)

            pipeline(pool, NS, step, 5)
            for n in range(4):
                pool.wait_ge(scattered[n], 16 * len(range(n, NS, 4)))

        @block.tensor
        def _(pe):
            def step(i, u):
                t, v = i - 2, (u - 2) % 4
                if has(t, NS):
                    pe.wait_ge(gathered[v], 16 + 4 * (t - v))
                    if late(t, 2):
                        pe.wait_ge(xt_ready, t - 1)
                    pe.transpose(ps_x[v % 2][:, 0:P], xg[:, v, P:2 * P], k.ident[:]).then_inc(xt_made, 1)
                t, v = i - 3, (u - 3) % 4
                if has(t, NS):
                    pe.wait_ge(xt_ready, t + 1)
                    pe.wait_ge(wt_ready, t + 1)
                    if late(t, 2):
                        pe.wait_ge(hid_ready, t - 1)
                    for f in range(FF):
                        mm = pe.matmul(ps_h[v % 2][:, f], w1[:, v, f * P:(f + 1) * P], xt[:, v % 2], start=True, stop=True)
                    mm.then_inc(h_made, 1)
                t, v = i - 4, u
                if has(t, NS):
                    pe.wait_ge(hid_ready, t + 1)
                    if late(t, 2):
                        pe.wait_ge(y_ready, t - 1)
                    for f in range(FF):
                        mm = pe.matmul(ps_y[v % 2][:, 0:P], hid[:, v % 2, f], w2[:, v, f], start=(f == 0), stop=(f == FF - 1))
                    mm.then_inc(y_made, 1)

            pipeline(pe, NS, step, 4)

        @block.scalar
        def _(act):
            def step(i, u):
                t, v = i - 2, (u - 2) % 4
                if has(t, NS):
                    act.wait_ge(xt_made, t + 1)
                    if late(t, 2):
                        act.wait_ge(h_made, t - 1)
                    act.copy(xt[:, v % 2], ps_x[v % 2][:, 0:P]).then_inc(xt_ready, 1)
                t, v = i - 3, (u - 3) % 4
                if has(t, NS):
                    act.wait_ge(h_made, t + 1)
                    if late(t, 2):
                        act.wait_ge(y_made, t - 1)
                    for f in range(FF):
                        op = act.activation(hid[:, v % 2, f], ps_h[v % 2][:, f], ACT.Gelu, bias=b1[:, v, f:f + 1])
                    op.then_inc(hid_ready, 1)

            pipeline(act, NS, step, 3)

        @block.vector
        def _(dve):
            def step(i, u):
                t, v = i - 2, (u - 2) % 4
                if has(t, NS):
                    if late(t, 4):
                        dve.wait_ge(y_ready, t - 3)
                        dve.wait_ge(hid_ready, t - 3)
                        dve.wait_ge(y_made, t - 3)
                    expert = dve.value_load(k.tile_expert[0:1, bass.ds(t, 1)], min_val=0, max_val=NE - 1)
                    dve.tensor_scalar(wt[:, v], k.l1_ffn[:, expert], 1.0, None, ALU.mult).then_inc(wt_ready, 1)
                    dve.wait_ge(wt_ready, t + 1)
                    dve.wait_ge(gathered[v], 16 + 4 * (t - v))
                    dve.tensor_tensor(xb[:, v], xg[:, v, 0:P], b2[:, v], ALU.add).then_inc(xb_ready, 1)
                t, v = i - 4, u
                if has(t, NS):
                    dve.wait_ge(xb_ready, t + 1)
                    if late(t, 4):
                        dve.wait_ge(scattered[v], 4 * (t - v))
                    dve.wait_ge(y_made, t + 1)
                    dve.tensor_tensor(y[:, v], ps_y[v % 2][:, 0:P], xb[:, v], ALU.add).then_inc(y_ready, 1)

            pipeline(dve, NS, step, 4)


def load(nc, k, name):
    with ExitStack() as c:
        loaded = c.enter_context(stage_semaphores(nc))(f"{name}_loaded")
        block = c.enter_context(nc.Block())

        @block.sync
        def _(sp):
            for tile, src in k.loads:
                sp.dma_start(tile, src).then_inc(loaded, 16)
            sp.wait_ge(loaded, 16 * len(k.loads))
    k.loads = []


def route_constants(nc, k, a, rm, slots):
    NT = k.tiles
    k.logits = rm("logits", [P, NT, NE])
    k.iota_e = rm("iota_e", [P, NE], src=a["iota"][:, 0:NE].to_broadcast([P, NE]))
    k.iota_cap = rm("iota_cap", [P, NE], src=a["iota_cap"].to_broadcast([P, NE]))
    k.iota_s = rm("iota_s", [P, P], src=a["iota"][:, 0:P].to_broadcast([P, P]))
    k.iota_s1 = rm("iota_s1", [P, NT], src=a["iota"][:, 1:NT + 1].to_broadcast([P, NT]))
    k.iota_p = k.iota_s
    k.place = rm("place", [P, 1], src=a["place"])
    k.empty_id = rm("empty_id", [P, slots], src=a["empty_id"][:, 0:slots])
    k.before = rm("before", [P, P], BF16, src=a["before"])
    k.ones_bf = rm("ones_bf", [P, P], BF16, src=a["ones_bf"])
    k.gather_idx = rm("gather_idx", [P, slots], U32)
    k.scatter_idx = rm("scatter_idx", [P, slots], U32)


def build(nc, a):
    NT = a["x"].shape[0]
    k = Kept(NT)
    with ExitStack() as outer:
        k.loads = []
        new_sem = outer.enter_context(stage_semaphores(nc))
        k.gathered0 = [new_sem(f"gathered0_{n}") for n in range(NE * CAP // P)]
        k.added0 = [new_sem(f"added0_{e}") for e in range(NE)]
        k.gathered1 = [new_sem(f"gathered1_{n}") for n in range(4)]
        k.scattered1 = [new_sem(f"scattered1_{n}") for n in range(4)]

        def res(n, shape, dt=F32, src=None, stack=outer):
            t = stack.enter_context(nc.sbuf_tensor(n, shape, dt))
            if src is not None:
                k.loads.append((t[:], src))
            return t

        def rows(n):
            return a[n].to_broadcast([P, a[n].shape[1]])

        k.in_x, k.in_mask, k.in_ctx_t, k.in_dist, k.in_dd = a["x"], a["mask"], a["ctx_t"], a["dist"], a["dd"]
        k.x_dram, k.xn_dram = a["x_dram"], a["xn_dram"]
        k.in_ctx, k.xx_dram = a["ctx"], a["xx_dram"]
        k.xx_rows = k.xx_dram.rearrange("n p c -> (n p) c")
        k.x_rows = k.x_dram.rearrange("n p c -> (n p) c")
        k.xn_rows = k.xn_dram.rearrange("n p c -> (n p) c")
        k.x_res = res("x_res", [P, NT, P])
        k.mean_var = res("mean_var", [P, NT, 2])
        k.ln_scale = res("ln_scale", [P, NT])
        k.ln_shift = res("ln_shift", [P, NT])
        k.ident = res("ident", [P, P], src=a["ident"])
        k.ident_bf = res("ident_bf", [P, P], BF16, src=a["ident_bf"])
        k.causal = res("causal", [P, SEQ], BF16, src=a["causal"])
        with ExitStack() as layer0:
            def r0(n, shape, dt=F32, src=None):
                return res(n, shape, dt, src, layer0)
            k.head_mask = r0("head_mask", [P, GRP, 1], src=a["head_mask"])
            k.group_mask = r0("group_mask", [P, GRP, 1], src=a["group_mask"])
            k.a_wq, k.a_wk, k.a_wv, k.a_wo, k.x_wq, k.x_wk, k.x_wv, k.x_wo = (
                r0(n, [P, P], src=a[n]) for n in ("a_wq", "a_wk", "a_wv", "a_wo", "x_wq", "x_wk", "x_wv", "x_wo"))
            k.a_bq, k.a_bk, k.a_bv, k.x_bq, k.x_bk, k.x_ln_g, k.x_ln_b = (
                r0(n, [P, 1], src=a[n]) for n in ("a_bq", "a_bk", "a_bv", "x_bq", "x_bk", "x_ln_g", "x_ln_b"))
            k.a_bo = r0("a_bo_rows", [P, P], src=rows("a_bo"))
            k.x_bo = r0("x_bo_rows", [P, P], src=rows("x_bo"))
            k.x_bv_rows = r0("x_bv_rows", [P, P], src=rows("x_bv"))
            k.decay = r0("decay", [P, SEQ])
            k.mask_all = r0("mask_all", [P, NT, SEQ], BF16)
            set_up(nc, k)
            k.loads = []
            layer_norm_scales(nc, k, k.mean_var, k.ln_scale[:], k.ln_shift[:], "ln0")
            small_head_attention(nc, k, "sa", cross=False)
            with ExitStack() as cross:
                k.o_all = res("o_all", [P, NT, P], stack=cross)
                k.o_mean_var = res("o_mean_var", [P, NT, 2], stack=cross)
                k.o_scale = res("o_scale", [P, NT], stack=cross)
                k.o_shift = res("o_shift", [P, NT], stack=cross)
                layer_norm_scales(nc, k, k.mean_var, k.ln_scale[:], k.ln_shift[:], "ln1")
                small_head_attention(nc, k, "ca", cross=True)
                layer_norm_scales(nc, k, k.o_mean_var, k.o_scale[:], k.o_shift[:], "lno")
                project_cross(nc, k)
        with ExitStack() as moe0:
            layer_norm_scales(nc, k, k.mean_var, k.ln_scale[:], k.ln_shift[:], "ln2")

            def rm(n, shape, dt=F32, src=None):
                return res(f"moe0_{n}", shape, dt, src, moe0)

            route_constants(nc, k, a, rm, NE * CAP // P)
            rw = rm("f0_rw", [P, NE], src=a["f0_rw"])
            rb = rm("f0_rb", [P, NE], src=rows("f0_rb"))
            k.f0_w = rm("f0_w", [P, NE, 2 * P], src=a["f0_w"])
            k.f0_v = rm("f0_v", [P, NE, 2 * P], src=a["f0_v"])
            k.f0_out = rm("f0_out", [P, NE, 2, P], src=a["f0_out"])
            k.w_slot = rm("w_slot", [P, NE * CAP // P])
            load(nc, k, "ld2")
            router(nc, k, "r0", rw, rb, k.xn_dram, None)
            chosen_slots(nc, k, "c0", 2, NE * CAP // P, k.w_slot)
            two_expert_ffn(nc, k)
        with ExitStack() as wide:
            layer_norm_scales(nc, k, k.mean_var, k.ln_scale[:], k.ln_shift[:], "ln3")

            def rw1(n, shape, dt=F32, src=None):
                return res(n, shape, dt, src, wide)

            k.l1_wq = rw1("l1_wq", [P, H1 * D1], src=a["l1_wq"])
            k.l1_wk = rw1("l1_wk", [P, H1 * D1], src=a["l1_wk"])
            k.l1_wv = rw1("l1_wv", [P, 2, PAIRS * D1], src=a["l1_wv"])
            k.l1_wo = rw1("l1_wo", [P, PAIRS, P], src=a["l1_wo"])
            k.l1_bo = rw1("l1_bo", [P, P], src=rows("l1_bo"))
            k.cos = rw1("cos", [P, D1 // 2], src=a["cos"])
            k.sin = rw1("sin", [P, D1 // 2], src=a["sin"])
            k.neg_sin = rw1("neg_sin", [P, D1 // 2], src=a["neg_sin"])
            load(nc, k, "ld3")
            wide_head_attention(nc, k)
        with ExitStack() as context:
            layer_norm_scales(nc, k, k.mean_var, k.ln_scale[:], k.ln_shift[:], "ln4")

            def rc(n, shape, dt=F32, src=None):
                return res(n, shape, dt, src, context)

            k.l1_wcq = rc("l1_wcq", [P, 1], src=a["l1_wcq"])
            k.l1_wq_col = rc("l1_w_q", [P, 1], src=a["l1_w_q"])
            k.l1_wc = rc("l1_wc", [P, P], src=rows("l1_wc"))
            k.l1_b3 = rc("l1_b3", [P, 1])
            b3 = rc("l1_b3_parts", [P, 3])
            for n, part in enumerate(("l1_b_cq", "l1_b_c", "l1_b_q")):
                k.loads.append((b3[:, n:n + 1], rows(part)))
            k.l1_wl = rc("l1_wl", [P, 4, P], src=a["l1_wl"])
            k.l1_bl = rc("l1_bl", [P, P], src=rows("l1_bl"))
            k.same_seq = rc("same_seq", [P, P], src=a["same_seq"])
            k.other_seq = rc("other_seq", [P, P], BF16, src=a["other_seq"])
            k.at_all = rc("at_all", [P, NT, P])
            k.row_max = rc("row_max", [P, NT])
            k.token_w = rc("token_w", [P, NT])
            load(nc, k, "ld4")
            with nc.Block() as block:
                @block.vector
                def _(dve):
                    dve.tensor_reduce(k.l1_b3[:], b3[:], AX.X, ALU.add)
            context_scores(nc, k)
            token_weights(nc, k)
            context_mix(nc, k)
        with ExitStack() as moe1:
            layer_norm_scales(nc, k, k.mean_var, k.ln_scale[:], k.ln_shift[:], "ln5")

            def rm1(n, shape, dt=F32, src=None):
                return res(f"moe1_{n}", shape, dt, src, moe1)

            slots = NT + NE - 1
            FF = a["f1_w1"].shape[2]
            route_constants(nc, k, a, rm1, slots)
            rw = rm1("f1_rw", [P, NE], src=a["f1_rw"])
            rb = rm1("f1_rb", [P, NE], src=rows("f1_rb"))
            k.tile_expert = rm1("tile_expert", [P, slots], I32)
            k.l1_ffn = rm1("l1_ffn", [P, NE, 2 * FF + FF // P + P])
            at = 0
            for n in ("f1_w1", "f1_b1", "f1_w2", "f1_b2"):
                w = a[n].shape[-1]
                k.loads.append((k.l1_ffn[:, :, at:at + w], bc(a[n], 0, P) if n == "f1_b2" else a[n]))
                at += w
            load(nc, k, "ld5")
            router(nc, k, "r1", rw, rb, k.xx_dram[:, :, P:2 * P], k.xx_dram[:, :, 0:P])
            chosen_slots(nc, k, "c1", 1, slots, None)
            one_expert_ffn(nc, k, a["out"].rearrange("n p c -> (n p) c"))


def _layout(v):
    c, f, bf = np.ascontiguousarray, np.float32, mybir.dt.np(BF16)
    B = v["x"].shape[0]
    NT = B * SEQ // P
    i, s = np.arange(P), np.arange(SEQ)
    same = (i // SEQ)[:, None] == (i // SEQ)[None]
    o = {}
    o["dist"] = np.abs((i % SEQ)[:, None] - s[None]).astype(f)
    o["ident"] = np.eye(P, dtype=f)
    o["ident_bf"] = np.eye(P).astype(bf)
    o["causal"] = np.where(s[None] <= (i % SEQ)[:, None], 0, NEG).astype(bf)
    o["head_mask"] = ((i // D0) % GRP == np.arange(GRP)[:, None]).T.astype(f)[:, :, None]
    o["group_mask"] = (i // (GRP * D0) == np.arange(GRP)[:, None]).T.astype(f)[:, :, None]
    o["iota"] = np.arange(256, dtype=f).reshape(1, 256)
    o["iota_cap"] = (CAP * np.arange(NE) + 1).astype(f).reshape(1, NE)
    o["place"] = i.astype(f).reshape(P, 1)
    o["empty_id"] = (P + NT * P + i[:, None] + P * np.arange(NT + NE)[None]).astype(f)
    o["before"] = (i[:, None] < i[None]).astype(bf)
    o["ones_bf"] = np.ones((P, P), bf)
    o["same_seq"] = same.astype(f)
    o["other_seq"] = np.where(same, 0, NEG).astype(bf)
    freq = (f(1.0) / f(10000.0) ** (np.arange(0, D1, 2, dtype=f) / f(D1))).astype(f)
    angle = (i % SEQ).astype(f)[:, None] * freq[None]
    o["cos"], o["sin"] = np.cos(angle).astype(f), np.sin(angle).astype(f)
    o["neg_sin"] = -o["sin"]
    o["x"] = v["x"].reshape(NT, P, P)
    o["mask"] = v["mask_BxSxS2_ik1"].reshape(NT, P, SEQ)
    o["ctx"] = v["ctx_1024"].reshape(NT, P, P)
    o["ctx_t"] = o["ctx"].transpose(0, 2, 1)
    W, b = v["L0_attn_Wqkv_w"], v["L0_attn_Wqkv_b"]
    for n, q in enumerate("qkv"):
        o["a_w" + q], o["a_b" + q] = W[n * P:(n + 1) * P].T, b[n * P:(n + 1) * P].reshape(P, 1)
    o["dd"] = v["L0_attn_distance_decay"].reshape(1, 1)
    o["a_wo"], o["a_bo"] = v["L0_attn_out_w"].T, v["L0_attn_out_b"].reshape(1, P)

    def repeated(w):
        return np.repeat(w.reshape(H0 // GRP, 1, D0, -1), GRP, axis=1).reshape(P, -1)

    o["x_wq"], o["x_bq"] = v["L0_xattn_Wq"].T, v["L0_xattn_bq"].reshape(P, 1)
    o["x_wk"], o["x_bk"] = repeated(v["L0_xattn_Wk"]).T, repeated(v["L0_xattn_bk"])
    o["x_wv"], o["x_bv"] = repeated(v["L0_xattn_Wv"]).T, repeated(v["L0_xattn_bv"]).reshape(1, P)
    o["x_wo"], o["x_bo"] = v["L0_xattn_Wo"].T, v["L0_xattn_bo"].reshape(1, P)
    o["x_ln_g"], o["x_ln_b"] = v["L0_xattn_ln_g"].reshape(P, 1), v["L0_xattn_ln_b"].reshape(P, 1)
    o["f0_rw"], o["f0_rb"] = v["L0_ffn_router_w"].T, v["L0_ffn_router_b"].reshape(1, NE)
    o["f0_w"], o["f0_v"] = v["L0_ffn_W"].transpose(1, 0, 2), v["L0_ffn_V"].transpose(1, 0, 2)
    o["f0_out"] = v["L0_ffn_W_out"].reshape(NE, 2, P, P).transpose(2, 0, 1, 3)
    halves = np.concatenate([np.arange(0, D1, 2), np.arange(1, D1, 2)])
    for q in "qk":
        o["l1_w" + q] = v["L1_attn_W" + q].reshape(P, H1, D1)[:, :, halves].reshape(P, H1 * D1)
    o["l1_wv"] = v["L1_attn_Wv"].reshape(P, PAIRS, 2, D1).transpose(0, 2, 1, 3).reshape(P, 2, PAIRS * D1)
    o["l1_wo"] = v["L1_attn_Wo"].reshape(PAIRS, P, P).transpose(1, 0, 2)
    o["l1_bo"] = v["L1_attn_bo"].reshape(1, P)
    o["l1_wcq"], o["l1_w_q"] = v["L1_xattn_w_cq"].reshape(P, 1), v["L1_xattn_w_q"].reshape(P, 1)
    o["l1_wc"] = v["L1_xattn_w_c"].reshape(1, P)
    for n in ("b_cq", "b_c", "b_q"):
        o["l1_" + n] = v["L1_xattn_" + n].reshape(1, 1)
    o["l1_wl"] = v["L1_xattn_W_l"].T.reshape(4, P, P).transpose(1, 0, 2)
    o["l1_bl"] = v["L1_xattn_b_l"].reshape(1, P)
    o["f1_rw"], o["f1_rb"] = v["L1_ffn_wr"], v["L1_ffn_br"].reshape(1, NE)
    o["f1_w1"] = v["L1_ffn_w1"].transpose(1, 0, 2)
    o["f1_b1"] = v["L1_ffn_b1"].reshape(NE, -1, P).transpose(2, 0, 1)
    o["f1_w2"] = v["L1_ffn_w2"].reshape(NE, -1, P, P).transpose(2, 0, 1, 3).reshape(P, NE, -1)
    o["f1_b2"] = v["L1_ffn_b2"]
    return {n: c(x) for n, x in o.items()}


def kernel(**inputs):
    import numpy as _np
    import concourse.bacc as _bacc
    from concourse import mybir as _mybir
    from concourse.bass_utils import run_bass_kernel_spmd as _run

    nc = _bacc.Bacc("TRN2", target_bir_lowering=False, num_devices=1)
    tensors = _layout({n: _np.asarray(x) for n, x in inputs.items()})
    arrays, a = {}, {}
    for n, x in tensors.items():
        x = _np.ascontiguousarray(x)
        arrays[f"in_{n}_dram"] = x
        a[n] = nc.dram_tensor(f"in_{n}_dram", x.shape, _mybir.dt.from_np(x.dtype), kind="ExternalInput").ap()
    NT = a["x"].shape[0]
    a["out"] = nc.dram_tensor("out_0_dram", [NT, P, P], F32, kind="ExternalOutput").ap()
    a["x_dram"] = nc.dram_tensor("x_dram", [NT + NE * CAP // P, P, P], F32).ap()
    a["xn_dram"] = nc.dram_tensor("xn_dram", [NT, P, P], F32).ap()
    a["xx_dram"] = nc.dram_tensor("xx_dram", [NT, P, 2 * P], F32).ap()
    build(nc, a)
    r = _run(nc, [arrays], core_ids=[0])
    return r.results[0]["out_0_dram"].reshape(inputs["x"].shape)
```

```python
from contextlib import ExitStack, contextmanager

import numpy as np

import concourse.bass as bass
from concourse import mybir

F32 = mybir.dt.float32
BF16 = mybir.dt.bfloat16
I32 = mybir.dt.int32
U32 = mybir.dt.uint32
ALU = mybir.AluOpType
ACT = mybir.ActivationFunctionType
AX = mybir.AxisListType

P = 128
SEQ = 64
LN_EPS = 1e-5
RSQRT_BITS = float(0x5F3759DF)
NEG = -1e30

H0, D0 = 16, 8
GRP = 4
H1, D1 = 16, 64
NE = 8
CAP = 256
PAIRS = 8
UNROLL = 4
GROUP = 4
PEEL = 8


class Kept:

    def __init__(self, tiles):
        self.tiles = tiles


@contextmanager
def stage_semaphores(nc):
    made = []

    def new(name):
        made.append(nc.alloc_semaphore(name))
        return made[-1]

    yield new
    numbers = sorted(s.num for s in made)
    while numbers:
        n = next((n for n in range(1, len(numbers)) if numbers[n] != numbers[0] + n), len(numbers))
        nc.gpsimd.sem_clear(range(numbers[0], numbers[0] + n))
        numbers = numbers[n:]
    for s in made:
        nc.release_semaphore(s)


def pipeline(eng, tiles, step, lag, unroll=UNROLL, peel=PEEL):
    body = (tiles - peel) // unroll
    for i in range(peel):
        step(i, i % unroll)
    with eng.Fori(0, body) as j:
        for u in range(unroll):
            step(j * unroll + (peel + u), u)
    for i in range(peel + body * unroll, tiles + lag):
        step(i, i % unroll)


def late(t, n):
    return not isinstance(t, int) or t >= n


def has(t, tiles):
    return not isinstance(t, int) or 0 <= t < tiles


def bc(ap, axis, n):
    return ap.unsqueeze(axis).to_broadcast([*ap.shape[:axis], n, *ap.shape[axis:]])


def keep_with_stats(dve, row, kept, st, mv, kept_mv, t, st_ready, mv_ready, mv_kept):
    dve.bn_stats(st, row).then_inc(st_ready, 1)
    dve.wait_ge(st_ready, t + 1)
    dve.tensor_scalar(kept, row, 1.0, None, ALU.mult)
    dve.bn_aggr(mv, st).then_inc(mv_ready, 1)
    dve.wait_ge(mv_ready, t + 1)
    dve.tensor_scalar(kept_mv, mv, 1.0, None, ALU.mult).then_inc(mv_kept, 1)


def group_pipeline(eng, tiles, step, lag):
    pipeline(eng, tiles // GROUP, step, lag, 2, 6)


def group(g):
    return bass.ds(g * GROUP, GROUP)


class LoadedStats:

    def __init__(self, dve, k, st, sems, half, loaded):
        self.dve, self.k, self.st, self.loaded = dve, k, st, loaded
        self.st_ready, self.mv_ready, self.newton = sems
        self.count = k.tiles // GROUP // 2
        self.first = half * self.count

    def step(self, n):
        dve, k = self.dve, self.k
        if n < self.count:
            dve.wait_ge(k.x_loaded[self.first + n], self.loaded)
            if n >= 2:
                dve.wait_ge(self.mv_ready, n - 1)
            for m in range(GROUP):
                op = dve.bn_stats(self.st[:, n % 2, m], k.x_res[:, (self.first + n) * GROUP + m])
            op.then_inc(self.st_ready, 1)
        if n:
            dve.wait_ge(self.st_ready, n)
            for m in range(GROUP):
                op = dve.bn_aggr(k.mean_var[:, (self.first + n - 1) * GROUP + m], self.st[:, (n - 1) % 2, m])
            op.then_inc(self.mv_ready, 1)
        if n == self.count:
            tiles = slice(self.first * GROUP, (self.first + self.count) * GROUP)
            dve.wait_ge(self.mv_ready, self.count)
            layer_norm_scales(dve, k, k.mean_var[:, tiles], k.ln_scale[:, tiles], k.ln_shift[:, tiles], self.newton)


def normalise_group(dve, k, g, to):
    for n in range(GROUP):
        t = g * GROUP + n
        op = dve.tensor_scalar(to[:, n], k.x_res[:, t], k.ln_scale[:, bass.ds(t, 1)], k.ln_shift[:, bass.ds(t, 1)],
                               ALU.mult, ALU.add)
    return op


class GroupStats:

    def __init__(self, dve, tiles, row, all_stats, st, mv, st_ready, mv_ready, mv_kept):
        self.dve, self.groups, self.row, self.all_stats, self.st, self.mv = dve, tiles // GROUP, row, all_stats, st, mv
        self.st_ready, self.mv_ready, self.mv_kept = st_ready, mv_ready, mv_kept

    def by_row(self, g, v):
        for n in range(GROUP):
            op = self.dve.bn_stats(self.st[:, v, n], self.row[:, v, n])
        op.then_inc(self.st_ready, 1)

    def keep_and_aggregate(self, made, v):
        kept = made - 1
        if has(made, self.groups):
            self.dve.wait_ge(self.st_ready, made + 1)
            if late(made, 2):
                self.dve.wait_ge(self.mv_kept, made - 1)
        if has(kept, self.groups):
            self.dve.wait_ge(self.mv_ready, kept + 1)
            self.dve.tensor_scalar(self.all_stats[:, group(kept)], self.mv[:, 1 - v], 1.0, None, ALU.mult)\
                .then_inc(self.mv_kept, 1)
        if has(made, self.groups):
            for n in range(GROUP):
                op = self.dve.bn_aggr(self.mv[:, v, n], self.st[:, v, n])
            op.then_inc(self.mv_ready, 1)


def layer_norm_scales(dve, k, mean_var, scale, shift, newton):
    tiles = mean_var.shape[1]
    ve, square = k.ln_var[:, 0:tiles], k.ln_square[:, 0:tiles]
    count = [0]

    def op(instruction):
        count[0] += 1
        instruction.then_inc(newton, 1)
        dve.wait_ge(newton, count[0])

    op(dve.tensor_scalar(ve, mean_var[:, :, 1], LN_EPS, None, ALU.add))
    op(dve.tensor_scalar(scale.bitcast(I32), ve.bitcast(I32), -0.5, RSQRT_BITS, ALU.mult, ALU.add))
    for _ in range(3):
        op(dve.tensor_tensor(square, scale, scale, ALU.mult))
        op(dve.scalar_tensor_tensor(out=square, in0=square, scalar=-0.5, in1=ve, op0=ALU.mult, op1=ALU.mult))
        op(dve.scalar_tensor_tensor(out=scale, in0=square, scalar=1.5, in1=scale, op0=ALU.add, op1=ALU.mult))
    op(dve.scalar_tensor_tensor(out=shift, in0=mean_var[:, :, 0], scalar=-1.0, in1=scale, op0=ALU.mult, op1=ALU.mult))


def small_head_attention(nc, k, name, cross):
    NT = k.tiles
    scale = float(1.0 / np.sqrt(D0))
    wq, wk, wv, bq, bk, bv = ((k.x_wq, k.x_wk, k.x_wv, k.x_bq, k.x_bk, k.x_bv_rows) if cross else
                              (k.a_wq, k.a_wk, k.a_wv, k.a_bq, k.a_bk, k.a_bv))
    with ExitStack() as c:
        def sb(n, shape, dt=F32):
            return c.enter_context(nc.sbuf_tensor(f"{name}_{n}", shape, dt))

        def ps(n, shape):
            return c.enter_context(nc.psum_tensor(f"{name}_{n}", shape, F32))

        new_sem = c.enter_context(stage_semaphores(nc))

        def sem(n):
            return new_sem(f"{name}_{n}")

        xn = sb("xn", [P, 2, P])
        xt = sb("xt", [P, 2, P])
        q_sb = sb("q", [P, 2, P])
        k_sb = sb("k", [P, 2, P])
        qm = sb("qm", [P, 2, GRP, P])
        km = sb("km", [P, 2, GRP, P])
        vbd = sb("vbd", [P, 4, 2, PAIRS, 2, D0 + 1])
        sd = sb("sd", [P, 4, H0, SEQ])
        mx = sb("mx", [P, 4, H0])
        pt = sb("pt", [P, 2, PAIRS, P])
        rec = sb("rec", [P, 2, H0])
        o_sb = sb("o", [P, 2, H0, D0])
        ctx_t = sb("ctx_t", [P, 4, P]) if cross else None
        ot_sb = sb("ot", [P, 2, P])
        xb = sb("xb", [P, 2, P])
        row = sb("row", [P, 2, P])
        st = sb("st", [P, 2, 6])
        rest_st = sb("rest_st", [P, 2, GROUP, 6])
        mv = sb("mv", [P, 2, 2])

        ps_xt = ps("ps_xt", [P, 512])
        ps_qkv = ps("ps_qkv", [P, 4, P])
        ps_s = ps("ps_s", [P, H0, SEQ])
        ps_pt = ps("ps_pt", [P, PAIRS, P])
        ps_o = ps("ps_o", [P, 512])
        ps_y = ps("ps_y", [P, 512])
        o_ps = ps_o[:, 0:H0 * (D0 + 1)].rearrange("p (h d) -> p h d", d=D0 + 1)
        ot_ps, y_ps = ps_y[:, 0:P], ps_y[:, P:2 * P]

        newton = sem("newton")
        rest_sums, rest_ready, rest_newton = sem("rest_sums"), sem("rest_ready"), sem("rest_newton")
        setup = sem("setup")
        mask_loaded, later_loaded = sem("mask_loaded"), sem("later_loaded")
        ctx_loaded = [sem(f"ctx_loaded{n}") for n in range(4)]
        xn_ready = sem("xn_ready")
        xt_made = sem("xt_made")
        xt_ready = sem("xt_ready")
        qkv_made = sem("qkv_made")
        qkv_ready = sem("qkv_ready")
        masked = sem("masked")
        s_made = sem("s_made")
        s_taken = sem("s_taken")
        mx_ready = sem("mx_ready")
        sub_ready = sem("sub_ready")
        p_ready = sem("p_ready")
        pt_made = sem("pt_made")
        pt_ready = sem("pt_ready")
        o_made = sem("o_made")
        rec_ready = sem("rec_ready")
        o_ready = sem("o_ready")
        ot_made = sem("ot_made")
        ot_ready = sem("ot_ready")
        y_made = sem("y_made")
        xb_ready = sem("xb_ready")
        x_added = sem("x_added")
        st_ready = sem("st_ready")
        mv_ready = sem("mv_ready")
        mv_kept = sem("mv_kept")

        nc.scalar.preload_act_table(ACT.Exp)
        block = c.enter_context(nc.Block())

        @block.sync
        def _(sp):
            if not cross:
                sp.dma_start(k.mask_in[:], k.in_mask.rearrange("n p s -> p n s")).then_inc(mask_loaded, 16)
                issue_loads(sp, k.later_loads, later_loaded)
                sp.wait_ge(later_loaded, 16 * len(k.later_loads))
                return

            def load_ctx(t, u):
                if late(t, 4):
                    sp.wait_ge(qkv_made, t - 3)
                sp.dma_start(ctx_t[:, u, :], k.in_ctx_t[t]).then_inc(ctx_loaded[u], 16)

            pipeline(sp, NT, load_ctx, 0)

        @block.gpsimd
        def _(pool):
            pool.memset(vbd[:], 0.0).then_inc(setup, 1)
            pool.wait_ge(setup, 1)
            pool.memset(vbd[0:SEQ, :, :, :, 0, D0:D0 + 1], 1.0)
            pool.memset(vbd[SEQ:P, :, :, :, 1, D0:D0 + 1], 1.0).then_inc(setup, 1)

            def subtract_max(t, v):
                pool.wait_ge(mx_ready, t + 1)
                pool.tensor_tensor(sd[:, v], sd[:, v], mx[:, v].unsqueeze(2).to_broadcast([P, H0, SEQ]),
                                   ALU.subtract).then_inc(sub_ready, 1)

            def split_heads(t, v):
                pool.wait_ge(qkv_ready, t + 1)
                if late(t, 2):
                    pool.wait_ge(s_made, t - 1)
                pool.tensor_tensor(km[:, v % 2], bc(k_sb[:, v % 2], 1, GRP), k.head_mask[:].to_broadcast([P, GRP, P]),
                                   ALU.mult)
                pool.tensor_tensor(qm[:, v % 2], bc(q_sb[:, v % 2], 1, GRP), k.group_mask[:].to_broadcast([P, GRP, P]),
                                   ALU.mult).then_inc(masked, 1)

            def add_bias(t, v):
                if cross:
                    pool.wait_ge(o_ready, t + 1)
                    if late(t, 2):
                        pool.wait_ge(mv_kept, t - 1)
                    pool.tensor_tensor(row[:, v % 2], o_sb[:, v % 2].rearrange("p h d -> p (h d)"), bv[:],
                                       ALU.add).then_inc(xb_ready, 1)
                else:
                    if late(t, 2):
                        pool.wait_ge(x_added, t - 1)
                    pool.tensor_tensor(xb[:, v % 2], k.x_res[:, t], k.a_bo[:], ALU.add).then_inc(xb_ready, 1)

            def step(i, u):
                for stage, behind in ((subtract_max, 4), (split_heads, 2), (add_bias, 6)):
                    if has(i - behind, NT):
                        stage(i - behind, (u - behind) % UNROLL)

            pipeline(pool, NT, step, 6, UNROLL, 3 * UNROLL)

        @block.tensor
        def _(pe):
            pe.wait_ge(setup, 2)

            def x_transpose(t, v):
                pe.wait_ge(xn_ready, t + 1)
                if late(t, 1):
                    pe.wait_ge(xt_ready, t)
                pe.transpose(ps_xt[:, 0:P], xn[:, v % 2], k.ident[:]).then_inc(xt_made, 1)

            def project(t, v):
                pe.wait_ge(xt_ready, t + 1)
                if late(t, 1):
                    pe.wait_ge(qkv_ready, t)
                if cross:
                    pe.wait_ge(ctx_loaded[v], 16 + 4 * (t - v))
                kv = ctx_t[:, v] if cross else xt[:, v % 2]
                pe.matmul(ps_qkv[:, 0], wq[:], xt[:, v % 2], start=True, stop=True)
                pe.matmul(ps_qkv[:, 1], wk[:], kv, start=True, stop=True)
                for b in range(2):
                    for half in range(2):
                        mm = pe.matmul(ps_qkv[half * SEQ:(half + 1) * SEQ, 2 + b], kv[:, b * SEQ:(b + 1) * SEQ],
                                       wv[:], start=True, stop=True)
                mm.then_inc(qkv_made, 1)

            def scores(t, v):
                pe.wait_ge(masked, t + 1)
                if late(t, 1):
                    pe.wait_ge(s_taken, t)
                for g in range(GRP):
                    for b in range(2):
                        rows = slice(b * SEQ, (b + 1) * SEQ)
                        mm = pe.matmul(ps_s[rows, GRP * g:GRP * g + GRP], qm[:, v % 2, g, rows],
                                       km[:, v % 2, :, rows], start=True, stop=True)
                mm.then_inc(s_made, 1)

            def p_transpose(t, v):
                pe.wait_ge(p_ready, t + 1)
                if late(t, 1):
                    pe.wait_ge(pt_ready, 2 * t)
                flat = sd[:, v].rearrange("p (n h) s -> p n (h s)", h=2)
                for n in range(PAIRS):
                    mm = pe.transpose(ps_pt[:, n], flat[:, n], k.ident[:])
                mm.then_inc(pt_made, 1)

            def values(t, v):
                pe.wait_ge(pt_ready, 2 * t + 1)
                if late(t, 1):
                    pe.wait_ge(o_ready, t)
                for n in range(PAIRS):
                    if n == PAIRS // 2:
                        pe.wait_ge(pt_ready, 2 * t + 2)
                    for b in range(2):
                        rows = slice(b * SEQ, (b + 1) * SEQ)
                        mm = pe.matmul(o_ps[rows, 2 * n:2 * n + 2], pt[:, v % 2, n, rows], vbd[:, v, b, n],
                                       start=True, stop=True)
                mm.then_inc(o_made, 1)

            def o_transpose(t, v):
                pe.wait_ge(o_ready, t + 1)
                if late(t, 1):
                    pe.wait_ge(x_added, t)
                pe.transpose(ot_ps, o_sb[:, v % 2].rearrange("p h d -> p (h d)"), k.ident[:]).then_inc(ot_made, 1)

            def out_project(t, v):
                pe.wait_ge(ot_ready, t + 1)
                pe.matmul(y_ps, ot_sb[:, v % 2], k.a_wo[:], start=True, stop=True).then_inc(y_made, 1)

            def step(i, u):
                for stage, behind in ((x_transpose, 1), (o_transpose, 7), (p_transpose, 6), (project, 2),
                                      (out_project, 7), (values, 6), (scores, 3)):
                    if cross and stage in (o_transpose, out_project):
                        continue
                    if has(i - behind, NT):
                        stage(i - behind, (u - behind) % UNROLL)

            pipeline(pe, NT, step, 7, UNROLL, 3 * UNROLL)

        @block.scalar
        def _(act):
            act.wait_ge(setup, 2)

            def x_copy(t, v):
                act.wait_ge(xt_made, t + 1)
                if late(t, 2):
                    act.wait_ge(qkv_made, t - 1)
                act.copy(xt[:, v % 2], ps_xt[:, 0:P]).then_inc(xt_ready, 1)

            def qkv_copy(t, v):
                act.wait_ge(qkv_made, t + 1)
                if late(t, 2):
                    act.wait_ge(masked, t - 1)
                act.activation(k_sb[:, v % 2], ps_qkv[:, 1], ACT.Identity, bias=bk[:])
                act.activation(q_sb[:, v % 2], ps_qkv[:, 0], ACT.Identity, bias=bq[:])
                if late(t, 4):
                    act.wait_ge(o_made, t - 3)
                for half in range(2):
                    rows = slice(half * SEQ, (half + 1) * SEQ)
                    src = ps_qkv[rows, 2:4].rearrange("p b (n h d) -> p b n h d", h=2, d=D0)
                    op = act.copy(vbd[rows, v, :, :, half, 0:D0], src[:, :, :, half])
                op.then_inc(qkv_ready, 1)

            def exponential(t, v):
                act.wait_ge(sub_ready, t + 1)
                act.activation(sd[:, v], sd[:, v], ACT.Exp, scale=scale).then_inc(p_ready, 1)

            def p_copy(t, v):
                act.wait_ge(pt_made, t + 1)
                if late(t, 2):
                    act.wait_ge(o_made, t - 1)
                for half in range(2):
                    pairs = slice(half * PAIRS // 2, (half + 1) * PAIRS // 2)
                    act.copy(pt[:, v % 2, pairs], ps_pt[:, pairs]).then_inc(pt_ready, 1)

            def o_copy(t, v):
                act.wait_ge(ot_made, t + 1)
                if late(t, 2):
                    act.wait_ge(y_made, t - 1)
                act.activation(ot_sb[:, v % 2], ot_ps, ACT.Identity, bias=bv[:]).then_inc(ot_ready, 1)

            def step(i, u):
                for stage, behind in ((x_copy, 1), (o_copy, 7), (p_copy, 6), (qkv_copy, 2), (exponential, 4)):
                    if cross and stage is o_copy:
                        continue
                    if has(i - behind, NT):
                        stage(i - behind, (u - behind) % UNROLL)

            pipeline(act, NT, step, 7, UNROLL, 3 * UNROLL)

        @block.vector
        def _(dve):
            norm = ((k.o_mean_var, k.o_scale[:], k.o_shift[:]) if cross else
                    (k.mean_var, k.ln_scale[:], k.ln_shift[:]))

            def normalise(t, v):
                if late(t, 2):
                    dve.wait_ge(xt_made, t - 1)
                dve.tensor_scalar(xn[:, v % 2], k.x_res[:, t], k.ln_scale[:, bass.ds(t, 1)], k.ln_shift[:, bass.ds(t, 1)],
                                  ALU.mult, ALU.add).then_inc(xn_ready, 1)

            def softmax(t, v):
                dve.wait_ge(s_made, t + 1)
                if late(t, 4):
                    dve.wait_ge(pt_made, t - 3)
                if cross:
                    dve.scalar_tensor_tensor(out=sd[:, v], in0=bc(k.mask_all[:, t], 1, H0), scalar=NEG, in1=ps_s[:],
                                             op0=ALU.mult, op1=ALU.add).then_inc(s_taken, 1)
                else:
                    dve.tensor_tensor(sd[:, v], ps_s[:], bc(k.decay[:], 1, H0), ALU.mult).then_inc(s_taken, 1)
                dve.wait_ge(s_taken, t + 1)
                dve.tensor_reduce(mx[:, v], sd[:, v], AX.X, ALU.max).then_inc(mx_ready, 1)

            def divide(t, v):
                dve.wait_ge(o_made, t + 1)
                if late(t, 2):
                    dve.wait_ge(xb_ready if cross else ot_made, t - 1)
                dve.reciprocal(rec[:, v % 2], o_ps[:, :, D0]).then_inc(rec_ready, 1)
                dve.wait_ge(rec_ready, t + 1)
                dve.tensor_tensor(o_sb[:, v % 2], o_ps[:, :, 0:D0], rec[:, v % 2].unsqueeze(2).to_broadcast([P, H0, D0]),
                                  ALU.mult).then_inc(o_ready, 1)

            def residual(t, v):
                all_rows, all_stats = (k.o_all, k.o_mean_var) if cross else (k.x_res, k.mean_var)
                dve.wait_ge(xb_ready, t + 1)
                if late(t, 2):
                    dve.wait_ge(mv_kept, t - 1)
                if not cross:
                    dve.wait_ge(y_made, t + 1)
                    dve.tensor_tensor(row[:, v % 2], y_ps, xb[:, v % 2], ALU.add).then_inc(x_added, 1)
                    dve.wait_ge(x_added, t + 1)
                keep_with_stats(dve, row[:, v % 2], all_rows[:, t], st[:, v % 2], mv[:, v % 2], all_stats[:, t], t,
                                st_ready, mv_ready, mv_kept)

            def make_mask(t, v):
                if not late(t, 1):
                    dve.wait_ge(mask_loaded, 16)
                dve.scalar_tensor_tensor(out=k.mask_all[:, t], in0=k.mask_in[:, t], scalar=0.0, in1=k.future[:],
                                         op0=ALU.is_equal, op1=ALU.max)

            rest = LoadedStats(dve, k, rest_st, (rest_sums, rest_ready, rest_newton), 1, 16)

            def step(i, u):
                for stage, behind in ((softmax, 4), (residual, 7), (divide, 6), (normalise, 0), (make_mask, 7)):
                    if cross and stage is make_mask:
                        continue
                    if has(i - behind, NT):
                        stage(i - behind, (u - behind) % UNROLL)
                if not cross and isinstance(i, int) and 3 <= i <= 3 + rest.count:
                    rest.step(i - 3)

            pipeline(dve, NT, step, 7, UNROLL, 3 * UNROLL)
            dve.wait_ge(mv_kept, NT)
            layer_norm_scales(dve, k, *norm, newton)


def project_cross(nc, k):
    NT = k.tiles
    with ExitStack() as c:
        def sb(n, shape, dt=F32):
            return c.enter_context(nc.sbuf_tensor(f"xp_{n}", shape, dt))

        new_sem = c.enter_context(stage_semaphores(nc))

        def sem(n):
            return new_sem(f"xp_{n}")

        ROWS = [P, 2, GROUP, P]
        on, ot, xb, row = sb("on", ROWS), sb("ot", ROWS), sb("xb", ROWS), sb("row", ROWS)
        st = sb("st", [P, 2, GROUP, 6])
        mv = sb("mv", [P, 2, GROUP, 2])
        zero_row = sb("zero_row", [P, P])
        ps_t = [c.enter_context(nc.psum_tensor(f"xp_t{n}", [P, GROUP, P], F32)) for n in range(2)]
        ps_y = [c.enter_context(nc.psum_tensor(f"xp_y{n}", [P, GROUP, P], F32)) for n in range(2)]
        on_ready, ot_made, ot_ready, y_made = sem("on_ready"), sem("ot_made"), sem("ot_ready"), sem("y_made")
        newton = sem("newton")
        xb_ready, x_added, row_kept = sem("xb_ready"), sem("x_added"), sem("row_kept")
        stored = [sem(f"stored{n}") for n in range(2)]
        st_ready, mv_ready, mv_kept = sem("st_ready"), sem("mv_ready"), sem("mv_kept")
        zeroed, zeros_stored = sem("zeroed"), sem("zeros_stored")
        block = c.enter_context(nc.Block())

        @block.gpsimd
        def _(pool):
            pool.memset(zero_row[:], 0.0).then_inc(zeroed, 1)

            def step(g, u):
                if late(g, 2):
                    pool.wait_ge(x_added, g - 1)
                pool.tensor_tensor(xb[:, u], k.x_res[:, group(g)], bc(k.x_bo[:], 1, GROUP), ALU.add).then_inc(xb_ready, 1)

            group_pipeline(pool, NT, step, 0)

        @block.tensor
        def _(pe):
            def step(i, u):
                if has(i, NT // GROUP):
                    pe.wait_ge(on_ready, i + 1)
                    if late(i, 2):
                        pe.wait_ge(ot_ready, i - 1)
                    for n in range(GROUP):
                        mm = pe.transpose(ps_t[u][:, n], on[:, u, n], k.ident[:])
                    mm.then_inc(ot_made, 1)
                g, v = i - 1, 1 - u
                if has(g, NT // GROUP):
                    pe.wait_ge(ot_ready, g + 1)
                    if late(g, 2):
                        pe.wait_ge(x_added, g - 1)
                    for n in range(GROUP):
                        mm = pe.matmul(ps_y[v][:, n], ot[:, v, n], k.x_wo[:], start=True, stop=True)
                    mm.then_inc(y_made, 1)

            group_pipeline(pe, NT, step, 1)

        @block.scalar
        def _(act):
            def step(i, u):
                if has(i, NT // GROUP):
                    act.wait_ge(ot_made, i + 1)
                    if late(i, 2):
                        act.wait_ge(y_made, i - 1)
                    act.activation(ot[:, u], ps_t[u][:], ACT.Identity, scale=k.x_ln_g[:], bias=k.x_ln_b[:])\
                       .then_inc(ot_ready, 1)
                g, v = i - 2, u
                if has(g, NT // GROUP):
                    act.wait_ge(x_added, g + 1)
                    act.copy(k.x_res[:, group(g)], row[:, v]).then_inc(row_kept, 1)

            group_pipeline(act, NT, step, 2)

        @block.sync
        def _(sp):
            def step(g, u):
                sp.wait_ge(x_added, g + 1)
                sp.dma_start(k.x_dram[group(g)].rearrange("n p c -> p n c"), row[:, u]).then_inc(stored[u], 16)

            sp.wait_ge(zeroed, 1)
            sp.dma_start(k.x_dram[NT:NT + NE * CAP // P].rearrange("n p c -> p n c"),
                         bc(zero_row[:], 1, NE * CAP // P)).then_inc(zeros_stored, 16)
            group_pipeline(sp, NT, step, 0)
            for n in range(2):
                sp.wait_ge(stored[n], 16 * len(range(n, NT // GROUP, 2)))
            sp.wait_ge(zeros_stored, 16)

        @block.vector
        def _(dve):
            stats = GroupStats(dve, NT, row, k.mean_var, st, mv, st_ready, mv_ready, mv_kept)

            def step(i, u):
                if has(i, NT // GROUP):
                    if late(i, 2):
                        dve.wait_ge(ot_made, i - 1)
                    for n in range(GROUP):
                        op = dve.tensor_scalar(on[:, u, n], k.o_all[:, i * GROUP + n],
                                               k.o_scale[:, bass.ds(i * GROUP + n, 1)],
                                               k.o_shift[:, bass.ds(i * GROUP + n, 1)], ALU.mult, ALU.add)
                    op.then_inc(on_ready, 1)
                g, v = i - 2, u
                if has(g, NT // GROUP):
                    dve.wait_ge(xb_ready, g + 1)
                    dve.wait_ge(y_made, g + 1)
                    if late(g, 2):
                        dve.wait_ge(row_kept, g - 1)
                        dve.wait_ge(stored[v], 8 * (g - v))
                    dve.tensor_tensor(row[:, v], ps_y[v][:], xb[:, v], ALU.add).then_inc(x_added, 1)
                stats.keep_and_aggregate(i - 3, 1 - u)
                if has(g, NT // GROUP):
                    dve.wait_ge(x_added, g + 1)
                    stats.by_row(g, v)

            group_pipeline(dve, NT, step, 4)
            dve.wait_ge(mv_kept, NT // GROUP)
            layer_norm_scales(dve, k, k.mean_var, k.ln_scale[:], k.ln_shift[:], newton)


def set_up(nc, k):
    NT = k.tiles
    with ExitStack() as c:
        new_sem = c.enter_context(stage_semaphores(nc))

        def sem(n):
            return new_sem(f"su_{n}")

        dist = c.enter_context(nc.sbuf_tensor("su_dist", [P, SEQ], F32))
        dd = c.enter_context(nc.sbuf_tensor("su_dd", [P, 1], F32))
        dd_neg = c.enter_context(nc.sbuf_tensor("su_dd_neg", [P, 1], F32))
        dd_abs = c.enter_context(nc.sbuf_tensor("su_dd_abs", [P, 1], F32))
        st = c.enter_context(nc.sbuf_tensor("su_st", [P, 2, GROUP, 6], F32))
        loaded, dd_loaded = sem("loaded"), sem("dd_loaded")
        newton = sem("newton")
        dd_ready, dec, st_ready, mv_ready = sem("dd_ready"), sem("dec"), sem("st_ready"), sem("mv_ready")
        block = c.enter_context(nc.Block())

        @block.sync
        def _(sp):
            for n in range(NT // GROUP):
                sp.dma_start(k.x_res[:, n * GROUP:(n + 1) * GROUP],
                             k.in_x[n * GROUP:(n + 1) * GROUP].rearrange("n p c -> p n c")).then_inc(k.x_loaded[n], 16)

        @block.scalar
        def _(act):
            act.dma_start(dist[:], k.in_dist).then_inc(dd_loaded, 16)
            act.dma_start(dd[:], k.in_dd.to_broadcast([P, 1])).then_inc(dd_loaded, 16)
            for tile, src in k.first_loads:
                act.dma_start(tile, src).then_inc(loaded, 16)
            act.wait_ge(dd_ready, 2)
            act.activation(k.decay[:], dist[:], ACT.Exp, scale=dd_abs[:]).then_inc(dec, 1)
            act.wait_ge(loaded, 16 * len(k.first_loads))

        @block.vector
        def _(dve):
            dve.wait_ge(dd_loaded, 32)
            dve.tensor_scalar(dd_neg[:], dd[:], -1.0, None, ALU.mult).then_inc(dd_ready, 1)
            dve.wait_ge(dd_ready, 1)
            dve.tensor_tensor(dd_abs[:], dd[:], dd_neg[:], ALU.min).then_inc(dd_ready, 1)
            loaded_stats = LoadedStats(dve, k, st, (st_ready, mv_ready, newton), 0, 16)
            for n in range(loaded_stats.count + 1):
                loaded_stats.step(n)



def router(nc, k, name, weight, bias, xn_dram, x_copy_dram):
    NT = k.tiles
    NG = NT // GROUP
    with ExitStack() as c:
        def sb(n, shape, dt=F32):
            return c.enter_context(nc.sbuf_tensor(f"{name}_{n}", shape, dt))

        new_sem = c.enter_context(stage_semaphores(nc))

        def sem(n):
            return new_sem(f"{name}_{n}")

        BUFS = 4
        xn = sb("xn", [P, BUFS, GROUP, P])
        xt = sb("xt", [P, BUFS, GROUP, P])
        ps_t = [c.enter_context(nc.psum_tensor(f"{name}_t{n}", [P, GROUP, P], F32)) for n in range(BUFS)]
        lt = sb("lt", [NE, 2, GROUP, P])
        ps_e = [c.enter_context(nc.psum_tensor(f"{name}_e{n}", [P, GROUP, P], F32)) for n in range(2)]
        ps_l = [c.enter_context(nc.psum_tensor(f"{name}_l{n}", [P, 512], F32)) for n in range(2)]
        xn_ready, xt_made, xt_ready = sem("xn_ready"), sem("xt_made"), sem("xt_ready")
        lt_made, lt_ready = sem("lt_made"), sem("lt_ready")
        l_made, l_ready, x_stored = sem("l_made"), sem("l_ready"), sem("x_stored")
        xn_stored = [sem(f"xn_stored{n}") for n in range(BUFS)]
        block = c.enter_context(nc.Block())

        @block.sync
        def _(sp):
            def step(g, u):
                sp.wait_ge(xn_ready, g + 1)
                sp.dma_start(xn_dram[group(g)].rearrange("n p c -> p n c"), xn[:, u]).then_inc(xn_stored[u], 16)
                if x_copy_dram is not None:
                    sp.dma_start(x_copy_dram[group(g)].rearrange("n p c -> p n c"), k.x_res[:, group(g)])\
                        .then_inc(x_stored, 16)

            pipeline(sp, NG, step, 0, BUFS, BUFS)
            for n in range(BUFS):
                sp.wait_ge(xn_stored[n], 16 * len(range(n, NG, BUFS)))
            if x_copy_dram is not None:
                sp.wait_ge(x_stored, 16 * NG)

        @block.tensor
        def _(pe):
            def step(i, u):
                if has(i, NG):
                    pe.wait_ge(xn_ready, i + 1)
                    if late(i, BUFS):
                        pe.wait_ge(xt_ready, i - BUFS + 1)
                    for n in range(GROUP):
                        mm = pe.transpose(ps_t[u][:, n], xn[:, u, n], k.ident[:])
                    mm.then_inc(xt_made, 1)
                g = i - 2
                if has(g, NG):
                    pe.wait_ge(lt_ready, g + 1)
                    if late(g, 2):
                        pe.wait_ge(l_ready, g - 1)
                g, v = i - 1, (u - 1) % BUFS
                if has(g, NG):
                    pe.wait_ge(xt_ready, g + 1)
                    if late(g, 2):
                        pe.wait_ge(lt_ready, g - 1)
                    pe.matmul(ps_e[v % 2][0:NE], weight[:], xt[:, v], start=True, stop=True).then_inc(lt_made, 1)
                g, v = i - 2, (u - 2) % BUFS
                if has(g, NG):
                    for n in range(GROUP):
                        mm = pe.transpose(ps_l[v % 2][:, n * NE:(n + 1) * NE], lt[:, v % 2, n], k.ident[0:NE, 0:NE])
                    mm.then_inc(l_made, 1)

            pipeline(pe, NG, step, 2, BUFS, 2 * BUFS)

        @block.scalar
        def _(act):
            def step(i, u):
                g, v = i - 2, (u - 2) % BUFS
                if has(g, NG):
                    act.wait_ge(lt_made, g + 1)
                    if late(g, 2):
                        act.wait_ge(l_made, g - 1)
                    act.copy(lt[:, v % 2], ps_e[v % 2][0:NE]).then_inc(lt_ready, 1)
                if has(i, NG):
                    act.wait_ge(xt_made, i + 1)
                    if late(i, BUFS):
                        act.wait_ge(lt_made, i - BUFS + 1)
                    act.copy(xt[:, u], ps_t[u][:]).then_inc(xt_ready, 1)

            pipeline(act, NG, step, 2, BUFS, BUFS)

        @block.vector
        def _(dve):
            def step(i, u):
                if has(i, NG):
                    if late(i, BUFS):
                        dve.wait_ge(xt_made, i - BUFS + 1)
                        dve.wait_ge(xn_stored[u], 16 // BUFS * (i - u))
                    normalise_group(dve, k, i, xn[:, u]).then_inc(xn_ready, 1)
                g, v = i - 3, (u - 3) % BUFS
                if has(g, NG):
                    dve.wait_ge(l_made, g + 1)
                    dve.tensor_tensor(k.logits[:, group(g)],
                                      ps_l[v % 2][:, 0:GROUP * NE].rearrange("p (n e) -> p n e", e=NE),
                                      bc(bias[:], 1, GROUP), ALU.add).then_inc(l_ready, 1)

            pipeline(dve, NG, step, 3, BUFS, BUFS)


def chosen_slots(nc, k, name, top, slots, w_slot):
    NT = k.tiles
    NS = slots
    with ExitStack() as c:
        def sb(n, shape, dt=F32):
            return c.enter_context(nc.sbuf_tensor(f"{name}_{n}", shape, dt))

        new_sem = c.enter_context(stage_semaphores(nc))

        def sem(n):
            return new_sem(f"{name}_{n}")

        E = [P, NT, NE]
        m = sb("m", [P, top, NT])
        key = sb("key", E)
        first = sb("first", [P, NT])
        oh = [sb(f"oh{n}", E) for n in range(top)]
        rest = sb("rest", E)
        sel_bf = sb("sel_bf", E, BF16)
        total = sb("total", E)
        rank = sb("rank", E)
        slot_e = sb("slot_e", E)
        keep = sb("keep", E)
        tmp = sb("tmp", E)
        slot = sb("slot", [P, top, NT])
        slot_i = sb("slot_i", [P, top, NT], I32)
        part_i = sb("part_i", [P, 2, top, NT], I32)
        part = sb("part", [P, 2, top, NT])
        zeros = sb("zeros", [P, NT])
        small = sb("small", [P, 6, NE])
        small_i = sb("small_i", [P, 2, NE], I32)
        lists = 5 if top == 2 else 2
        row_hot = [sb(f"row_hot{n}", [P, NT, P], BF16) for n in range(top)]
        tile_hot = sb("tile_hot", [P, NT, NS], BF16)
        listed = [sb(f"listed{n}", [P, NT, lists, NS], BF16) for n in range(top)]
        w = sb("w", [P, 4, NT])
        parts = sb("parts", [P, 2, 3, NT])
        parts_bf = sb("parts_bf", [P, 2, 3, NT], BF16)
        table = sb("table", [P, lists, NS])
        ids = sb("ids", [P, 5, NS])
        ge = sb("ge", [P, NS, NE]) if top == 1 else None
        ps_r = c.enter_context(nc.psum_tensor(f"{name}_r", [P, 512], F32))
        ps_n = c.enter_context(nc.psum_tensor(f"{name}_n", [P, 512], F32))
        ps_l = c.enter_context(nc.psum_tensor(f"{name}_l", [P, 512], F32))
        neg_part = sb("neg_part", [P, NT])
        one = sb("one", [P, 1])
        distance = sb("distance", [P, NT if top == 2 else NT - NT * 5 // 8, P], BF16)
        part_ready, distance_ready, hot_ready = sem("part_ready"), sem("distance_ready"), sem("hot_ready")
        done = sem("done")
        e_ready = sem("e_ready")
        d_ready = sem("d_ready")
        sel_ready, ranks_made = sem("sel_ready"), sem("ranks_made")
        listed_ready, listed_made = sem("listed_ready"), sem("listed_made")
        block = c.enter_context(nc.Block())

        by_act = 0 if top == 2 else NT * 5 // 8

        @block.scalar
        def _(act):
            if top == 2:
                act.wait_ge(d_ready, 1)
                act.activation(w[:, 1], w[:, 0], ACT.Exp).then_inc(e_ready, 1)
            act.wait_ge(part_ready, 1)
            for t in range(by_act, NT):
                op = act.activation(distance[:, t - by_act], k.iota_s[:], ACT.Square, bias=neg_part[:, t:t + 1])
            op.then_inc(distance_ready, 1)
            act.wait_ge(distance_ready, 1)
            act.activation(row_hot[top - 1][:, by_act:NT], distance[:], ACT.Relu, scale=-1.0, bias=one[:])\
                .then_inc(hot_ready, 1)

        @block.tensor
        def _(pe):
            flat = sel_bf[:].rearrange("p n e -> p (n e)")
            pe.wait_ge(sel_ready, 1)
            pe.matmul(ps_r[:, 0:NT * NE], k.before[:], flat, start=True, stop=True)
            pe.matmul(ps_n[:, 0:NT * NE], k.ones_bf[:], flat, start=True, stop=True).then_inc(ranks_made, 1)
            for n in range(top):
                pe.wait_ge(listed_ready, n + 1)
                if n == top - 1:
                    pe.wait_ge(hot_ready, 1)
                for t in range(NT):
                    mm = pe.matmul(ps_l[:, 0:lists * NS], row_hot[n][:, t], listed[n][:, t].rearrange("p l s -> p (l s)"),
                                   start=(n == 0 and t == 0), stop=(n == top - 1 and t == NT - 1))
                mm.then_inc(listed_made, 1)

        @block.vector
        def _(dve):
            count = [0]

            def op(instruction):
                count[0] += 1
                instruction.then_inc(done, 1)
                dve.wait_ge(done, count[0])

            def all_e(ap):
                return ap.unsqueeze(2).to_broadcast(E)

            scores = k.logits
            for n in range(top):
                op(dve.tensor_reduce(m[:, n], scores[:], AX.X, ALU.max))
                op(dve.tensor_tensor(oh[n][:], scores[:], all_e(m[:, n]), ALU.is_equal))
                op(dve.scalar_tensor_tensor(out=key[:], in0=oh[n][:], scalar=-float(NE), in1=bc(k.iota_e[:], 1, NT),
                                            op0=ALU.mult, op1=ALU.add))
                op(dve.tensor_reduce(first[:], key[:], AX.X, ALU.min))
                op(dve.tensor_tensor(oh[n][:], key[:], all_e(first[:]), ALU.is_equal))
                if n == 0 and top == 2:
                    op(dve.scalar_tensor_tensor(out=rest[:], in0=oh[0][:], scalar=-3e38, in1=scores[:],
                                                op0=ALU.mult, op1=ALU.add))
                    scores = rest
            if top == 2:
                dve.tensor_tensor(w[:, 0], m[:, 1], m[:, 0], ALU.subtract).then_inc(d_ready, 1)
                op(dve.tensor_tensor(sel_bf[:], oh[0][:], oh[1][:], ALU.add))
            else:
                op(dve.tensor_copy(sel_bf[:], oh[0][:]))
            dve.memset(zeros[:], 0.0).then_inc(sel_ready, 1)

            dve.wait_ge(ranks_made, 1)
            op(dve.tensor_copy(total[:], ps_n[:, 0:NT * NE].rearrange("p (n e) -> p n e", e=NE)))
            for e in range(NE):
                op(dve.tensor_tensor_scan(rank[:, :, e], total[:, :, e], zeros[:], 0.0, ALU.add, ALU.add))
            if top == 1:
                op(dve.tensor_scalar(small_i[:, 0], rank[:, NT - 1], float(P - 1), None, ALU.add))
                op(dve.tensor_scalar(small_i[:, 1], small_i[:, 0], 7, None, ALU.arith_shift_right))
                op(dve.tensor_copy(small[:, 0], small_i[:, 1]))
                op(dve.tensor_tensor_scan(small[:, 1], small[:, 0], zeros[:, 0:NE], 0.0, ALU.add, ALU.add))
                op(dve.tensor_tensor(small[:, 2], small[:, 1], small[:, 0], ALU.subtract))
                op(dve.tensor_scalar(small[:, 3], small[:, 2], float(P), 1.0, ALU.mult, ALU.add))
                op(dve.tensor_tensor(ge[:], k.iota_s[:, 0:NS].unsqueeze(2).to_broadcast([P, NS, NE]),
                                     bc(small[:, 1], 1, NS), ALU.is_ge))
                op(dve.tensor_reduce(ids[:, 0], ge[:], AX.X, ALU.add))
                op(dve.tensor_scalar(k.tile_expert[:], ids[:, 0], float(NE - 1), None, ALU.min))
            op(dve.tensor_tensor(rank[:], rank[:], total[:], ALU.subtract))
            op(dve.tensor_tensor(rank[:], rank[:], ps_r[:, 0:NT * NE].rearrange("p (n e) -> p n e", e=NE), ALU.add))
            first_slot = k.iota_cap[:] if top == 2 else small[:, 3]
            op(dve.tensor_tensor(slot_e[:], rank[:], bc(first_slot, 1, NT), ALU.add))
            if top == 2:
                op(dve.tensor_scalar(keep[:], rank[:], float(CAP), None, ALU.is_lt))
                op(dve.tensor_tensor(slot_e[:], slot_e[:], keep[:], ALU.mult))
            for n in range(top):
                op(dve.tensor_tensor(tmp[:], slot_e[:], oh[n][:], ALU.mult))
                op(dve.tensor_reduce(slot[:, n], tmp[:], AX.X, ALU.add))
            op(dve.tensor_scalar(slot_i[:], slot[:], -1.0, None, ALU.add))
            op(dve.tensor_scalar(part_i[:, 0], slot_i[:], 7, None, ALU.arith_shift_right))
            op(dve.tensor_scalar(part_i[:, 1], slot_i[:], P - 1, None, ALU.bitwise_and))
            op(dve.tensor_copy(part[:], part_i[:]))
            op(dve.memset(one[:], 1.0))
            op(dve.tensor_scalar(neg_part[:], part[:, 1, top - 1], -1.0, None, ALU.mult))
            dve.memset(zeros[:, 0:1], 0.0).then_inc(part_ready, 1)

            if top == 2:
                dve.wait_ge(e_ready, 1)
                op(dve.tensor_scalar(w[:, 0], w[:, 1], 1.0, None, ALU.add))
                op(dve.reciprocal(w[:, 2], w[:, 0]))
                op(dve.tensor_tensor(w[:, 3], w[:, 1], w[:, 2], ALU.mult))
                op(dve.tensor_copy(parts[:, :, 0], w[:, 2:4]))
                for n in range(3):
                    op(dve.tensor_copy(parts_bf[:, :, n], parts[:, :, n]))
                    if n < 2:
                        op(dve.tensor_tensor(parts[:, :, n + 1], parts[:, :, n], parts_bf[:, :, n], ALU.subtract))

            for n in range(top):
                mine = by_act if n == top - 1 else NT
                if mine:
                    op(dve.tensor_tensor(row_hot[n][:, 0:mine], bc(k.iota_s[:], 1, mine),
                                         part[:, 1, n, 0:mine].unsqueeze(2).to_broadcast([P, mine, P]), ALU.is_equal))
                op(dve.tensor_tensor(tile_hot[:], bc(k.iota_s[:, 0:NS], 1, NT),
                                     part[:, 0, n].unsqueeze(2).to_broadcast([P, NT, NS]), ALU.is_equal))
                op(dve.tensor_tensor(listed[n][:, :, 0], tile_hot[:], k.iota_s1[:, 0:NT].unsqueeze(2).to_broadcast([P, NT, NS]),
                                     ALU.mult))
                op(dve.tensor_scalar(listed[n][:, :, 1], tile_hot[:], k.place[:], None, ALU.mult))
                for q in range(2, lists):
                    op(dve.tensor_tensor(listed[n][:, :, q], tile_hot[:],
                                         parts_bf[:, n, q - 2].unsqueeze(2).to_broadcast([P, NT, NS]), ALU.mult))
                dve.memset(zeros[:, 0:1], 0.0).then_inc(listed_ready, 1)
            dve.wait_ge(listed_made, top)
            op(dve.tensor_copy(table[:], ps_l[:, 0:lists * NS].rearrange("p (l s) -> p l s", s=NS)))
            op(dve.tensor_scalar(ids[:, 1], table[:, 0], float(P), -float(P), ALU.mult, ALU.add))
            op(dve.tensor_tensor(ids[:, 2], ids[:, 1], table[:, 1], ALU.add))
            op(dve.tensor_scalar(k.gather_idx[:, 0:NS], ids[:, 2], 0.0, None, ALU.max))
            op(dve.tensor_scalar(ids[:, 3], table[:, 0], 0.0, None, ALU.is_equal))
            op(dve.tensor_tensor(ids[:, 3], ids[:, 3], k.empty_id[:, 0:NS], ALU.mult))
            op(dve.tensor_tensor(k.scatter_idx[:, 0:NS], ids[:, 2], ids[:, 3], ALU.add))
            if top == 2:
                op(dve.tensor_tensor(w_slot[:], table[:, 4], table[:, 3], ALU.add))
                op(dve.tensor_tensor(w_slot[:], w_slot[:], table[:, 2], ALU.add))


def two_expert_ffn(nc, k):
    NT = k.tiles
    with ExitStack() as c:
        def sb(n, shape, dt=F32):
            return c.enter_context(nc.sbuf_tensor(f"m0_{n}", shape, dt))

        new_sem = c.enter_context(stage_semaphores(nc))

        def sem(n):
            return new_sem(f"m0_{n}")

        HALVES = CAP // P
        xg = sb("xg", [P, NE * HALVES, P])
        xgt = sb("xgt", [P, 2, CAP])
        gate = sb("gate", [P, 2, 2, CAP])
        hid = sb("hid", [P, 2, 2, CAP])
        y = sb("weighted", [P, NE * HALVES, P])
        st = sb("st", [P, 2, GROUP, 6])
        ps_t = c.enter_context(nc.psum_tensor("m0_t", [P, 512], F32))
        ps_h = [c.enter_context(nc.psum_tensor(f"m0_h{n}", [P, 2, 2, CAP], F32)) for n in range(2)]
        ps_y = c.enter_context(nc.psum_tensor("m0_y", [P, 512], F32))
        gathered, added = k.gathered0, k.added0
        xt_made, xt_ready, h_made, gate_ready = sem("xt_made"), sem("xt_ready"), sem("h_made"), sem("gate_ready")
        hid_ready, y_made, y_ready = sem("hid_ready"), sem("y_made"), sem("y_ready")
        newton = sem("newton")
        st_ready, mv_ready = sem("st_ready"), sem("mv_ready")
        nc.scalar.preload_act_table(ACT.Silu)
        block = c.enter_context(nc.Block())

        @block.gpsimd
        def _(pool):
            def gather(e):
                for n in range(HALVES * e, HALVES * (e + 1)):
                    pool.indirect_dma_start(xg[:, n], None, k.xn_rows,
                                            bass.IndirectOffsetOnAxis(ap=k.gather_idx[:, n:n + 1], axis=0))\
                        .then_inc(gathered[n], 16)

            ahead = 5
            for e in range(ahead):
                gather(e)
            for e in range(NE):
                pool.wait_ge(y_ready, HALVES * (e + 1))
                if e:
                    pool.wait_ge(added[e - 1], 16 * HALVES)
                for half in range(HALVES):
                    n = HALVES * e + half
                    pool.indirect_dma_start(k.x_rows, bass.IndirectOffsetOnAxis(ap=k.scatter_idx[:, n:n + 1], axis=0),
                                            y[:, n], None, compute_op=ALU.add).then_inc(added[e], 16)
                if e + ahead < NE:
                    gather(e + ahead)

        @block.tensor
        def _(pe):
            def transposes(e):
                if e:
                    pe.wait_ge(xt_ready, e)
                for half in range(HALVES):
                    pe.wait_ge(gathered[HALVES * e + half], 16)
                    mm = pe.transpose(ps_t[:, half * P:(half + 1) * P], xg[:, HALVES * e + half], k.ident[:])
                mm.then_inc(xt_made, 1)

            def hidden(e):
                pe.wait_ge(xt_ready, e + 1)
                if e >= 2:
                    pe.wait_ge(hid_ready, e - 1)
                for n, weight in ((1, k.f0_v), (0, k.f0_w)):
                    for f in range(2):
                        mm = pe.matmul(ps_h[e % 2][:, n, f], weight[:, e, f * P:(f + 1) * P], xgt[:, e % 2],
                                       start=True, stop=True)
                mm.then_inc(h_made, 1)

            def output(e):
                pe.wait_ge(hid_ready, e + 1)
                if e:
                    pe.wait_ge(y_ready, HALVES * e)
                for half in range(HALVES):
                    for f in range(2):
                        mm = pe.matmul(ps_y[:, half * P:(half + 1) * P], hid[:, e % 2, f, half * P:(half + 1) * P],
                                       k.f0_out[:, e, f], start=(f == 0), stop=(f == 1))
                mm.then_inc(y_made, 1)

            for i in range(NE + 2):
                if i < NE:
                    transposes(i)
                if 1 <= i <= NE:
                    hidden(i - 1)
                if i >= 2:
                    output(i - 2)

        @block.scalar
        def _(act):
            for i in range(NE + 1):
                if i < NE:
                    act.wait_ge(xt_made, i + 1)
                    if i >= 2:
                        act.wait_ge(h_made, i - 1)
                    act.copy(xgt[:, i % 2], ps_t[:, 0:CAP]).then_inc(xt_ready, 1)
                if i >= 1:
                    e = i - 1
                    act.wait_ge(h_made, e + 1)
                    if e >= 2:
                        act.wait_ge(hid_ready, e - 1)
                    act.activation(gate[:, e % 2], ps_h[e % 2][:, 1], ACT.Silu).then_inc(gate_ready, 1)

        @block.sync
        def _(sp):
            for e in range(NE):
                sp.wait_ge(added[e], 16 * HALVES)
            for n in range(NT // GROUP):
                sp.dma_start(k.x_res[:, n * GROUP:(n + 1) * GROUP],
                             k.x_dram[n * GROUP:(n + 1) * GROUP].rearrange("n p c -> p n c"))\
                    .then_inc(k.x_loaded[n], 16)

        @block.vector
        def _(dve):
            for e in range(NE):
                dve.wait_ge(gate_ready, e + 1)
                if e >= 2:
                    dve.wait_ge(y_made, e - 1)
                dve.tensor_tensor(hid[:, e % 2], ps_h[e % 2][:, 0], gate[:, e % 2], ALU.mult).then_inc(hid_ready, 1)
                dve.wait_ge(y_made, e + 1)
                for half in range(HALVES):
                    n = HALVES * e + half
                    dve.tensor_scalar(y[:, n], ps_y[:, half * P:(half + 1) * P], k.w_slot[:, n:n + 1], None,
                                      ALU.mult).then_inc(y_ready, 1)
            loaded_stats = LoadedStats(dve, k, st, (st_ready, mv_ready, newton), 0, 32)
            for n in range(loaded_stats.count + 1):
                loaded_stats.step(n)


def wide_head_attention(nc, k):
    NT = k.tiles
    HALF = D1 // 2
    scale = float(D1) ** -0.5
    with ExitStack() as c:
        def sb(n, shape, dt=F32):
            return c.enter_context(nc.sbuf_tensor(f"wa_{n}", shape, dt))

        def ps(n, shape):
            return c.enter_context(nc.psum_tensor(f"wa_{n}", shape, F32))

        new_sem = c.enter_context(stage_semaphores(nc))

        def sem(n):
            return new_sem(f"wa_{n}")

        xn = sb("xn", [P, 2, P])
        xt = sb("xt", [P, 2, P])
        rot = [sb(f"rot{n}", [P, H1, 2, HALF]) for n in range(2)]
        cross = [sb(f"cross{n}", [P, H1, 2, HALF]) for n in range(2)]
        qt = sb("qt", [P, 2, PAIRS, P])
        kbd = sb("kbd", [P, 2, PAIRS, 2, P])
        vbd = sb("vbd", [P, 4, 2, PAIRS, 2, D1])
        sd = sb("sd", [P, 4, H1, SEQ])
        mx = sb("mx", [P, 4, H1])
        total = sb("total", [P, 2, H1])
        rec = sb("rec", [P, 2, H1])
        pt = sb("pt", [P, 2, PAIRS, P])
        o_sb = sb("o", [P, 2, H1, D1])
        ot = sb("ot", [P, 2, PAIRS, P])
        xb = sb("xb", [P, 2, P])
        row = sb("row", [P, 2, P])
        st = sb("st", [P, 2, 6])
        rest_st = sb("rest_st", [P, 2, GROUP, 6])
        mv = sb("mv", [P, 2, 2])

        ps_p = ps("ps_p", [P, 2, 512])
        ps_t = ps("ps_t", [P, PAIRS, P])
        ps_s = ps("ps_s", [P, H1, SEQ])
        ps_o = ps("ps_o", [P, 2, 512])

        newton = sem("newton")
        rest_sums, rest_ready, rest_newton = sem("rest_sums"), sem("rest_ready"), sem("rest_newton")
        setup = sem("setup")
        xn_ready, xt_made, xt_ready = sem("xn_ready"), sem("xt_made"), sem("xt_ready")
        qk_made = [sem("q_made"), sem("k_made")]
        crossed = [sem("q_crossed"), sem("k_crossed")]
        rotated = [sem("q_rotated"), sem("k_rotated")]
        qk_t_made = [sem("qt_made"), sem("kt_made")]
        qk_t_ready = [sem("qt_ready"), sem("kt_ready")]
        v_made, v_ready = sem("v_made"), sem("v_ready")
        s_made, mx_ready, s_taken, p_ready = sem("s_made"), sem("mx_ready"), sem("s_taken"), sem("p_ready")
        sub_ready = sem("sub_ready")
        total_ready, rec_ready = sem("total_ready"), sem("rec_ready")
        pt_made, pt_ready = sem("pt_made"), sem("pt_ready")
        o_made, o_ready, ot_made, ot_ready = sem("o_made"), sem("o_ready"), sem("ot_made"), sem("ot_ready")
        y_made, xb_ready, x_added = sem("y_made"), sem("xb_ready"), sem("x_added")
        st_ready, mv_ready, mv_kept = sem("st_ready"), sem("mv_ready"), sem("mv_kept")

        TURNS = [("o", 4, ot_ready), ("q", 1, qk_t_ready[0]), ("p", 3, pt_ready),
                 ("k", 1, qk_t_ready[1])]

        def wait_for_turn(pe, user, i):
            at = [n for n, _, _ in TURNS].index(user)
            for back in range(1, 4 * len(TURNS)):
                steps, n = divmod(at - back, len(TURNS))
                _, behind, copied = TURNS[n]
                t = i + steps - behind
                if has(t, NT):
                    pe.wait_ge(copied, t + 1)
                    return

        nc.scalar.preload_act_table(ACT.Exp)
        block = c.enter_context(nc.Block())

        @block.gpsimd
        def _(pool):
            pool.memset(vbd[:], 0.0)
            pool.memset(kbd[:], 0.0).then_inc(setup, 1)

            def rotate(n):
                def stage(t, v):
                    pool.wait_ge(crossed[n], t + 1)
                    pool.tensor_tensor(rot[n][:], rot[n][:], cross[n][:], ALU.add).then_inc(rotated[n], 1)
                return stage

            def subtract_max(t, v):
                pool.wait_ge(mx_ready, t + 1)
                pool.tensor_tensor(sd[:, v], sd[:, v], mx[:, v].unsqueeze(2).to_broadcast([P, H1, SEQ]),
                                   ALU.subtract).then_inc(sub_ready, 1)

            def add_bias(t, v):
                if late(t, 2):
                    pool.wait_ge(x_added, t - 1)
                pool.tensor_tensor(xb[:, v % 2], k.x_res[:, t], k.l1_bo[:], ALU.add).then_inc(xb_ready, 1)

            def step(i, u):
                for stage, behind in ((rotate(0), 1), (subtract_max, 2), (rotate(1), 1), (add_bias, 3)):
                    if has(i - behind, NT):
                        stage(i - behind, (u - behind) % UNROLL)

            pipeline(pool, NT, step, 3, UNROLL, 3 * UNROLL)

        @block.tensor
        def _(pe):
            def x_transpose(i, t, v):
                pe.wait_ge(xn_ready, t + 1)
                pe.transpose(ps_o[:, 1, 0:P], xn[:, v % 2], k.ident[:]).then_inc(xt_made, 1)

            def project(n):
                def stage(i, t, v):
                    if n == 0:
                        pe.wait_ge(xt_ready, t + 1)
                        if late(t, 1):
                            pe.wait_ge(v_ready, t)
                    else:
                        pe.wait_ge(crossed[0], t + 1)
                    weight = (k.l1_wq, k.l1_wk)[n]
                    for half in range(2):
                        mm = pe.matmul(ps_p[:, half], xt[:, v % 2], weight[:, half * 512:(half + 1) * 512],
                                       start=True, stop=True)
                    mm.then_inc(qk_made[n], 1)
                return stage

            def project_v(i, t, v):
                pe.wait_ge(crossed[1], t + 1)
                for b in range(2):
                    for half in range(2):
                        mm = pe.matmul(ps_p[half * SEQ:(half + 1) * SEQ, b], xt[:, v % 2, b * SEQ:(b + 1) * SEQ],
                                       k.l1_wv[:, half], start=True, stop=True)
                mm.then_inc(v_made, 1)

            def qk_transpose(n):
                def stage(i, t, v):
                    pe.wait_ge(rotated[n], t + 1)
                    wait_for_turn(pe, "qk"[n], i)
                    flat = rot[n][:].rearrange("p (n h) s d -> p n (h s d)", h=2)
                    for m in range(PAIRS):
                        mm = pe.transpose(ps_t[:, m], flat[:, m], k.ident[:])
                    mm.then_inc(qk_t_made[n], 1)
                return stage

            def scores(i, t, v):
                pe.wait_ge(qk_t_ready[0], t + 1)
                pe.wait_ge(qk_t_ready[1], t + 1)
                if late(t, 1):
                    pe.wait_ge(s_taken, t)
                for m in range(PAIRS):
                    for b in range(2):
                        rows = slice(b * SEQ, (b + 1) * SEQ)
                        mm = pe.matmul(ps_s[rows, 2 * m:2 * m + 2], qt[:, v % 2, m, rows], kbd[:, v % 2, m, :, rows],
                                       start=True, stop=True)
                mm.then_inc(s_made, 1)

            def p_transpose(i, t, v):
                pe.wait_ge(p_ready, t + 1)
                wait_for_turn(pe, "p", i)
                flat = sd[:, v].rearrange("p (n h) s -> p n (h s)", h=2)
                for m in range(PAIRS):
                    mm = pe.transpose(ps_t[:, m], flat[:, m], k.ident[:])
                mm.then_inc(pt_made, 1)

            def values(i, t, v):
                pe.wait_ge(pt_ready, t + 1)
                pe.wait_ge(v_ready, t + 1)
                if late(t, 1):
                    pe.wait_ge(x_added, t)
                if has(i, NT):
                    pe.wait_ge(xt_ready, i + 1)
                for m in range(PAIRS):
                    for b in range(2):
                        rows = slice(b * SEQ, (b + 1) * SEQ)
                        mm = pe.matmul(ps_o[rows, m // 4, m % 4 * P:(m % 4 + 1) * P], pt[:, v % 2, m, rows], vbd[:, v, b, m],
                                       start=True, stop=True)
                mm.then_inc(o_made, 1)

            def o_transpose(i, t, v):
                pe.wait_ge(o_ready, t + 1)
                wait_for_turn(pe, "o", i)
                flat = o_sb[:, v % 2].rearrange("p (n h) d -> p n (h d)", h=2)
                for m in range(PAIRS):
                    mm = pe.transpose(ps_t[:, m], flat[:, m], k.ident[:])
                mm.then_inc(ot_made, 1)

            def out_project(i, t, v):
                pe.wait_ge(ot_ready, t + 1)
                for m in range(PAIRS):
                    mm = pe.matmul(ps_o[:, 0, 0:P], ot[:, v % 2, m], k.l1_wo[:, m], start=(m == 0), stop=(m == PAIRS - 1))
                mm.then_inc(y_made, 1)

            def step(i, u):
                for stage, behind in ((project(0), 1), (o_transpose, 4), (scores, 2), (project(1), 1),
                                      (qk_transpose(0), 1), (out_project, 4), (x_transpose, 0), (p_transpose, 3),
                                      (project_v, 1), (qk_transpose(1), 1), (values, 3)):
                    if has(i - behind, NT):
                        stage(i, i - behind, (u - behind) % UNROLL)

            pipeline(pe, NT, step, 4, UNROLL, 3 * UNROLL)

        @block.scalar
        def _(act):
            def x_copy(t, v):
                act.wait_ge(xt_made, t + 1)
                if late(t, 2):
                    act.wait_ge(v_made, t - 1)
                act.copy(xt[:, v % 2], ps_o[:, 1, 0:P]).then_inc(xt_ready, 1)

            def q_copy(t, v):
                act.wait_ge(qk_t_made[0], t + 1)
                if late(t, 2):
                    act.wait_ge(s_made, t - 1)
                act.copy(qt[:, v % 2], ps_t[:]).then_inc(qk_t_ready[0], 1)

            def k_copy(t, v):
                act.wait_ge(qk_t_made[1], t + 1)
                act.copy(kbd[0:SEQ, v % 2, :, 0], ps_t[0:SEQ])
                act.copy(kbd[SEQ:P, v % 2, :, 1], ps_t[SEQ:P]).then_inc(qk_t_ready[1], 1)

            def v_copy(t, v):
                if not late(t, 1):
                    act.wait_ge(setup, 1)
                act.wait_ge(v_made, t + 1)
                if late(t, 4):
                    act.wait_ge(o_made, t - 3)
                for half in range(2):
                    rows = slice(half * SEQ, (half + 1) * SEQ)
                    op = act.copy(vbd[rows, v, :, :, half], ps_p[rows].rearrange("p b (n d) -> p b n d", d=D1))
                op.then_inc(v_ready, 1)

            def exponential(t, v):
                act.wait_ge(sub_ready, t + 1)
                act.activation(sd[:, v], sd[:, v], ACT.Exp, scale=scale).then_inc(p_ready, 1)

            def p_copy(t, v):
                act.wait_ge(pt_made, t + 1)
                if late(t, 2):
                    act.wait_ge(o_made, t - 1)
                act.copy(pt[:, v % 2], ps_t[:]).then_inc(pt_ready, 1)

            def o_copy(t, v):
                act.wait_ge(ot_made, t + 1)
                if late(t, 2):
                    act.wait_ge(y_made, t - 1)
                act.copy(ot[:, v % 2], ps_t[:]).then_inc(ot_ready, 1)

            def step(i, u):
                for stage, behind in ((o_copy, 4), (q_copy, 1), (x_copy, 0), (exponential, 2), (p_copy, 3),
                                      (v_copy, 1), (k_copy, 1)):
                    if has(i - behind, NT):
                        stage(i - behind, (u - behind) % UNROLL)

            pipeline(act, NT, step, 4, UNROLL, 3 * UNROLL)

        @block.vector
        def _(dve):
            def normalise(t, v):
                if late(t, 2):
                    dve.wait_ge(xt_made, t - 1)
                dve.tensor_scalar(xn[:, v % 2], k.x_res[:, t], k.ln_scale[:, bass.ds(t, 1)], k.ln_shift[:, bass.ds(t, 1)],
                                  ALU.mult, ALU.add).then_inc(xn_ready, 1)

            def rotate(n):
                def stage(t, v):
                    dve.wait_ge(qk_made[n], t + 1)
                    if late(t, 1):
                        dve.wait_ge(qk_t_made[n], t)
                    src = ps_p[:].rearrange("p b (h s d) -> p (b h) s d", s=2, d=HALF)
                    dve.tensor_tensor(rot[n][:].rearrange("p h s d -> p (h s) d"), src.rearrange("p h s d -> p (h s) d"),
                                      bc(k.cos[:], 1, 2 * H1), ALU.mult)
                    dve.tensor_tensor(cross[n][:, :, 0], src[:, :, 1], bc(k.neg_sin[:], 1, H1), ALU.mult)
                    dve.tensor_tensor(cross[n][:, :, 1], src[:, :, 0], bc(k.sin[:], 1, H1), ALU.mult)\
                        .then_inc(crossed[n], 1)
                return stage

            def mask_and_max(t, v):
                dve.wait_ge(s_made, t + 1)
                if late(t, 4):
                    dve.wait_ge(pt_made, t - 3)
                    dve.wait_ge(total_ready, t - 3)
                dve.scalar_tensor_tensor(out=sd[:, v], in0=bc(k.future[:], 1, H1), scalar=NEG, in1=ps_s[:],
                                         op0=ALU.mult, op1=ALU.add).then_inc(s_taken, 1)
                dve.wait_ge(s_taken, t + 1)
                dve.tensor_reduce(mx[:, v], sd[:, v], AX.X, ALU.max).then_inc(mx_ready, 1)

            def add_up(t, v):
                dve.wait_ge(p_ready, t + 1)
                if late(t, 2):
                    dve.wait_ge(rec_ready, t - 1)
                dve.tensor_reduce(total[:, v % 2], sd[:, v], AX.X, ALU.add).then_inc(total_ready, 1)
                dve.wait_ge(total_ready, t + 1)
                if late(t, 2):
                    dve.wait_ge(o_ready, t - 1)
                dve.reciprocal(rec[:, v % 2], total[:, v % 2]).then_inc(rec_ready, 1)

            def divide(t, v):
                dve.wait_ge(o_made, t + 1)
                dve.wait_ge(rec_ready, t + 1)
                if late(t, 2):
                    dve.wait_ge(ot_made, t - 1)
                dve.tensor_tensor(o_sb[:, v % 2], ps_o[:].rearrange("p b (h d) -> p (b h) d", d=D1),
                                  rec[:, v % 2].unsqueeze(2).to_broadcast([P, H1, D1]), ALU.mult).then_inc(o_ready, 1)

            def residual(t, v):
                dve.wait_ge(xb_ready, t + 1)
                dve.wait_ge(y_made, t + 1)
                if late(t, 2):
                    dve.wait_ge(mv_kept, t - 1)
                dve.tensor_tensor(row[:, v % 2], ps_o[:, 0, 0:P], xb[:, v % 2], ALU.add).then_inc(x_added, 1)
                dve.wait_ge(x_added, t + 1)
                keep_with_stats(dve, row[:, v % 2], k.x_res[:, t], st[:, v % 2], mv[:, v % 2], k.mean_var[:, t], t,
                                st_ready, mv_ready, mv_kept)

            rest = LoadedStats(dve, k, rest_st, (rest_sums, rest_ready, rest_newton), 1, 32)

            def step(i, u):
                for stage, behind in ((rotate(0), 1), (normalise, 0), (mask_and_max, 2), (rotate(1), 1),
                                      (add_up, 3), (residual, 4), (divide, 3)):
                    if has(i - behind, NT):
                        stage(i - behind, (u - behind) % UNROLL)
                if isinstance(i, int) and 3 <= i <= 3 + rest.count:
                    rest.step(i - 3)

            pipeline(dve, NT, step, 4, UNROLL, 3 * UNROLL)
            dve.wait_ge(mv_kept, NT)
            layer_norm_scales(dve, k, k.mean_var, k.ln_scale[:], k.ln_shift[:], newton)


def context_scores(nc, k):
    NT = k.tiles
    NG = NT // GROUP
    with ExitStack() as c:
        def sb(n, shape, dt=F32):
            return c.enter_context(nc.sbuf_tensor(f"cs_{n}", shape, dt))

        new_sem = c.enter_context(stage_semaphores(nc))

        def sem(n):
            return new_sem(f"cs_{n}")

        ROWS = [P, 2, GROUP, P]
        xn, prod, att, e = sb("xn", ROWS), sb("prod", ROWS), sb("att", ROWS), sb("e", ROWS)
        cs = sb("cs", ROWS)
        ctx_t = sb("ctx_t", ROWS)
        COLUMN = [P, 2, GROUP]
        own = sb("own", COLUMN)
        neg_mx, total, rec = sb("neg_mx", COLUMN), sb("total", COLUMN), sb("rec", COLUMN)
        ps_x = [c.enter_context(nc.psum_tensor(f"cs_x{n}", [P, GROUP, P], F32)) for n in range(2)]
        ps_s = [c.enter_context(nc.psum_tensor(f"cs_s{n}", [P, GROUP, P], F32)) for n in range(2)]
        ps_a = [c.enter_context(nc.psum_tensor(f"cs_a{n}", [P, GROUP, P], F32)) for n in range(2)]
        ctx_loaded = [sem(f"ctx_loaded{n}") for n in range(2)]
        xn_ready, prod_ready, own_ready, xt_made = sem("xn_ready"), sem("prod_ready"), sem("own_ready"), sem("xt_made")
        cs_ready, s_made, mx_ready, e_ready = sem("cs_ready"), sem("s_made"), sem("mx_ready"), sem("e_ready")
        rec_ready, att_ready, at_made, at_ready = sem("rec_ready"), sem("att_ready"), sem("at_made"), sem("at_ready")
        max_kept, b3_ready = sem("max_kept"), sem("b3_ready")
        nc.scalar.preload_act_table(ACT.Exp)
        block = c.enter_context(nc.Block())

        @block.sync
        def _(sp):
            def step(g, u):
                if late(g, 2):
                    sp.wait_ge(s_made, g - 1)
                sp.dma_start(ctx_t[:, u], k.in_ctx_t[group(g)].rearrange("n p c -> p n c")).then_inc(ctx_loaded[u], 16)

            group_pipeline(sp, NT, step, 0)
            issue_loads(sp, k.later_loads, k.ffn_loaded)

        @block.gpsimd
        def _(pool):
            def step(g, u):
                pool.wait_ge(xn_ready, g + 1)
                if late(g, 2):
                    pool.wait_ge(own_ready, g - 1)
                pool.tensor_tensor(prod[:, u], xn[:, u], bc(k.l1_wc[:], 1, GROUP), ALU.mult).then_inc(prod_ready, 1)

            group_pipeline(pool, NT, step, 0)

        @block.tensor
        def _(pe):
            def step(i, u):
                if has(i, NG):
                    pe.wait_ge(xn_ready, i + 1)
                    if late(i, 2):
                        pe.wait_ge(cs_ready, i - 1)
                    for n in range(GROUP):
                        mm = pe.transpose(ps_x[u][:, n], xn[:, u, n], k.ident[:])
                    mm.then_inc(xt_made, 1)
                g, v = i - 1, 1 - u
                if has(g, NG):
                    pe.wait_ge(cs_ready, g + 1)
                    pe.wait_ge(ctx_loaded[v], 16 + 8 * (g - v))
                    if late(g, 2):
                        pe.wait_ge(e_ready, g - 1)
                    pe.matmul(ps_s[v][:], k.neg_ident[:], bc(k.other_seq[:], 1, GROUP), start=True, stop=True)
                    for n in range(GROUP):
                        mm = pe.matmul(ps_s[v][:, n], cs[:, v, n], ctx_t[:, v, n], start=False, stop=True,
                                       skip_group_check=True)
                    mm.then_inc(s_made, 1)
                g, v = i - 3, 1 - u
                if has(g, NG):
                    pe.wait_ge(att_ready, g + 1)
                    if late(g, 2):
                        pe.wait_ge(at_ready, g - 1)
                    for n in range(GROUP):
                        mm = pe.transpose(ps_a[v][:, n], att[:, v, n], k.ident[:])
                    mm.then_inc(at_made, 1)

            group_pipeline(pe, NT, step, 3)

        @block.scalar
        def _(act):
            def step(i, u):
                if has(i, NG):
                    act.wait_ge(xt_made, i + 1)
                    if late(i, 2):
                        act.wait_ge(s_made, i - 1)
                    act.activation(cs[:, u], ps_x[u][:], ACT.Identity, scale=k.l1_wcq[:], bias=k.l1_wq_col[:])\
                        .then_inc(cs_ready, 1)
                g, v = i - 2, u
                if has(g, NG):
                    act.wait_ge(mx_ready, g + 1)
                    if late(g, 2):
                        act.wait_ge(att_ready, g - 1)
                    for n in range(GROUP):
                        op = act.activation(e[:, v, n], ps_s[v][:, n], ACT.Exp, bias=neg_mx[:, v, n:n + 1],
                                            accum_out=total[:, v, n:n + 1])
                    op.then_inc(e_ready, 1)
                g, v = i - 3, 1 - u
                if has(g, NG):
                    act.wait_ge(at_made, g + 1)
                    act.copy(k.at_all[:, group(g)], ps_a[v][:]).then_inc(at_ready, 1)

            group_pipeline(act, NT, step, 3)

        @block.vector
        def _(dve):
            dve.tensor_reduce(k.l1_b3[:], k.l1_b3_parts[:], AX.X, ALU.add).then_inc(b3_ready, 1)
            dve.wait_ge(b3_ready, 1)

            def step(i, u):
                if has(i, NG):
                    if late(i, 2):
                        dve.wait_ge(xt_made, i - 1)
                        dve.wait_ge(prod_ready, i - 1)
                    normalise_group(dve, k, i, xn[:, u]).then_inc(xn_ready, 1)
                g, v = i - 2, u
                if has(g, NG):
                    dve.wait_ge(s_made, g + 1)
                    if late(g, 2):
                        dve.wait_ge(max_kept, g - 1)
                    dve.tensor_reduce(neg_mx[:, v], ps_s[v][:], AX.X, ALU.max, negate=True).then_inc(mx_ready, 1)
                g, v = i - 3, 1 - u
                if has(g, NG):
                    dve.wait_ge(e_ready, g + 1)
                    dve.reciprocal(rec[:, v], total[:, v]).then_inc(rec_ready, 1)
                g, v = i - 3, 1 - u
                if has(g, NG):
                    dve.wait_ge(rec_ready, g + 1)
                    if late(g, 2):
                        dve.wait_ge(at_made, g - 1)
                    dve.tensor_tensor(att[:, v], e[:, v], rec[:, v].unsqueeze(2).to_broadcast([P, GROUP, P]),
                                      ALU.mult).then_inc(att_ready, 1)
                g, v = i - 2, u
                if has(g, NG):
                    dve.wait_ge(prod_ready, g + 1)
                    dve.tensor_reduce(own[:, v], prod[:, v], AX.X, ALU.add).then_inc(own_ready, 1)
                g, v = i - 2, u
                if has(g, NG):
                    dve.wait_ge(mx_ready, g + 1)
                    dve.wait_ge(own_ready, g + 1)
                    dve.scalar_tensor_tensor(out=k.row_max[:, group(g)], in0=own[:, v], scalar=k.l1_b3[:],
                                             in1=neg_mx[:, v], op0=ALU.add, op1=ALU.subtract).then_inc(max_kept, 1)

            group_pipeline(dve, NT, step, 3)


def token_weights(nc, k):
    NT = k.tiles
    with ExitStack() as c:
        def sb(n, shape):
            return c.enter_context(nc.sbuf_tensor(f"tw_{n}", shape, F32))

        new_sem = c.enter_context(stage_semaphores(nc))

        def sem(n):
            return new_sem(f"tw_{n}")

        e = sb("e", [NT, 2, SEQ])
        mx = sb("mx", [NT, 2])
        rec = sb("rec", [NT, 2])
        ps_m = c.enter_context(nc.psum_tensor("tw_m", [P, 512], F32))
        ps_w = c.enter_context(nc.psum_tensor("tw_w", [P, 512], F32))
        m_made, sub_ready, e_ready, w_ready, w_made, op_done = (sem(n) for n in ("m_made", "sub_ready", "e_ready", "w_ready",
                                                                              "w_made", "op_done"))
        block = c.enter_context(nc.Block())

        @block.tensor
        def _(pe):
            pe.transpose(ps_m[0:NT, 0:P], k.row_max[:], k.ident[:]).then_inc(m_made, 1)
            pe.wait_ge(w_ready, 1)
            pe.transpose(ps_w[:, 0:NT], e[:].rearrange("n b s -> n (b s)"), k.ident[0:NT, 0:NT]).then_inc(w_made, 1)

        @block.scalar
        def _(act):
            act.wait_ge(sub_ready, 1)
            act.activation(e[:], e[:], ACT.Exp).then_inc(e_ready, 1)

        @block.vector
        def _(dve):
            rows = ps_m[0:NT, 0:P].rearrange("n (b s) -> n b s", b=2)
            dve.wait_ge(m_made, 1)
            dve.tensor_reduce(mx[:], rows, AX.X, ALU.max).then_inc(op_done, 1)
            dve.wait_ge(op_done, 1)
            dve.tensor_tensor(e[:], rows, mx[:].unsqueeze(2).to_broadcast([NT, 2, SEQ]), ALU.subtract)\
                .then_inc(sub_ready, 1)
            dve.wait_ge(e_ready, 1)
            dve.tensor_reduce(mx[:], e[:], AX.X, ALU.add).then_inc(op_done, 1)
            dve.wait_ge(op_done, 2)
            dve.reciprocal(rec[:], mx[:]).then_inc(op_done, 1)
            dve.wait_ge(op_done, 3)
            dve.tensor_tensor(e[:], e[:], rec[:].unsqueeze(2).to_broadcast([NT, 2, SEQ]), ALU.mult).then_inc(w_ready, 1)
            dve.wait_ge(w_made, 1)
            dve.tensor_copy(k.token_w[:], ps_w[:, 0:NT])


def context_mix(nc, k):
    NT = k.tiles
    NG = NT // GROUP
    with ExitStack() as c:
        def sb(n, shape, dt=F32):
            return c.enter_context(nc.sbuf_tensor(f"cm_{n}", shape, dt))

        new_sem = c.enter_context(stage_semaphores(nc))

        def sem(n):
            return new_sem(f"cm_{n}")

        ROWS = [P, 2, GROUP, P]
        ctx, xn, xb, row = sb("ctx", ROWS), sb("xn", ROWS), sb("xb", ROWS), sb("row", ROWS)
        wb = sb("wb", ROWS)
        feat = sb("feat", [P, 2, 4, GROUP, P])
        st = sb("st", [P, 2, GROUP, 6])
        mv = sb("mv", [P, 2, GROUP, 2])
        ps_x, ps_c, ps_q, ps_z = ([c.enter_context(nc.psum_tensor(f"cm_{q}{n}", [P, GROUP, P], F32)) for n in range(2)]
                                  for q in "xcqz")
        ctx_loaded = [sem(f"ctx_loaded{n}") for n in range(2)]
        xn_ready, wb_ready, xt_made, c_ready = sem("xn_ready"), sem("wb_ready"), sem("xt_made"), sem("c_ready")
        c2q_made, c2q_ready, q2c_made = sem("c2q_made"), sem("c2q_ready"), sem("q2c_made")
        c_c2q_ready, c_q2c_ready, z_made = sem("c_c2q_ready"), sem("c_q2c_ready"), sem("z_made")
        newton = sem("newton")
        xb_ready, x_added, row_kept = sem("xb_ready"), sem("x_added"), sem("row_kept")
        st_ready, mv_ready, mv_kept = sem("st_ready"), sem("mv_ready"), sem("mv_kept")
        block = c.enter_context(nc.Block())

        @block.sync
        def _(sp):
            def step(g, u):
                if late(g, 2):
                    sp.wait_ge(c2q_made, g - 1)
                sp.dma_start(ctx[:, u], k.in_ctx[group(g)].rearrange("n p c -> p n c")).then_inc(ctx_loaded[u], 16)

            group_pipeline(sp, NT, step, 0)
            sp.wait_ge(k.ffn_loaded, 16 * len(k.later_loads))

        @block.gpsimd
        def _(pool):
            def step(i, u):
                if has(i, NG):
                    if late(i, 2):
                        pool.wait_ge(q2c_made, i - 1)
                    pool.tensor_tensor(wb[:, u], bc(k.same_seq[:], 1, GROUP),
                                       k.token_w[:, group(i)].unsqueeze(2).to_broadcast([P, GROUP, P]), ALU.mult)\
                        .then_inc(wb_ready, 1)
                g, v = i - 1, 1 - u
                if has(g, NG):
                    pool.wait_ge(c2q_ready, g + 1)
                    pool.tensor_tensor(feat[:, v, 2], feat[:, v, 1], feat[:, v, 0], ALU.mult).then_inc(c_c2q_ready, 1)
                    if late(g, 2):
                        pool.wait_ge(x_added, g - 1)
                    pool.tensor_tensor(xb[:, v], k.x_res[:, group(g)], bc(k.l1_bl[:], 1, GROUP), ALU.add)\
                        .then_inc(xb_ready, 1)

            group_pipeline(pool, NT, step, 1)

        @block.tensor
        def _(pe):
            def step(i, u):
                if has(i, NG):
                    pe.wait_ge(xn_ready, i + 1)
                    if late(i, 2):
                        pe.wait_ge(c_ready, i - 1)
                    for n in range(GROUP):
                        mm = pe.transpose(ps_x[u][:, n], xn[:, u, n], k.ident[:])
                    mm.then_inc(xt_made, 1)
                g, v = i - 2, u
                if has(g, NG):
                    pe.wait_ge(c_c2q_ready, g + 1)
                    pe.wait_ge(c_q2c_ready, g + 1)
                    if late(g, 2):
                        pe.wait_ge(x_added, g - 1)
                    for n in range(GROUP):
                        for f in range(4):
                            mm = pe.matmul(ps_z[v][:, n], feat[:, v, f, n], k.l1_wl[:, f], start=(f == 0), stop=(f == 3))
                    mm.then_inc(z_made, 1)
                if has(i, NG):
                    pe.wait_ge(ctx_loaded[u], 16 + 8 * (i - u))
                    if late(i, 2):
                        pe.wait_ge(c2q_ready, i - 1)
                    for n in range(GROUP):
                        mm = pe.matmul(ps_c[u][:, n], ctx[:, u, n], k.at_all[:, i * GROUP + n], start=True, stop=True)
                    mm.then_inc(c2q_made, 1)
                    pe.wait_ge(wb_ready, i + 1)
                    if late(i, 2):
                        pe.wait_ge(c_q2c_ready, i - 1)
                    for n in range(GROUP):
                        mm = pe.matmul(ps_q[u][:, n], xn[:, u, n], wb[:, u, n], start=True, stop=True)
                    mm.then_inc(q2c_made, 1)

            group_pipeline(pe, NT, step, 2)

        @block.scalar
        def _(act):
            def step(i, u):
                if has(i, NG):
                    act.wait_ge(xt_made, i + 1)
                    if late(i, 2):
                        act.wait_ge(z_made, i - 1)
                    act.copy(feat[:, u, 0], ps_x[u][:]).then_inc(c_ready, 1)
                    act.wait_ge(c2q_made, i + 1)
                    act.copy(feat[:, u, 1], ps_c[u][:]).then_inc(c2q_ready, 1)
                g, v = i - 3, 1 - u
                if has(g, NG):
                    act.wait_ge(x_added, g + 1)
                    act.copy(k.x_res[:, group(g)], row[:, v]).then_inc(row_kept, 1)

            group_pipeline(act, NT, step, 3)

        @block.vector
        def _(dve):
            stats = GroupStats(dve, NT, row, k.mean_var, st, mv, st_ready, mv_ready, mv_kept)

            def step(i, u):
                if has(i, NG):
                    if late(i, 2):
                        dve.wait_ge(q2c_made, i - 1)
                    normalise_group(dve, k, i, xn[:, u]).then_inc(xn_ready, 1)
                g, v = i - 1, 1 - u
                if has(g, NG):
                    dve.wait_ge(c_ready, g + 1)
                    dve.wait_ge(q2c_made, g + 1)
                    if late(g, 2):
                        dve.wait_ge(z_made, g - 1)
                    dve.tensor_tensor(feat[:, v, 3], ps_q[v][:], feat[:, v, 0], ALU.mult).then_inc(c_q2c_ready, 1)
                g, v = i - 3, 1 - u
                if has(g, NG):
                    dve.wait_ge(xb_ready, g + 1)
                    dve.wait_ge(z_made, g + 1)
                    if late(g, 2):
                        dve.wait_ge(row_kept, g - 1)
                    dve.tensor_tensor(row[:, v], ps_z[v][:], xb[:, v], ALU.add).then_inc(x_added, 1)
                stats.keep_and_aggregate(i - 4, u)
                if has(g, NG):
                    dve.wait_ge(x_added, g + 1)
                    stats.by_row(g, v)

            group_pipeline(dve, NT, step, 5)
            dve.wait_ge(mv_kept, NT // GROUP)
            layer_norm_scales(dve, k, k.mean_var, k.ln_scale[:], k.ln_shift[:], newton)


def one_expert_ffn(nc, k, out_rows):
    NT = k.tiles
    NS = NT + NE - 1
    FF = 4
    with ExitStack() as c:
        def sb(n, shape, dt=F32):
            return c.enter_context(nc.sbuf_tensor(f"m1_{n}", shape, dt))

        new_sem = c.enter_context(stage_semaphores(nc))

        def sem(n):
            return new_sem(f"m1_{n}")

        WIDTH = k.l1_ffn.shape[2]
        from_row = sb("from_row", [P, 4, 1], U32)
        no_shift = sb("no_shift", [P, 1], U32)
        to_row = sb("to_row", [P, 4, 1], U32)
        xg = sb("xg", [P, 4, 2 * P])
        wt = sb("wt", [P, 4, WIDTH])
        xt = sb("xt", [P, 2, P])
        hid = sb("hid", [P, 2, FF, P])
        xb = sb("xb", [P, 4, P])
        y = sb("y", [P, 4, P])
        w1, b1 = wt[:, :, 0:FF * P], wt[:, :, FF * P:FF * P + FF]
        w2 = wt[:, :, FF * P + FF:2 * FF * P + FF].rearrange("p b (f c) -> p b f c", c=P)
        b2 = wt[:, :, 2 * FF * P + FF:WIDTH]
        ps_x = [c.enter_context(nc.psum_tensor(f"m1_x{n}", [P, 512], F32)) for n in range(2)]
        ps_h = [c.enter_context(nc.psum_tensor(f"m1_h{n}", [P, FF, P], F32)) for n in range(2)]
        ps_y = [c.enter_context(nc.psum_tensor(f"m1_y{n}", [P, 512], F32)) for n in range(2)]
        gathered, scattered = k.gathered1, k.scattered1
        setup = sem("setup")
        from_ready, wt_ready, xt_made, xt_ready = (sem(n) for n in ("from_ready", "wt_ready", "xt_made", "xt_ready"))
        h_made, hid_ready, y_made, xb_ready, y_ready = (sem(n) for n in ("h_made", "hid_ready", "y_made", "xb_ready",
                                                                          "y_ready"))
        nc.scalar.preload_act_table(ACT.Gelu)
        block = c.enter_context(nc.Block())

        @block.gpsimd
        def _(pool):
            def copy_idx(t, v, of_all, to):
                column = of_all[:, bass.ds(t, 1)] if not isinstance(t, int) else of_all[:, t:t + 1]
                return pool.tensor_tensor(to[:, v], column, no_shift[:], ALU.add)

            pool.memset(no_shift[:], 0).then_inc(setup, 1)
            pool.wait_ge(setup, 1)
            copy_idx(0, 0, k.gather_idx, from_row).then_inc(from_ready, 1)

            def step(i, u):
                g, gv = i + 1, (u + 1) % 4
                if has(i, NS):
                    pool.wait_ge(from_ready, i + 1)
                    if late(i, 4):
                        pool.wait_ge(xt_made, i - 3)
                if has(i - 5, NS):
                    pool.wait_ge(y_ready, i - 4)
                if has(g, NS):
                    if late(g, 4):
                        pool.wait_ge(xb_ready, g - 3)
                    copy_idx(g, gv, k.gather_idx, from_row).then_inc(from_ready, 1)
                if has(i, NS):
                    pool.indirect_dma_start(xg[:, u], None, k.xx_rows,
                                            bass.IndirectOffsetOnAxis(ap=from_row[:, u], axis=0)).then_inc(gathered[u], 16)
                if has(i - 5, NS):
                    pool.indirect_dma_start(out_rows, bass.IndirectOffsetOnAxis(ap=to_row[:, (u - 1) % 4], axis=0),
                                            y[:, (u - 1) % 4], None, bounds_check=NT * P - 1, oob_is_err=False)\
                        .then_inc(scattered[(u - 1) % 4], 16)

            pipeline(pool, NS, step, 5)
            for n in range(4):
                pool.wait_ge(scattered[n], 16 * len(range(n, NS, 4)))

        @block.tensor
        def _(pe):
            def step(i, u):
                t, v = i - 2, (u - 2) % 4
                if has(t, NS):
                    pe.wait_ge(gathered[v], 16 + 4 * (t - v))
                    if late(t, 2):
                        pe.wait_ge(xt_ready, t - 1)
                    pe.transpose(ps_x[v % 2][:, 0:P], xg[:, v, P:2 * P], k.ident[:]).then_inc(xt_made, 1)
                t, v = i - 3, (u - 3) % 4
                if has(t, NS):
                    pe.wait_ge(xt_ready, t + 1)
                    pe.wait_ge(wt_ready, t + 1)
                    if late(t, 2):
                        pe.wait_ge(hid_ready, t - 1)
                    for f in range(FF):
                        mm = pe.matmul(ps_h[v % 2][:, f], w1[:, v, f * P:(f + 1) * P], xt[:, v % 2], start=True, stop=True)
                    mm.then_inc(h_made, 1)
                t, v = i - 4, u
                if has(t, NS):
                    pe.wait_ge(hid_ready, t + 1)
                    if late(t, 2):
                        pe.wait_ge(y_ready, t - 1)
                    for f in range(FF):
                        mm = pe.matmul(ps_y[v % 2][:, 0:P], hid[:, v % 2, f], w2[:, v, f], start=(f == 0), stop=(f == FF - 1))
                    mm.then_inc(y_made, 1)

            pipeline(pe, NS, step, 4)

        @block.scalar
        def _(act):
            def step(i, u):
                t, v = i - 2, (u - 2) % 4
                if has(t, NS):
                    act.wait_ge(xt_made, t + 1)
                    if late(t, 2):
                        act.wait_ge(h_made, t - 1)
                    act.copy(xt[:, v % 2], ps_x[v % 2][:, 0:P]).then_inc(xt_ready, 1)
                t, v = i - 3, (u - 3) % 4
                if has(t, NS):
                    act.wait_ge(h_made, t + 1)
                    if late(t, 2):
                        act.wait_ge(y_made, t - 1)
                    for f in range(FF):
                        op = act.activation(hid[:, v % 2, f], ps_h[v % 2][:, f], ACT.Gelu, bias=b1[:, v, f:f + 1])
                    op.then_inc(hid_ready, 1)

            pipeline(act, NS, step, 3)

        @block.vector
        def _(dve):
            def step(i, u):
                t, v = i - 2, (u - 2) % 4
                if has(t, NS):
                    if late(t, 4):
                        dve.wait_ge(y_ready, t - 3)
                        dve.wait_ge(hid_ready, t - 3)
                        dve.wait_ge(y_made, t - 3)
                    expert = dve.value_load(k.tile_expert[0:1, bass.ds(t, 1)], min_val=0, max_val=NE - 1)
                    dve.tensor_scalar(wt[:, v], k.l1_ffn[:, expert], 1.0, None, ALU.mult).then_inc(wt_ready, 1)
                    dve.wait_ge(wt_ready, t + 1)
                    dve.wait_ge(gathered[v], 16 + 4 * (t - v))
                    dve.tensor_tensor(xb[:, v], xg[:, v, 0:P], b2[:, v], ALU.add).then_inc(xb_ready, 1)
                t, v = i - 4, u
                if has(t, NS):
                    dve.wait_ge(xb_ready, t + 1)
                    if late(t, 4):
                        dve.wait_ge(scattered[v], 4 * (t - v))
                    dve.wait_ge(y_made, t + 1)
                    dve.tensor_scalar(to_row[:, v], k.scatter_idx[:, bass.ds(t, 1)], 1.0, None, ALU.mult)
                    dve.tensor_tensor(y[:, v], ps_y[v % 2][:, 0:P], xb[:, v], ALU.add).then_inc(y_ready, 1)

            pipeline(dve, NS, step, 4)


def issue_loads(queue, loads, loaded):
    for tile, src in loads:
        queue.dma_start(tile, src).then_inc(loaded, 16)


def build(nc, a):
    NT = a["x"].shape[0]
    k = Kept(NT)
    with ExitStack() as outer:
        new_sem = outer.enter_context(stage_semaphores(nc))
        k.gathered0 = [new_sem(f"gathered0_{n}") for n in range(NE * CAP // P)]
        k.added0 = [new_sem(f"added0_{e}") for e in range(NE)]
        k.gathered1 = [new_sem(f"gathered1_{n}") for n in range(4)]
        k.scattered1 = [new_sem(f"scattered1_{n}") for n in range(4)]
        k.x_loaded = [new_sem(f"x_loaded{g}") for g in range(NT // GROUP)]
        k.ffn_loaded = new_sem("ffn_loaded")

        def res(n, shape, dt=F32, src=None, stack=outer, loads=None):
            t = stack.enter_context(nc.sbuf_tensor(n, shape, dt))
            if src is not None:
                loads.append((t[:], src))
            return t

        def rows(n):
            return a[n].to_broadcast([P, a[n].shape[1]])

        k.in_x, k.in_mask, k.in_ctx_t, k.in_dist, k.in_dd = a["x"], a["mask"], a["ctx_t"], a["dist"], a["dd"]
        k.in_ctx, k.xx_dram = a["ctx"], a["xx_dram"]
        k.xx_rows = k.xx_dram.rearrange("n p c -> (n p) c")
        k.x_dram, k.xn_dram = a["x_dram"], a["xn_dram"]
        k.x_rows = k.x_dram.rearrange("n p c -> (n p) c")
        k.xn_rows = k.xn_dram.rearrange("n p c -> (n p) c")

        k.first_loads = []
        k.later_loads = []

        def first(n, shape, dt=F32, src=None):
            return res(n, shape, dt, src, outer, k.first_loads)

        def later(n, shape, dt=F32, src=None):
            return res(n, shape, dt, src, outer, k.later_loads)

        k.x_res = first("x_res", [P, NT, P])
        k.mean_var = first("mean_var", [P, NT, 2])
        k.ln_scale = first("ln_scale", [P, NT])
        k.ln_shift = first("ln_shift", [P, NT])
        k.ln_var = first("ln_var", [P, NT])
        k.ln_square = first("ln_square", [P, NT])
        k.ident = first("ident", [P, P], src=a["ident"])
        k.neg_ident = first("neg_ident", [P, P], BF16, src=a["neg_ident"])
        k.future = first("future", [P, SEQ], BF16, src=a["future"])

        slots = NT + NE - 1
        k.logits = later("logits", [P, NT, NE])
        k.iota_e = later("iota_e", [P, NE], src=a["iota"][:, 0:NE].to_broadcast([P, NE]))
        k.iota_cap = later("iota_cap", [P, NE], src=a["iota_cap"].to_broadcast([P, NE]))
        k.iota_s = later("iota_s", [P, P], src=a["iota"][:, 0:P].to_broadcast([P, P]))
        k.iota_s1 = later("iota_s1", [P, NT], src=a["iota"][:, 1:NT + 1].to_broadcast([P, NT]))
        k.place = later("place", [P, 1], src=a["place"])
        k.empty_id = later("empty_id", [P, slots], src=a["empty_id"][:, 0:slots])
        k.before = later("before", [P, P], BF16, src=a["before"])
        k.ones_bf = later("ones_bf", [P, P], BF16, src=a["ones_bf"])
        k.gather_idx = later("gather_idx", [P, slots], U32)
        k.scatter_idx = later("scatter_idx", [P, slots], U32)
        f0_rw = later("f0_rw", [P, NE], src=a["f0_rw"])
        f0_rb = later("f0_rb", [P, NE], src=rows("f0_rb"))
        f1_rw = later("f1_rw", [P, NE], src=a["f1_rw"])
        f1_rb = later("f1_rb", [P, NE], src=rows("f1_rb"))
        k.tile_expert = later("tile_expert", [P, slots], I32)
        k.l1_wq = later("l1_wq", [P, H1 * D1], src=a["l1_wq"])
        k.l1_wk = later("l1_wk", [P, H1 * D1], src=a["l1_wk"])
        k.l1_wv = later("l1_wv", [P, 2, PAIRS * D1], src=a["l1_wv"])
        k.l1_wo = later("l1_wo", [P, PAIRS, P], src=a["l1_wo"])
        k.l1_bo = later("l1_bo", [P, P], src=rows("l1_bo"))
        k.cos = later("cos", [P, D1 // 2], src=a["cos"])
        k.sin = later("sin", [P, D1 // 2], src=a["sin"])
        k.neg_sin = later("neg_sin", [P, D1 // 2], src=a["neg_sin"])
        k.l1_wcq = later("l1_wcq", [P, 1], src=a["l1_wcq"])
        k.l1_wq_col = later("l1_w_q", [P, 1], src=a["l1_w_q"])
        k.l1_wc = later("l1_wc", [P, P], src=rows("l1_wc"))
        k.l1_b3 = later("l1_b3", [P, 1])
        k.l1_b3_parts = later("l1_b3_parts", [P, 3])
        for n, part in enumerate(("l1_b_cq", "l1_b_c", "l1_b_q")):
            k.later_loads.append((k.l1_b3_parts[:, n:n + 1], rows(part)))
        k.l1_wl = later("l1_wl", [P, 4, P], src=a["l1_wl"])
        k.l1_bl = later("l1_bl", [P, P], src=rows("l1_bl"))
        k.same_seq = later("same_seq", [P, P], src=a["same_seq"])
        k.other_seq = later("other_seq", [P, P], BF16, src=a["other_seq"])

        with ExitStack() as moe0:
            def m0(n, shape, dt=F32, src=None):
                return res(n, shape, dt, src, moe0, k.later_loads)

            k.f0_w = m0("f0_w", [P, NE, 2 * P], src=a["f0_w"])
            k.f0_v = m0("f0_v", [P, NE, 2 * P], src=a["f0_v"])
            k.f0_out = m0("f0_out", [P, NE, 2, P], src=a["f0_out"])
            k.w_slot = m0("w_slot", [P, NE * CAP // P])
            with ExitStack() as layer0:
                def r0(n, shape, dt=F32, src=None):
                    return res(n, shape, dt, src, layer0, k.first_loads)
                k.head_mask = r0("head_mask", [P, GRP, 1], src=a["head_mask"])
                k.group_mask = r0("group_mask", [P, GRP, 1], src=a["group_mask"])
                k.a_wq, k.a_wk, k.a_wv, k.a_wo, k.x_wq, k.x_wk, k.x_wv, k.x_wo = (
                    r0(n, [P, P], src=a[n]) for n in ("a_wq", "a_wk", "a_wv", "a_wo", "x_wq", "x_wk", "x_wv", "x_wo"))
                k.a_bq, k.a_bk, k.a_bv, k.x_bq, k.x_bk, k.x_ln_g, k.x_ln_b = (
                    r0(n, [P, 1], src=a[n]) for n in ("a_bq", "a_bk", "a_bv", "x_bq", "x_bk", "x_ln_g", "x_ln_b"))
                k.a_bo = r0("a_bo_rows", [P, P], src=rows("a_bo"))
                k.x_bo = r0("x_bo_rows", [P, P], src=rows("x_bo"))
                k.x_bv_rows = r0("x_bv_rows", [P, P], src=rows("x_bv"))
                k.decay = r0("decay", [P, SEQ])
                k.mask_all = r0("mask_all", [P, NT, SEQ], BF16)
                set_up(nc, k)
                with ExitStack() as mask:
                    k.mask_in = res("mask_in", [P, NT, SEQ], I32, stack=mask)
                    small_head_attention(nc, k, "sa", cross=False)
                k.o_all = res("o_all", [P, NT, P], stack=layer0)
                k.o_mean_var = res("o_mean_var", [P, NT, 2], stack=layer0)
                k.o_scale = res("o_scale", [P, NT], stack=layer0)
                k.o_shift = res("o_shift", [P, NT], stack=layer0)
                small_head_attention(nc, k, "ca", cross=True)
                project_cross(nc, k)
            router(nc, k, "r0", f0_rw, f0_rb, k.xn_dram, None)
            chosen_slots(nc, k, "c0", 2, NE * CAP // P, k.w_slot)
            two_expert_ffn(nc, k)

        wide_head_attention(nc, k)

        k.later_loads = []
        FF = a["f1_w1"].shape[2]
        k.l1_ffn = res("l1_ffn", [P, NE, 2 * FF + FF // P + P])
        at = 0
        for n in ("f1_w1", "f1_b1", "f1_w2", "f1_b2"):
            w = a[n].shape[-1]
            k.later_loads.append((k.l1_ffn[:, :, at:at + w], bc(a[n], 0, P) if n == "f1_b2" else a[n]))
            at += w
        with ExitStack() as context:
            k.at_all = res("at_all", [P, NT, P], stack=context)
            k.row_max = res("row_max", [P, NT], stack=context)
            k.token_w = res("token_w", [P, NT], stack=context)
            context_scores(nc, k)
            token_weights(nc, k)
            context_mix(nc, k)

        router(nc, k, "r1", f1_rw, f1_rb, k.xx_dram[:, :, P:2 * P], k.xx_dram[:, :, 0:P])
        chosen_slots(nc, k, "c1", 1, slots, None)
        one_expert_ffn(nc, k, a["out"].rearrange("n p c -> (n p) c"))


def _layout(v):
    c, f, bf = np.ascontiguousarray, np.float32, mybir.dt.np(BF16)
    B = v["x"].shape[0]
    NT = B * SEQ // P
    i, s = np.arange(P), np.arange(SEQ)
    same = (i // SEQ)[:, None] == (i // SEQ)[None]
    o = {}
    o["dist"] = np.abs((i % SEQ)[:, None] - s[None]).astype(f)
    o["ident"] = np.eye(P, dtype=f)
    o["neg_ident"] = (NEG * np.eye(P)).astype(bf)
    o["future"] = (s[None] > (i % SEQ)[:, None]).astype(bf)
    o["head_mask"] = ((i // D0) % GRP == np.arange(GRP)[:, None]).T.astype(f)[:, :, None]
    o["group_mask"] = (i // (GRP * D0) == np.arange(GRP)[:, None]).T.astype(f)[:, :, None]
    o["iota"] = np.arange(256, dtype=f).reshape(1, 256)
    o["iota_cap"] = (CAP * np.arange(NE) + 1).astype(f).reshape(1, NE)
    o["place"] = i.astype(f).reshape(P, 1)
    o["empty_id"] = (P + NT * P + i[:, None] + P * np.arange(NT + NE)[None]).astype(f)
    o["before"] = (i[:, None] < i[None]).astype(bf)
    o["ones_bf"] = np.ones((P, P), bf)
    o["same_seq"] = same.astype(f)
    o["other_seq"] = (~same).astype(bf)
    freq = (f(1.0) / f(10000.0) ** (np.arange(0, D1, 2, dtype=f) / f(D1))).astype(f)
    angle = (i % SEQ).astype(f)[:, None] * freq[None]
    o["cos"], o["sin"] = np.cos(angle).astype(f), np.sin(angle).astype(f)
    o["neg_sin"] = -o["sin"]
    o["x"] = v["x"].reshape(NT, P, P)
    o["mask"] = v["mask_BxSxS2_ik1"].reshape(NT, P, SEQ)
    o["ctx"] = v["ctx_1024"].reshape(NT, P, P)
    o["ctx_t"] = o["ctx"].transpose(0, 2, 1)
    W, b = v["L0_attn_Wqkv_w"], v["L0_attn_Wqkv_b"]
    for n, q in enumerate("qkv"):
        o["a_w" + q], o["a_b" + q] = W[n * P:(n + 1) * P].T, b[n * P:(n + 1) * P].reshape(P, 1)
    o["dd"] = v["L0_attn_distance_decay"].reshape(1, 1)
    o["a_wo"], o["a_bo"] = v["L0_attn_out_w"].T, v["L0_attn_out_b"].reshape(1, P)

    def repeated(w):
        return np.repeat(w.reshape(H0 // GRP, 1, D0, -1), GRP, axis=1).reshape(P, -1)

    o["x_wq"], o["x_bq"] = v["L0_xattn_Wq"].T, v["L0_xattn_bq"].reshape(P, 1)
    o["x_wk"], o["x_bk"] = repeated(v["L0_xattn_Wk"]).T, repeated(v["L0_xattn_bk"])
    o["x_wv"], o["x_bv"] = repeated(v["L0_xattn_Wv"]).T, repeated(v["L0_xattn_bv"]).reshape(1, P)
    o["x_wo"], o["x_bo"] = v["L0_xattn_Wo"].T, v["L0_xattn_bo"].reshape(1, P)
    o["x_ln_g"], o["x_ln_b"] = v["L0_xattn_ln_g"].reshape(P, 1), v["L0_xattn_ln_b"].reshape(P, 1)
    o["f0_rw"], o["f0_rb"] = v["L0_ffn_router_w"].T, v["L0_ffn_router_b"].reshape(1, NE)
    o["f0_w"], o["f0_v"] = v["L0_ffn_W"].transpose(1, 0, 2), v["L0_ffn_V"].transpose(1, 0, 2)
    o["f0_out"] = v["L0_ffn_W_out"].reshape(NE, 2, P, P).transpose(2, 0, 1, 3)
    halves = np.concatenate([np.arange(0, D1, 2), np.arange(1, D1, 2)])
    for q in "qk":
        o["l1_w" + q] = v["L1_attn_W" + q].reshape(P, H1, D1)[:, :, halves].reshape(P, H1 * D1)
    o["l1_wv"] = v["L1_attn_Wv"].reshape(P, PAIRS, 2, D1).transpose(0, 2, 1, 3).reshape(P, 2, PAIRS * D1)
    o["l1_wo"] = v["L1_attn_Wo"].reshape(PAIRS, P, P).transpose(1, 0, 2)
    o["l1_bo"] = v["L1_attn_bo"].reshape(1, P)
    o["l1_wcq"], o["l1_w_q"] = v["L1_xattn_w_cq"].reshape(P, 1), v["L1_xattn_w_q"].reshape(P, 1)
    o["l1_wc"] = v["L1_xattn_w_c"].reshape(1, P)
    for n in ("b_cq", "b_c", "b_q"):
        o["l1_" + n] = v["L1_xattn_" + n].reshape(1, 1)
    o["l1_wl"] = v["L1_xattn_W_l"].T.reshape(4, P, P).transpose(1, 0, 2)
    o["l1_bl"] = v["L1_xattn_b_l"].reshape(1, P)
    o["f1_rw"], o["f1_rb"] = v["L1_ffn_wr"], v["L1_ffn_br"].reshape(1, NE)
    o["f1_w1"] = v["L1_ffn_w1"].transpose(1, 0, 2)
    o["f1_b1"] = v["L1_ffn_b1"].reshape(NE, -1, P).transpose(2, 0, 1)
    o["f1_w2"] = v["L1_ffn_w2"].reshape(NE, -1, P, P).transpose(2, 0, 1, 3).reshape(P, NE, -1)
    o["f1_b2"] = v["L1_ffn_b2"]
    return {n: c(x) for n, x in o.items()}


def kernel(**inputs):
    import numpy as _np
    import concourse.bacc as _bacc
    from concourse import mybir as _mybir
    from concourse.bass_utils import run_bass_kernel_spmd as _run

    nc = _bacc.Bacc("TRN2", target_bir_lowering=False, num_devices=1)
    tensors = _layout({n: _np.asarray(x) for n, x in inputs.items()})
    arrays, a = {}, {}
    for n, x in tensors.items():
        x = _np.ascontiguousarray(x)
        arrays[f"in_{n}_dram"] = x
        a[n] = nc.dram_tensor(f"in_{n}_dram", x.shape, _mybir.dt.from_np(x.dtype), kind="ExternalInput").ap()
    NT = a["x"].shape[0]
    a["out"] = nc.dram_tensor("out_0_dram", [NT, P, P], F32, kind="ExternalOutput").ap()
    a["x_dram"] = nc.dram_tensor("x_dram", [NT + NE * CAP // P, P, P], F32).ap()
    a["xn_dram"] = nc.dram_tensor("xn_dram", [NT, P, P], F32).ap()
    a["xx_dram"] = nc.dram_tensor("xx_dram", [NT, P, 2 * P], F32).ap()
    build(nc, a)
    r = _run(nc, [arrays], core_ids=[0])
    return r.results[0]["out_0_dram"].reshape(inputs["x"].shape)
```
